# Optimizing a Trainium2 kernel written in Bass

```python
import numpy as np
import jax
import jax.numpy as jnp

def _softmax(x, axis=-1):
    return jax.nn.softmax(x, axis=axis)

def _gelu(x):
    return jax.nn.gelu(x, approximate=True)

def _silu(x):
    return jax.nn.silu(x)

def _sigmoid(x):
    return jax.nn.sigmoid(x)

def _layernorm(x, axis=-1, eps=1e-05):
    m = jnp.mean(x, axis=axis, keepdims=True)
    v = jnp.var(x, axis=axis, keepdims=True)
    return (x - m) / jnp.sqrt(v + eps)

def _scatter_add(tgt, idx, src, axis=0):
    return tgt.at[idx].add(src)

def _segment_sum(src, seg, n):
    return jax.ops.segment_sum(src, seg, n)
kernel_name = 'mk_gnn_resnorm_d4_gnn_r8_304420'

def setup_inputs(seed: int=0):
    np.random.seed(seed)
    _w = jnp.asarray

    def _rec_inputs():
        import jax
        import jax.numpy as jnp
        _gk = jax.random.key(seed)
        x = -0.0005121 + 1.001 * jax.random.normal(jax.random.fold_in(_gk, 1), (12500, 32), jnp.float32)
        _s = jax.random.randint(jax.random.fold_in(_gk, 2), (100000,), 0, 12500, jnp.int32)
        _d = jax.random.randint(jax.random.fold_in(_gk, 3), (100000,), 0, 12500, jnp.int32)
        _loop = jnp.arange(12500, dtype=jnp.int32)
        src = jnp.concatenate([_s, _d, _loop])
        dst = jnp.concatenate([_d, _s, _loop])
        _o = jnp.argsort(dst, stable=True)
        src = src[_o]
        dst = dst[_o]
        edge_attr_4 = 0.00086875 + 0.999764 * jax.random.normal(jax.random.fold_in(_gk, 12), (212500, 4), jnp.float32)
        edge_attr_8 = jax.random.uniform(jax.random.fold_in(_gk, 13), (212500, 8), jnp.float32, 0.0, 1)
        return (x, src, dst, edge_attr_4, edge_attr_8)
    x, src, dst, edge_attr_4, edge_attr_8 = _rec_inputs()

    def _L0_gnn_setup():
        import jax, jax.numpy as jnp
        import numpy as np
        import math
        N_NODES = 12500
        N_EDGES = 200000
        IN_DIM = 32
        OUT_DIM = 32
        key = jax.random.key(seed)
        k1, k2, k3, k4 = jax.random.split(key, 4)
        X = jax.random.normal(k1, (N_NODES, IN_DIM), dtype=jnp.float32)
        src_idx = jax.random.randint(k2, (N_EDGES,), 0, N_NODES, dtype=jnp.int64)
        dst_idx = jax.random.randint(k3, (N_EDGES,), 0, N_NODES, dtype=jnp.int64)
        stdv = 1.0 / math.sqrt(OUT_DIM)
        W = jax.random.uniform(k4, (IN_DIM, OUT_DIM), dtype=jnp.float32, minval=-stdv, maxval=stdv)
        return {'X': X, 'W': W, 'src_idx': src_idx, 'dst_idx': dst_idx}
    _L0_gnn_all = _L0_gnn_setup()
    _L0_gnn_in = {k: v for k, v in _L0_gnn_all.items() if k in ('W',)}
    del _L0_gnn_all

    def _L1_gnn_setup():
        import jax, jax.numpy as jnp
        import numpy as np
        N_NODES = 6250
        N_EDGES = 100000
        IN_FEATS = 32
        OUT_FEATS = 32
        NUM_HEADS = 4
        key = jax.random.key(seed)
        ks = jax.random.split(key, 12)
        H, F, IN = (NUM_HEADS, OUT_FEATS, IN_FEATS)
        h = jax.random.normal(ks[0], (N_NODES, IN), dtype=jnp.float32)
        src = jax.random.randint(ks[1], (N_EDGES,), 0, N_NODES, dtype=jnp.int64)
        dst = jax.random.randint(ks[2], (N_EDGES,), 0, N_NODES, dtype=jnp.int64)
        s = 0.1
        W_gat = jax.random.normal(ks[3], (IN, H * F), dtype=jnp.float32) * s
        attn_l = jax.random.normal(ks[4], (H, F), dtype=jnp.float32) * s
        attn_r = jax.random.normal(ks[5], (H, F), dtype=jnp.float32) * s
        W_ih = jax.random.normal(ks[6], (3 * F, H * F), dtype=jnp.float32) * s
        W_hh = jax.random.normal(ks[7], (3 * F, F), dtype=jnp.float32) * s
        b_ih = jax.random.normal(ks[8], (3 * F,), dtype=jnp.float32) * s
        b_hh = jax.random.normal(ks[9], (3 * F,), dtype=jnp.float32) * s
        return {'h': h, 'W_gat': W_gat, 'attn_l': attn_l, 'attn_r': attn_r, 'W_ih': W_ih, 'W_hh': W_hh, 'b_ih': b_ih, 'b_hh': b_hh, 'src': src, 'dst': dst}
    _L1_gnn_all = _L1_gnn_setup()
    _L1_gnn_in = {k: v for k, v in _L1_gnn_all.items() if k in ('W_gat', 'attn_l', 'attn_r', 'W_ih', 'W_hh', 'b_ih', 'b_hh')}
    del _L1_gnn_all

    def _L2_gnn_setup():
        import jax, jax.numpy as jnp
        import numpy as np
        N_NODES = 12500
        N_EDGES = 800000
        D = 32
        key = jax.random.key(seed)
        k1, k2, k3, k4 = jax.random.split(key, 4)
        x = jax.random.normal(k1, (N_NODES, D), dtype=jnp.float32)
        W = jax.random.normal(k2, (D, D), dtype=jnp.float32) / np.sqrt(D)
        b = jnp.zeros((D,), dtype=jnp.float32)
        src = jax.random.randint(k3, (N_EDGES,), 0, N_NODES, dtype=jnp.int32)
        dst = jax.random.randint(k4, (N_EDGES,), 0, N_NODES, dtype=jnp.int32)
        return {'x': x, 'W': W, 'b': b, 'src': src, 'dst': dst}
    _L2_gnn_all = _L2_gnn_setup()
    _L2_gnn_in = {k: v for k, v in _L2_gnn_all.items() if k in ('W', 'b')}
    del _L2_gnn_all

    def _L3_gnn_setup():
        import jax, jax.numpy as jnp
        import numpy as np
        N = 4096
        E = 65536
        MUL = 8
        NB = 8
        HR = 64
        NTP = 4 * MUL * MUL
        AVG_NEI = 16.0
        INV_SQRT3 = 1.0 / np.sqrt(3.0)
        ALPHA = 1.0 / np.sqrt(2.0 * MUL)
        key = jax.random.key(seed)
        ks = jax.random.split(key, 12)
        h = jax.random.normal(ks[0], (N, 4 * MUL), jnp.float32)
        edge_index = jax.random.randint(ks[1], (2, E), 0, N)
        edge_sh = jax.random.normal(ks[2], (E, 4), jnp.float32)
        edge_radial = jax.random.uniform(ks[3], (E, NB), jnp.float32)

        def lin(k, fi, fo):
            return (jax.random.normal(k, (fi, fo), jnp.float32) / np.sqrt(fi)).astype(jnp.float32)
        W1 = lin(ks[4], NB, HR)
        b1 = jnp.zeros((HR,), jnp.float32)
        W2 = lin(ks[5], HR, HR)
        b2 = jnp.zeros((HR,), jnp.float32)
        W3 = lin(ks[6], HR, NTP)
        b3 = jnp.zeros((NTP,), jnp.float32)
        Ws = jax.random.normal(ks[7], (MUL, MUL), jnp.float32)
        Wv = jax.random.normal(ks[8], (MUL, MUL), jnp.float32)
        return dict(h=h, edge_index=edge_index, edge_sh=edge_sh, edge_radial=edge_radial, n_atoms=N, W1=W1, b1=b1, W2=W2, b2=b2, W3=W3, b3=b3, Ws=Ws, Wv=Wv)
    _L3_gnn_all = _L3_gnn_setup()
    _L3_gnn_in = {k: v for k, v in _L3_gnn_all.items() if k in ('W1', 'b1', 'W2', 'b2', 'W3', 'b3', 'Ws', 'Wv')}
    del _L3_gnn_all
    return {'x': x, 'src': src, 'dst': dst, 'edge_attr_4': edge_attr_4, 'edge_attr_8': edge_attr_8, 'L0_gnn_W': _L0_gnn_in['W'], 'L1_gnn_W_gat': _L1_gnn_in['W_gat'], 'L1_gnn_attn_l': _L1_gnn_in['attn_l'], 'L1_gnn_attn_r': _L1_gnn_in['attn_r'], 'L1_gnn_W_ih': _L1_gnn_in['W_ih'], 'L1_gnn_W_hh': _L1_gnn_in['W_hh'], 'L1_gnn_b_ih': _L1_gnn_in['b_ih'], 'L1_gnn_b_hh': _L1_gnn_in['b_hh'], 'L2_gnn_W': _L2_gnn_in['W'], 'L2_gnn_b': _L2_gnn_in['b'], 'L3_gnn_W1': _L3_gnn_in['W1'], 'L3_gnn_b1': _L3_gnn_in['b1'], 'L3_gnn_W2': _L3_gnn_in['W2'], 'L3_gnn_b2': _L3_gnn_in['b2'], 'L3_gnn_W3': _L3_gnn_in['W3'], 'L3_gnn_b3': _L3_gnn_in['b3'], 'L3_gnn_Ws': _L3_gnn_in['Ws'], 'L3_gnn_Wv': _L3_gnn_in['Wv']}

def reference(x, src, dst, edge_attr_4, edge_attr_8, L0_gnn_W, L1_gnn_W_gat, L1_gnn_attn_l, L1_gnn_attn_r, L1_gnn_W_ih, L1_gnn_W_hh, L1_gnn_b_ih, L1_gnn_b_hh, L2_gnn_W, L2_gnn_b, L3_gnn_W1, L3_gnn_b1, L3_gnn_W2, L3_gnn_b2, L3_gnn_W3, L3_gnn_b3, L3_gnn_Ws, L3_gnn_Wv):
    import jax
    import jax.numpy as jnp

    def _L0_gnn_ref(X, W, src_idx, dst_idx):
        import jax, jax.numpy as jnp
        import numpy as np
        import math
        N_NODES = 12500
        N_EDGES = 200000
        IN_DIM = 32
        OUT_DIM = 32
        agg = jax.ops.segment_sum(X[src_idx], dst_idx, num_segments=N_NODES)
        return agg @ W

    def _L1_gnn_ref(h, W_gat, attn_l, attn_r, W_ih, W_hh, b_ih, b_hh, src, dst):
        import jax, jax.numpy as jnp
        import numpy as np
        N_NODES = 6250
        N_EDGES = 100000
        IN_FEATS = 32
        OUT_FEATS = 32
        NUM_HEADS = 4
        N = h.shape[0]
        H, F = attn_l.shape
        feat = (h @ W_gat).reshape(N, H, F)
        el = jnp.einsum('nhf,hf->nh', feat, attn_l)
        er = jnp.einsum('nhf,hf->nh', feat, attn_r)
        e = jax.nn.leaky_relu(el[src] + er[dst], 0.2)
        emax = jax.ops.segment_max(e, dst, num_segments=N)
        ee = jnp.exp(e - emax[dst])
        denom = jax.ops.segment_sum(ee, dst, num_segments=N)
        alpha = ee / denom[dst]
        msg = feat[src] * alpha[:, :, None]
        agg = jax.ops.segment_sum(msg, dst, num_segments=N)
        x = agg.reshape(N, H * F)
        gi = x @ W_ih.T + b_ih
        gh = h @ W_hh.T + b_hh
        i_r, i_z, i_n = jnp.split(gi, 3, axis=1)
        h_r, h_z, h_n = jnp.split(gh, 3, axis=1)
        r = jax.nn.sigmoid(i_r + h_r)
        z = jax.nn.sigmoid(i_z + h_z)
        n = jnp.tanh(i_n + r * h_n)
        h_new = (1.0 - z) * n + z * h
        return jax.nn.elu(h_new)

    def _L2_gnn_ref(x, W, b, src, dst):
        import jax, jax.numpy as jnp
        import numpy as np
        N_NODES = 12500
        N_EDGES = 800000
        D = 32
        ones = jnp.ones_like(src, dtype=x.dtype)
        out_deg = jax.ops.segment_sum(ones, src, num_segments=N_NODES)
        in_deg = jax.ops.segment_sum(ones, dst, num_segments=N_NODES)
        out_norm = jax.lax.rsqrt(jnp.maximum(out_deg, 1.0))
        in_norm = jax.lax.rsqrt(jnp.maximum(in_deg, 1.0))
        h = x * out_norm[:, None]
        msgs = h[src]
        agg = jax.ops.segment_sum(msgs, dst, num_segments=N_NODES)
        out = agg * in_norm[:, None] @ W + b
        return out

    def _L3_gnn_ref(h, edge_index, edge_sh, edge_radial, n_atoms, W1, b1, W2, b2, W3, b3, Ws, Wv):
        import jax, jax.numpy as jnp
        import numpy as np
        N = 4096
        E = 65536
        MUL = 8
        NB = 8
        HR = 64
        NTP = 4 * MUL * MUL
        AVG_NEI = 16.0
        INV_SQRT3 = 1.0 / np.sqrt(3.0)
        ALPHA = 1.0 / np.sqrt(2.0 * MUL)
        src, dst = (edge_index[0], edge_index[1])
        x = jax.nn.silu(edge_radial @ W1 + b1)
        x = jax.nn.silu(x @ W2 + b2)
        tpw = x @ W3 + b3
        P = MUL * MUL
        W00 = tpw[:, 0 * P:1 * P].reshape(-1, MUL, MUL)
        W110 = tpw[:, 1 * P:2 * P].reshape(-1, MUL, MUL)
        W01 = tpw[:, 2 * P:3 * P].reshape(-1, MUL, MUL)
        W10 = tpw[:, 3 * P:4 * P].reshape(-1, MUL, MUL)
        hs = h[:, :MUL]
        hv = h[:, MUL:].reshape(-1, MUL, 3)
        hs_e = hs[src]
        hv_e = hv[src]
        sh0 = edge_sh[:, 0]
        sh1 = edge_sh[:, 1:4]
        m0 = ALPHA * (jnp.einsum('eu,euw->ew', hs_e * sh0[:, None], W00) + INV_SQRT3 * jnp.einsum('eui,ei,euw->ew', hv_e, sh1, W110))
        m1 = ALPHA * (jnp.einsum('eu,ei,euw->ewi', hs_e, sh1, W01) + jnp.einsum('eui,euw->ewi', hv_e * sh0[:, None, None], W10))
        messages = jnp.concatenate([m0, m1.reshape(-1, 3 * MUL)], axis=-1)
        agg = jax.ops.segment_sum(messages, dst, num_segments=n_atoms) / np.sqrt(AVG_NEI)
        self0 = hs @ Ws / np.sqrt(MUL)
        self1 = jnp.einsum('nui,uw->nwi', hv, Wv) / np.sqrt(MUL)
        h_self = jnp.concatenate([self0, self1.reshape(-1, 3 * MUL)], axis=-1)
        return h_self + agg
    edge_index = jnp.stack([src, dst])
    x = _layernorm(x + _L0_gnn_ref(x, L0_gnn_W, src, dst), axis=-1)
    x = _layernorm(x + _L1_gnn_ref(x, L1_gnn_W_gat, L1_gnn_attn_l, L1_gnn_attn_r, L1_gnn_W_ih, L1_gnn_W_hh, L1_gnn_b_ih, L1_gnn_b_hh, src, dst), axis=-1)
    x = _layernorm(x + _L2_gnn_ref(x, L2_gnn_W, L2_gnn_b, src, dst), axis=-1)
    x = _layernorm(x + _L3_gnn_ref(x, edge_index, edge_attr_4, edge_attr_8, 12500, L3_gnn_W1, L3_gnn_b1, L3_gnn_W2, L3_gnn_b2, L3_gnn_W3, L3_gnn_b3, L3_gnn_Ws, L3_gnn_Wv), axis=-1)
    return x

_drawn_inputs = setup_inputs


def setup_inputs(seed=0):
    import zlib

    import numpy as np

    out = dict(_drawn_inputs(seed))
    spreads = {'L2_gnn_b': (0.0, 0.1),
     'L3_gnn_b1': (0.0, 0.414),
     'L3_gnn_b2': (0.0, 0.1),
     'L3_gnn_b3': (0.0, 0.1)}
    factors = {'L1_gnn_attn_l': 3.751, 'L1_gnn_attn_r': 8.0, 'L1_gnn_b_hh': 2.716}
    for name, (base, spread) in spreads.items():
        noise = np.random.default_rng([zlib.crc32(name.encode()), seed]).standard_normal(out[name].shape)
        drawn = base * np.exp(spread * noise) if base else spread * noise
        out[name] = jnp.asarray(drawn.astype(out[name].dtype))
    for name, factor in factors.items():
        out[name] = (out[name] * factor).astype(out[name].dtype)
    return out
```

```python
import concourse.bass as bass
from concourse import mybir
from contextlib import ExitStack, contextmanager
from itertools import count
import numpy as np

F32 = mybir.dt.float32
BF16 = mybir.dt.bfloat16
I32 = mybir.dt.int32
ALU = mybir.AluOpType
ACT = mybir.ActivationFunctionType
AX = mybir.AxisListType

P = 128
N = 12500
E = 212500
D = 32
H = 4
J = 64
EC = 1664
CHUNKS = EC // J
PAIRS = CHUNKS // 2
EROWS = P * EC
NP_ = 125
NC_ = 100
G = 10
GROUPS = NC_ // G
QUADS = [(0, 4), (4, 4), (8, 2)]
OH = 8
ROW1 = 2 * H + H * D
T1W = D + 2 * H
BIG = 1e30
EPS = 1e-5
ROUND = 12582912.0
HR = 64
NTP = 256
MUL = 8
ALPHA = 1.0 / np.sqrt(2.0 * MUL)
INV_SQRT3 = 1.0 / np.sqrt(3.0)
NBRS = float(np.sqrt(16.0))
SC = 8
RC = 4
RW = RC * P
RSTEPS = J // RC

assert EC % (2 * J) == 0 and P * EC >= E and NP_ * NC_ == N and NC_ % (2 * G) == 0


class Graph:
    pass


@contextmanager
def stage(nc, g):
    with ExitStack() as ph:
        used = []

        def sem(name):
            used.append(ph.enter_context(nc.semaphore(name)))
            return used[-1]

        def gather_sem(k):
            return g.sem_for_good(f"gathered{next(g.gather_count)}_{k}")
        g.sem, g.gather_sem = sem, gather_sem
        yield
        with nc.Block() as block:
            @block.gpsimd
            def _(pool):
                for one in used:
                    pool.sem_clear(one)


def bcast(ap, axis, count):
    ap = ap.unsqueeze(axis)
    return ap.broadcast_to([count if k == axis else n for k, n in enumerate(ap.shape)])



def load_weights(nc, g, w):
    with ExitStack() as ph:
        sb = lambda n, s, d=F32: ph.enter_context(nc.sbuf_tensor(n, s, d))
        sem = g.sem
        cleared, loaded, made, ids, trans = sem("w_cleared"), sem("w_loaded"), sem("w_made"), sem("w_ids"), sem("w_mm")
        gatT_bd = sb("gatT_bd", [P, P])
        gatT_rep = sb("gatT_rep", [P, P])
        attn = sb("attn", [P, 2 * H])
        ihT = sb("ihT", [P, 96])
        whh = sb("whh_rows", [P, 96])
        w3raw = sb("w3raw", [HR + 1, NTP])
        bih = sb("bih", [1, 96])
        bhh = sb("bhh", [1, 96])
        psA = g.ps[:, 0, :]
        psB = g.ps[:, 1, :]
        n_load = [0]
        with nc.Block() as block:
            @block.sync
            def _(sp):
                def load(dst, src):
                    n_load[0] += 1
                    sp.dma_start(dst, src).then_inc(loaded, 16)
                sp.wait_ge(cleared, 1)
                for c in range(4):
                    r = slice(D * c, D * c + D)
                    load(g.bd0[r, D * c:D * c + D], w["W0"][:, :])
                    load(g.bd2[r, D * c:D * c + D], w["W2g"][:, :])
                    load(gatT_bd[r, D * c:D * c + D], w["gatT"][r, :])
                    load(gatT_rep[:, D * c:D * c + D], w["gatT"][:, :])
                    load(whh[r, :], w["whhT"][:, :])
                    load(g.bdself[r, D * c:D * c + D], w["self"][:, :])
                load(attn[:, :], w["attn"][:, :])
                load(ihT[:, :], w["wihT"][:, :])
                load(bih[:, :], w["b_ih"])
                load(bhh[:, :], w["b_hh"])
                load(g.w1[:, :], w["W1"][:, :])
                load(g.w2[:, :], w["W2"][:, :])
                load(g.b1[:, :], w["b1"])
                load(g.b2[:, :], w["b2"])
                load(w3raw[0:HR, :], w["W3"][:, :])
                load(w3raw[HR:HR + 1, :], w["b3"])
                load(g.b2row[:, :], w["b2g"])

            @block.vector
            def _(dve):
                for t in (gatT_bd, g.bd0, g.bd2, g.bdself, g.bdel):
                    nc.vector.memset(t[:, :], 0.0)
                nc.vector.memset(g.bdhh[:, :, :], 0.0)
                nc.vector.memset(g.wc[:, :], 0.0)
                nc.vector.memset(g.gate_bias[:, :], 0.0)
                nc.vector.memset(g.ones_row[:, :], 1.0)
                dve.drain().then_inc(cleared, 1)
                dve.wait_ge(loaded, 16 * n_load[0])
                nc.vector.tensor_tensor(g.gate_bias[0:1, 0:64], bih[0:1, 0:64], bhh[0:1, 0:64], ALU.add)
                nc.vector.tensor_copy(g.gate_bias[0:1, 64:96], bih[0:1, 64:96])
                nc.vector.tensor_copy(g.gate_bias[0:1, 96:128], bhh[0:1, 64:96])
                for c in range(4):
                    r = slice(D * c, D * c + D)
                    nc.vector.tensor_copy(g.bdhh[r, c, 0:64], whh[r, 0:64])
                    nc.vector.tensor_copy(g.bdhh[r, c, 96:128], whh[r, 64:96])
                nc.vector.tensor_scalar(g.bdself[:, :], g.bdself[:, :], float(1.0 / np.sqrt(MUL)), None, ALU.mult)
                k = float(ALPHA / NBRS)
                src = w3raw[:, :].rearrange("r (b u w) -> r b w u", b=4, u=MUL)
                dst = g.w3p[:, :].rearrange("r (b w u) -> r b w u", b=4, u=MUL)
                for block_, factor in enumerate((k, k * INV_SQRT3, k, k)):
                    nc.vector.tensor_scalar(dst[:, block_], src[:, block_], float(factor), None, ALU.mult)
                dve.drain()
                for q in range(4):
                    nc.vector.tensor_copy(g.bias_quads[0:1, q, :], g.gate_bias[0:1, :])
                dve.wait_ge(trans, 2)
                nc.vector.tensor_copy(g.wc[:, 0:96], psA[:, 0:96])
                for c in range(4):
                    r = slice(D * c, D * c + D)
                    nc.vector.tensor_copy(g.bdel[r, 8 * c:8 * c + 8], psB[r, 0:8])
                dve.drain().then_inc(made, 1)

            @block.gpsimd
            def _(pool):
                nc.gpsimd.memset(g.ident[:, :], 0.0)
                nc.gpsimd.memset(g.ltri[:, :], 1.0)
                nc.gpsimd.iota(g.iota_i[:, :], pattern=[[1, P]], base=0, channel_multiplier=0)
                nc.gpsimd.iota(g.node_i[:, :], pattern=[[1, NC_]], base=0, channel_multiplier=NC_)
                nc.gpsimd.iota(g.first_edge_i[:, :], pattern=[[1, 1]], base=0, channel_multiplier=EC)
                pool.drain()
                nc.gpsimd.affine_select(out=g.ident[:, :], in_=g.ident[:, :], compare_op=ALU.not_equal, fill=1.0,
                                        base=0, pattern=[[-1, P]], channel_multiplier=1)
                nc.gpsimd.affine_select(out=g.ltri[:, :], in_=g.ltri[:, :], compare_op=ALU.is_gt, fill=0.0,
                                        base=0, pattern=[[1, P]], channel_multiplier=-1)
                pool.drain().then_inc(ids, 1)

            @block.tensor
            def _(pe):
                pe.wait_ge(loaded, 16 * n_load[0])
                nc.tensor.matmul(psA[:, 0:96], gatT_bd[:, :], ihT[:, :], start=True, stop=True).then_inc(trans, 1)
                nc.tensor.matmul(psB[:, 0:8], gatT_rep[:, :], attn[:, :], start=True, stop=True).then_inc(trans, 1)



def gather_chunks(nc, g, pool, table, buf, s):
    for b in range(2):
        pool.sem_inc(s.buf_free[b], 16)
    with pool.Fori(0, PAIRS) as i:
        for b in range(2):
            pool.wait_ge(s.idx_in[b], 16 * i + 16)
            pool.wait_ge(s.buf_free[b], 16 * i + 16)
            pool.nop(nofuse=True)
            for j in range(J):
                pool.indirect_dma_start(buf[:, b, j, :], None, table,
                                        bass.IndirectOffsetOnAxis(g.idx[:, b, j:j + 1], 0)).then_inc(s.rows_in[b], 16)


def chunk_cols(i, b, width=1):
    return bass.ds(i * (2 * J * width) + b * J * width, J * width)


class EdgeSems:

    def __init__(self, sem, gather_sem, name):
        self.idx_in = [sem(f"{name}_idx_in{b}") for b in range(2)]
        self.rows_in = [gather_sem(b) for b in range(2)]
        self.buf_free = [sem(f"{name}_buf_free{b}") for b in range(2)]
        self.scanned = [sem(f"{name}_scanned{b}") for b in range(2)]


def scan_rows(nc, g, dve, i, b, buf, carry, width):
    cont = g.cont[:, chunk_cols(i, b)]
    for f in range(width):
        nc.vector.tensor_tensor_scan(buf[:, b, :, f], cont, buf[:, b, :, f], carry[:, f:f + 1], ALU.mult, ALU.add)
    dve.drain()
    nc.vector.tensor_copy(carry[:, 0:width], buf[:, b, J - 1, :])
    

def radial_tensor(nc, g, pe, rad, h1, r):
    def second_layer(i, n):
        k = n % 2
        pe.wait_ge(r.h1_out[k], i * RSTEPS + n // 2 + 1)
        pe.nop(nofuse=True)
        nc.tensor.matmul(g.ps[0:HR, 4 + k, :], g.w2[:, :], h1[:, k, :], start=True, stop=True).then_inc(r.h2_in[k], 1)

    with pe.Fori(0, PAIRS) as i:
        for b in range(2):
            pe.wait_ge(r.rad_in[b], 16 * i + 16)
            for m in range(RSTEPS):
                n = b * RSTEPS + m
                k = n % 2
                nc.tensor.matmul(g.ps[0:HR, 2 + k, :], g.w1[:, :], rad[:, b, m * RW:(m + 1) * RW], start=True, stop=True)\
                    .then_inc(r.h1_in[k], 1)
                if m == RSTEPS - 1:
                    pe.drain().then_inc(r.rad_free[b], 1)
                if n > 0:
                    second_layer(i, n - 1)
        second_layer(i, 2 * RSTEPS - 1)


def radial_scalar(nc, g, act, rad, h1, h2, r):
    def second_layer(i, n):
        k, b, m = n % 2, n // RSTEPS, n % RSTEPS
        if m == 0:
            act.wait_ge(r.h2_free[b], 16 * i + 16)
        act.wait_ge(r.h2_in[k], i * RSTEPS + n // 2 + 1)
        nc.scalar.activation(h2[:, b, m * RW:(m + 1) * RW], g.ps[0:HR, 4 + k, :], ACT.Silu, bias=g.b2[:, 0:1])
        if m == RSTEPS - 1:
            act.drain().then_inc(r.h2_made[b], 1)
            act.wait_ge(r.h2_made[b], i + 1)
            act.dma_start(g.hidden[:, chunk_cols(i, b, P)], h2[:, b, :]).then_inc(r.h2_free[b], 16)
            act.wait_ge(r.rad_free[b], i + 1)
            act.dma_start(rad[:, b, :], g.edge_rad[:, bass.ds(i * (2 * J * P) + (b + 2) * J * P, J * P)])\
               .then_inc(r.rad_in[b], 16)

    with act.Fori(0, PAIRS) as i:
        for n in range(2 * RSTEPS):
            k = n % 2
            act.wait_ge(r.h1_in[k], i * RSTEPS + n // 2 + 1)
            nc.scalar.activation(h1[:, k, :], g.ps[0:HR, 2 + k, :], ACT.Silu, bias=g.b1[:, 0:1]).then_inc(r.h1_out[k], 1)
            if n > 0:
                second_layer(i, n - 1)
        second_layer(i, 2 * RSTEPS - 1)
    for b in range(2):
        act.wait_ge(r.h2_free[b], 16 * PAIRS + 16)
        act.wait_ge(r.rad_in[b], 16 * PAIRS + 16)


class RadialSems:
    def __init__(self, sem):
        pair = lambda n: [sem(f"radial_{n}{b}") for b in range(2)]
        self.rad_in, self.rad_free, self.h1_in, self.h1_out = pair("in"), pair("free"), pair("h1_in"), pair("h1_out")
        self.h2_in, self.h2_made, self.h2_free = pair("h2_in"), pair("h2_made"), pair("h2_free")


def edge_stage_plain(nc, g, name, table, rows, first):
    with ExitStack() as ph:
        sb = lambda n, s, d=F32: ph.enter_context(nc.sbuf_tensor(f"{name}_{n}", s, d))
        s = EdgeSems(g.sem, g.gather_sem, name)
        buf = sb("rows", [P, 2, J, D])
        if first:
            dst_i = sb("dst_i", [P, EC], I32)
            prev_i = sb("prev_i", [P, EC], I32)
            src_i = sb("src_i", [P, EC], I32)
            dst_f = sb("dst_f", [P, EC])
            src_f = sb("src_f", [P, EC])
            tmp_f = sb("tmp_f", [P, EC])
            hi = sb("hi", [P, 2, EC], BF16)
            lo = sb("lo", [P, 2, EC], BF16)
            iota_b = sb("iota_b", [P, P], BF16)
            onehot_hi = sb("onehot_hi", [P, 2, 2, OH, NP_], BF16)
            onehot_lo = sb("onehot_lo", [P, 2, 2, OH, NC_], BF16)
            zero_b = sb("zero_b", [P, P], BF16)
            graph_in, oh_used, oh_made, hist_zero, hist_done = (
                g.sem("graph_in"), [g.sem(f"oh_used{b}") for b in range(2)], [g.sem(f"oh_made{b}") for b in range(2)],
                g.sem("hist_zero"), g.sem("hist_done"))
            er_zero = g.sem("er_zero")
            zeroed = g.sem("zeroed")
        else:
            rs = RadialSems(g.sem)
            rad = sb("rad", [8, 2, J * P])
            h1 = sb("h1", [HR, 2, RW])
            h2 = sb("h2", [HR, 2, J * P])
        with nc.Block() as block:
            @block.gpsimd
            def _(pool):
                if not first:
                    for b in range(2):
                        pool.sem_inc(rs.h2_free[b], 16)
                gather_chunks(nc, g, pool, table, buf, s)

            @block.sync
            def _(sp):
                if first:
                    dst_cols = lambda o: g.dst_flat[0:1, o:o + EROWS].rearrange("a (p c) -> (a p) c", c=EC)
                    for b in range(2):
                        sp.dma_start(g.idx[:, b, :], g.src_cols[:, b * J:(b + 1) * J]).then_inc(s.idx_in[b], 16)
                    sp.dma_start(dst_i[:, :], dst_cols(1)).then_inc(graph_in, 16)
                    sp.dma_start(prev_i[:, :], dst_cols(0)).then_inc(graph_in, 16)
                    sp.dma_start(src_i[:, :], g.src_cols[:, 0:EC]).then_inc(graph_in, 16)
                    sp.wait_ge(zeroed, 1)
                    for k in range(4):
                        sp.dma_start(g.er_edges[0:EROWS, :].rearrange("(p c) h -> p (c h)", p=P)[:, k * EC:(k + 1) * EC],
                                     tmp_f[:, :]).then_inc(er_zero, 16)
                    for r, width in ((g.rows0, D), (g.rows1, ROW1), (g.rows2, D), (g.rows3, D)):
                        sp.dma_start(r[EROWS:EROWS + 1, :], tmp_f[0:1, 0:width]).then_inc(er_zero, 16)
                else:
                    for b in range(2):
                        sp.dma_start(g.idx[:, b, :], g.src_cols[:, b * J:(b + 1) * J]).then_inc(s.idx_in[b], 16)
                        sp.dma_start(rad[:, b, :], g.edge_rad[:, b * J * P:(b + 1) * J * P]).then_inc(rs.rad_in[b], 16)
                rows_v = rows[0:EROWS, :].rearrange("(p c) f -> p (c f)", p=P)
                with sp.Fori(0, PAIRS) as i:
                    for b in range(2):
                        sp.wait_ge(s.rows_in[b], (16 * J) * i + 16 * J)
                        sp.dma_start(g.idx[:, b, :], g.src_cols[:, bass.ds(i * (2 * J) + (b + 2) * J, J)])\
                          .then_inc(s.idx_in[b], 16)
                        sp.wait_ge(s.scanned[b], i + 1)
                        sp.dma_start(rows_v[:, chunk_cols(i, b, D)], buf[:, b].rearrange("p j f -> p (j f)"))\
                          .then_inc(s.buf_free[b], 16)
                for b in range(2):
                    sp.wait_ge(s.buf_free[b], 16 * PAIRS + 16)
                    sp.wait_ge(s.idx_in[b], 16 * PAIRS + 16)
                if first:
                    sp.wait_ge(er_zero, 16 * 8)

            @block.vector
            def _(dve):
                if first:
                    nc.vector.memset(tmp_f[:, :], 0.0)
                    nc.vector.memset(zero_b[:, :], 0.0)
                    dve.drain().then_inc(zeroed, 1)
                    nc.vector.tensor_copy(iota_b[:, :], g.iota_i[:, :])
                    dve.wait_ge(graph_in, 48)
                    nc.vector.tensor_tensor(g.cont[:, :], dst_i[:, :], prev_i[:, :], ALU.is_equal)
                    nc.vector.tensor_copy(dst_f[:, :], dst_i[:, :])
                    nc.vector.tensor_copy(src_f[:, :], src_i[:, :])
                    dve.drain()
                    dve.wait_ge(er_zero, 16 * 8)
                    nc.vector.tensor_scalar(g.dst0_f[:, :], dst_f[:, 0:1], float(N - 1), None, ALU.min)
                    for k, n_f in enumerate((src_f, dst_f)):
                        nc.vector.tensor_scalar(tmp_f[:, :], n_f[:, :], 1.0 / NC_, -0.495, ALU.mult, ALU.add)
                        dve.drain()
                        nc.vector.tensor_scalar(tmp_f[:, :], tmp_f[:, :], ROUND, ROUND, ALU.add, ALU.subtract)
                        dve.drain()
                        nc.vector.scalar_tensor_tensor(lo[:, k, :], tmp_f[:, :], -float(NC_), n_f[:, :], ALU.mult, ALU.add)
                        nc.vector.tensor_copy(hi[:, k, :], tmp_f[:, :])
                        dve.drain()
                    nc.vector.tensor_scalar(tmp_f[:, :], dst_f[:, :], float(N), 2.0 * NP_, ALU.is_ge, ALU.mult)
                    nc.vector.tensor_copy(g.dst0_i[:, :], g.dst0_f[:, :])
                    dve.drain()
                    nc.vector.tensor_tensor(hi[:, 0, :], hi[:, 0, :], tmp_f[:, :], ALU.add)
                nc.vector.memset(g.carry[:, :], 0.0)
                dve.drain()
                with dve.Fori(0, PAIRS) as i:
                    for b in range(2):
                        if first:
                            for k in range(J // OH):
                                h = k % 2
                                dve.wait_ge(oh_used[h], i * (J // OH) + (b * (J // OH) + k) // 2 + 1)
                                cols = bass.ds(i * (2 * J) + (b * J + k * OH), OH)
                                for e in range(2):
                                    nc.vector.tensor_tensor(
                                        onehot_hi[:, h, e], bcast(iota_b[:, 0:NP_], 1, OH),
                                        bcast(hi[:, e, cols], 2, NP_), ALU.is_equal)
                                    last = nc.vector.tensor_tensor(
                                        onehot_lo[:, h, e], bcast(iota_b[:, 0:NC_], 1, OH),
                                        bcast(lo[:, e, cols], 2, NC_), ALU.is_equal)
                                dve.drain().then_inc(oh_made[h], 1)
                        dve.wait_ge(s.rows_in[b], (16 * J) * i + 16 * J)
                        scan_rows(nc, g, dve, i, b, buf, g.carry, D)
                        dve.drain().then_inc(s.scanned[b], 1)
                if first:
                    dve.wait_ge(hist_done, 1)
                    nc.vector.tensor_copy(g.deg[:, 0, :], g.ps[0:NP_, 0, 0:NC_])
                    nc.vector.tensor_copy(g.deg[:, 1, :], g.ps[0:NP_, 1, 0:NC_])
                    dve.drain()

            if not first:
                @block.tensor
                def _(pe):
                    radial_tensor(nc, g, pe, rad, h1, rs)

                @block.scalar
                def _(act):
                    radial_scalar(nc, g, act, rad, h1, h2, rs)
            else:
                @block.tensor
                def _(pe):
                    pe.wait_ge(zeroed, 1)
                    for e in range(2):
                        nc.tensor.matmul(g.ps[0:NP_, e, 0:NC_], zero_b[:, 0:NP_], zero_b[:, 0:NC_], start=True, stop=False)
                    for h in range(2):
                        pe.sem_inc(oh_used[h], 1)
                    with pe.Fori(0, CHUNKS) as i:
                        for k in range(J // OH):
                            h = k % 2
                            pe.wait_ge(oh_made[h], i * (J // OH // 2) + k // 2 + 1)
                            for e in range(2):
                                for c in range(OH):
                                    last = nc.tensor.matmul(g.ps[0:NP_, e, 0:NC_], onehot_hi[:, h, e, c, :],
                                                            onehot_lo[:, h, e, c, :], start=False, stop=False)
                            last.then_inc(oh_used[h], 1)
                    for e in range(2):
                        last = nc.tensor.matmul(g.ps[0:NP_, e, 0:NC_], zero_b[:, 0:NP_], zero_b[:, 0:NC_],
                                                start=False, stop=True)
                    last.then_inc(hist_done, 1)


def index_stage(nc, g):
    with ExitStack() as ph:
        sb = lambda n, s, d=F32: ph.enter_context(nc.sbuf_tensor(f"ix_{n}", s, d))
        run = sb("run", [NP_, NC_])
        ones = sb("ones", [NP_, NC_])
        node = sb("node", [NP_, NC_])
        last_e = sb("last_e", [NP_, NC_])
        first_e = sb("first_e", [NP_, NC_])
        alt = sb("alt", [NP_, NC_])
        empty = sb("empty", [NP_, NC_])
        base = sb("base", [NP_, 1])
        prod = sb("prod", [P, EC])
        lead = sb("lead", [P, 1])
        fe = sb("fe", [P, 1])
        flag = sb("flag", [P, 1])
        whole = sb("whole", [P, 1])
        flags_wide = sb("flags_wide", [P, 2, P])
        run_made, base_made, flags_made, flags_turned = (g.sem("ix_run"), g.sem("ix_base"), g.sem("ix_flags"), g.sem("ix_turned"))
        norm_in, norm_out, ends_made, ends_out = g.sem("ix_norm_in"), g.sem("ix_norm_out"), g.sem("ix_ends"), g.sem("ix_ends_out")
        with nc.Block() as block:
            @block.vector
            def _(dve):
                v = nc.vector
                v.memset(ones[:, :], 1.0)
                v.tensor_copy(node[:, :], g.node_i[0:NP_, :])
                v.tensor_scalar(g.norm[:, :, :], g.deg[:, :, :], 1.0, None, ALU.max)
                dve.drain().then_inc(norm_in, 1)
                v.tensor_tensor_scan(run[:, :], ones[:, :], g.deg[:, 1, :], 0.0, ALU.mult, ALU.add)
                dve.drain().then_inc(run_made, 1)
                v.tensor_tensor_scan(prod[:, 0:EC - 1], g.cont[:, 1:EC], g.cont[:, 1:EC], 1.0, ALU.mult, ALU.min)
                v.tensor_copy(fe[:, :], g.first_edge_i[:, :])
                dve.drain()
                v.reduce_sum(lead[:, :], prod[:, 0:EC - 1], axis=AX.X)
                v.tensor_tensor(whole[:, :], prod[:, EC - 2:EC - 1], g.cont[:, 0:1], ALU.mult)
                dve.drain()
                v.tensor_tensor(fe[:, :], fe[:, :], lead[:, :], ALU.add)
                v.tensor_copy(flags_wide[:, 0, :], g.cont[:, 0:1].broadcast_to([P, P]))
                v.tensor_copy(flags_wide[:, 1, :], whole[:, 0:1].broadcast_to([P, P]))
                dve.drain().then_inc(flags_made, 1)
                v.tensor_copy(g.border_idx[:, :], fe[:, :])
                dve.wait_ge(base_made, 1)
                v.tensor_copy(base[:, :], g.ps[0:NP_, 2, 0:1])
                v.tensor_scalar(empty[:, :], g.deg[:, 1, :], 0.0, None, ALU.is_equal)
                dve.drain()
                v.tensor_scalar(last_e[:, :], run[:, :], base[:, 0:1], -1.0, ALU.add, ALU.add)
                dve.drain()
                v.tensor_tensor(first_e[:, :], last_e[:, :], g.deg[:, 1, :], ALU.subtract)
                v.tensor_scalar(alt[:, :], last_e[:, :], -1.0, float(EROWS), ALU.mult, ALU.add)
                dve.drain()
                v.tensor_scalar(first_e[:, :], first_e[:, :], 1.0, None, ALU.add)
                v.tensor_tensor(alt[:, :], alt[:, :], empty[:, :], ALU.mult)
                dve.drain()
                v.tensor_tensor(last_e[:, :], last_e[:, :], alt[:, :], ALU.add)
                dve.drain()
                v.tensor_scalar(node[:, :], node[:, :], float(EROWS), None, ALU.add)
                dve.drain()
                v.tensor_tensor(node[:, :], node[:, :], first_e[:, :], ALU.subtract)
                dve.drain()
                v.tensor_tensor(node[:, :], node[:, :], empty[:, :], ALU.mult)
                dve.drain()
                v.tensor_tensor(first_e[:, :], first_e[:, :], node[:, :], ALU.add)
                v.tensor_copy(g.last_i[:, :], last_e[:, :])
                dve.drain().then_inc(ends_made, 1)
                v.tensor_copy(g.first_i[:, :], first_e[:, :])
                dve.wait_ge(norm_out, 1)
                v.reciprocal(g.norm[:, :, :], g.norm[:, :, :])
                dve.wait_ge(flags_turned, 1)
                v.tensor_copy(g.cont0[:, :], g.ps[:, 3, 0:P])
                v.tensor_copy(g.linked[:, :], g.ps[:, 3, P:2 * P])
                v.memset(g.link[:, :], 0.0)
                dve.drain()
                v.tensor_tensor(g.link[:, 1:P], g.cont0[:, 1:P], g.linked[:, 0:P - 1], ALU.mult)
                dve.drain()

            @block.scalar
            def _(act):
                act.wait_ge(norm_in, 1)
                nc.scalar.activation(g.norm[:, :, :], g.norm[:, :, :], ACT.Sqrt).then_inc(norm_out, 1)

            @block.tensor
            def _(pe):
                pe.wait_ge(run_made, 1)
                nc.tensor.matmul(g.ps[0:NP_, 2, 0:1], g.ltri[0:NP_, 0:NP_], run[:, NC_ - 1:NC_],
                                 start=True, stop=True).then_inc(base_made, 1)
                pe.wait_ge(flags_made, 1)
                nc.tensor.transpose(g.ps[:, 3, 0:P], flags_wide[:, 0, :], g.ident[:, :])
                nc.tensor.transpose(g.ps[:, 3, P:2 * P], flags_wide[:, 1, :], g.ident[:, :]).then_inc(flags_turned, 1)

            @block.sync
            def _(sp):
                sp.wait_ge(ends_made, 1)
                sp.dma_start(g.last_cols[:, 0:NC_], g.last_i[:, :]).then_inc(ends_out, 16)
                sp.wait_ge(ends_out, 16)


def border_stage_plain(nc, g, name, rows):
    with ExitStack() as ph:
        sb = lambda n, s, d=F32: ph.enter_context(nc.sbuf_tensor(f"{name}_{n}", s, d))
        patch = sb("patch", [P, D])
        item = sb("item", [D, P])
        into = sb("into", [D, P])
        turned, into_made, back, patched = (g.sem(f"{name}_{n}") for n in ("turned", "into", "back", "patched"))
        fetched, put = g.gather_sem(0), g.gather_sem(1)
        with nc.Block() as block:
            @block.tensor
            def _(pe):
                nc.tensor.transpose(g.ps[0:D, 0, 0:P], g.carry[:, 0:D], g.ident[:, :]).then_inc(turned, 1)
                pe.wait_ge(into_made, 1)
                nc.tensor.transpose(g.ps[:, 1, 0:D], into[:, :], g.ident[0:D, 0:D]).then_inc(back, 1)

            @block.vector
            def _(dve):
                nc.vector.memset(item[:, :], 0.0)
                dve.drain()
                dve.wait_ge(turned, 1)
                nc.vector.tensor_tensor(item[:, 1:P], g.cont0[0:D, 1:P], g.ps[0:D, 0, 0:P - 1], ALU.mult)
                dve.drain()
                nc.vector.tensor_tensor_scan(into[:, :], g.link[0:D, :], item[:, :], 0.0, ALU.mult, ALU.add)\
                    .then_inc(into_made, 1)
                dve.wait_ge(back, 1)
                dve.wait_ge(fetched, 16)
                nc.vector.tensor_tensor(patch[:, :], patch[:, :], g.ps[:, 1, 0:D], ALU.add).then_inc(patched, 1)

            @block.gpsimd
            def _(pool):
                pool.indirect_dma_start(patch[:, :], None, rows[:, :], bass.IndirectOffsetOnAxis(g.border_idx[:, 0:1], 0))\
                    .then_inc(fetched, 16)
                pool.wait_ge(patched, 1)
                pool.indirect_dma_start(rows[:, :], bass.IndirectOffsetOnAxis(g.border_idx[:, 0:1], 0), patch[:, :], None)\
                    .then_inc(put, 16)
                pool.wait_ge(put, 16)



class NodeSems:

    def __init__(self, sem, gather_sem, name):
        pair = lambda n: [sem(f"{name}_{n}{b}") for b in range(2)]
        self.gathered = [gather_sem(b) for b in range(2)]
        self.loaded, self.free, self.stored, self.new_ready = pair("loaded"), pair("free"), pair("stored"), pair("new_ready")
        self.turned, self.turned_sb, self.product = pair("turned"), pair("turned_sb"), pair("product")
        self.x_turned, self.x_turned_sb, self.x_product = pair("x_turned"), pair("x_turned_sb"), pair("x_product")
        self.agg_ready, self.var, self.std, self.prods_used = pair("agg_ready"), pair("var"), pair("std"), pair("prods_used")
        self.gates_act, self.hidden, self.hidden_act = pair("gates_act"), pair("hidden"), pair("hidden_act")
        self.low, self.low_act = pair("low"), pair("low_act")


def node_loads(nc, g, sp, s, nidx, xg, x_rows, gathers=True):
    x_v = x_rows.rearrange("(p j) f -> p (j f)", p=NP_)
    with sp.Fori(0, GROUPS // 2) as i:
        for b in range(2):
            sp.wait_ge(s.free[b], i + 1)
            sp.dma_start(nidx[:, b, :], g.last_cols[:, bass.ds(i * (2 * G) + b * G, G)]).then_inc(s.loaded[b], 16)
            sp.dma_start(xg[:, b].rearrange("p j f -> p (j f)"), x_v[:, bass.ds(i * (2 * G * D) + b * G * D, G * D)])\
              .then_inc(s.loaded[b], 16)


def node_gathers(nc, g, pool, s, nidx, agg, rows):
    with pool.Fori(0, GROUPS // 2) as i:
        for b in range(2):
            pool.wait_ge(s.loaded[b], 32 * i + 32)
            pool.nop(nofuse=True)
            for j in range(G):
                pool.indirect_dma_start(agg[:, b, j, :], None, rows[:, :],
                                        bass.IndirectOffsetOnAxis(nidx[:, b, j:j + 1], 0)).then_inc(s.gathered[b], 16)


def node_stores(nc, g, eng, s, i, b, new, dests):
    eng.wait_ge(s.new_ready[b], i + 1)
    for buf, rows in dests:
        width = rows.shape[1]
        eng.dma_start(rows.rearrange("(p j) f -> p (j f)", p=NP_)[:, bass.ds(i * (2 * G * width) + b * G * width, G * width)],
                      buf[:, b].rearrange("p j f -> p (j f)")).then_inc(s.stored[b], 16)


def turn_group(nc, g, pe, src, psum):
    for q, (c, k) in enumerate(QUADS):
        last = nc.tensor.transpose(psum[0:k * D, q * P:q * P + NP_], src[:, c:c + k, :].rearrange("p j f -> p (j f)"),
                                   g.ident[0:NP_, 0:NP_])
    return last


def copy_turned(nc, turned, psum):
    nc.scalar.activation(turned[:, 0:2, 0:NP_], psum[:, 0:2 * P].rearrange("p (q n) -> p q n", q=2)[:, :, 0:NP_], ACT.Copy)
    return nc.scalar.activation(turned[0:2 * D, 2, 0:NP_], psum[0:2 * D, 2 * P:2 * P + NP_], ACT.Copy)


def apply_bd(nc, pe, psum, turned, weight, width):
    for q, (c, k) in enumerate(QUADS):
        last = nc.tensor.matmul(psum[0:NP_, c * width:(c + k) * width], turned[0:k * D, q, 0:NP_],
                                weight[0:k * D, 0:k * width], start=True, stop=True)
    return last


def layernorm(nc, g, dve, s, i, b, r, t, stat, out):
    v = nc.vector
    v.reduce_sum(stat[:, b, 0, :], r, axis=AX.X)
    dve.drain()
    v.tensor_scalar(stat[:, b, 1, :], stat[:, b, 0, :], 1.0 / D, None, ALU.mult)
    dve.drain()
    v.tensor_tensor(r, r, bcast(stat[:, b, 1, :], 2, D), ALU.subtract)
    dve.drain()
    v.tensor_tensor(t, r, r, ALU.mult)
    dve.drain()
    v.reduce_sum(stat[:, b, 0, :], t, axis=AX.X)
    dve.drain()
    v.tensor_scalar(stat[:, b, 2, :], stat[:, b, 0, :], 1.0 / D, EPS, ALU.mult, ALU.add).then_inc(s.var[b], 1)
    dve.wait_ge(s.std[b], i + 1)
    v.reciprocal(stat[:, b, 4, :], stat[:, b, 3, :])
    dve.drain()
    return v.tensor_tensor(out, r, bcast(stat[:, b, 4, :], 2, D), ALU.mult)


def layernorm_sqrt(nc, act, s, i, b, stat):
    act.wait_ge(s.var[b], i + 1)
    nc.scalar.activation(stat[:, b, 3, :], stat[:, b, 2, :], ACT.Sqrt).then_inc(s.std[b], 1)


def node_stage_plain(nc, g, name, layer, rows, x_in, dests):
    with ExitStack() as ph:
        sb = lambda n, s_, d=F32: ph.enter_context(nc.sbuf_tensor(f"{name}_{n}", s_, d))
        s = NodeSems(g.sem, g.gather_sem, name)
        nidx = sb("nidx", [NP_, 2, G], I32)
        xg = sb("xg", [NP_, 2, G, D])
        agg = sb("agg", [NP_, 2, G, D])
        turned = sb("turned", [P, 2, 3, P])
        xturned = sb("xturned", [P, 2, 3, P])
        r = sb("r", [NP_, 2, G, D])
        t = sb("t", [NP_, 2, G, D])
        stat = sb("stat", [NP_, 2, 5, G])
        new = sb("new", [NP_, 2, G, D])
        t1 = sb("t1", [NP_, 2, G, T1W])
        bd = {0: g.bd0, 2: g.bd2, 3: g.bdself}[layer]
        bufs = {"x": new, "t1": t1}
        n_dest = len(dests)
        with nc.Block() as block:
            @block.sync
            def _(sp):
                node_loads(nc, g, sp, s, nidx, xg, x_in)
                for b in range(2):
                    sp.wait_ge(s.stored[b], 16 * n_dest * (GROUPS // 2 + 1))

            @block.gpsimd
            def _(pool):
                for b in range(2):
                    pool.sem_inc(s.free[b], 1)
                    pool.sem_inc(s.stored[b], 16 * n_dest)
                node_gathers(nc, g, pool, s, nidx, agg, rows)

            @block.tensor
            def _(pe):
                with pe.Fori(0, GROUPS // 2) as i:
                    for b in range(2):
                        if layer == 3:
                            pe.wait_ge(s.loaded[b], 32 * i + 32)
                            turn_group(nc, g, pe, xg[:, b], g.ps[:, b, :]).then_inc(s.turned[b], 1)
                        elif layer == 2:
                            pe.wait_ge(s.agg_ready[b], i + 1)
                            turn_group(nc, g, pe, r[:, b], g.ps[:, b, :]).then_inc(s.turned[b], 1)
                        else:
                            pe.wait_ge(s.gathered[b], 16 * G * i + 16 * G)
                            turn_group(nc, g, pe, agg[:, b], g.ps[:, b, :]).then_inc(s.turned[b], 1)
                        pe.wait_ge(s.turned_sb[b], i + 1)
                        apply_bd(nc, pe, g.ps[:, 2 + b, :], turned[:, b], bd, D).then_inc(s.product[b], 1)
                        if layer == 0:
                            pe.wait_ge(s.agg_ready[b], i + 1)
                            turn_group(nc, g, pe, new[:, b], g.ps[:, 4 + b, :]).then_inc(s.x_turned[b], 1)
                            pe.wait_ge(s.x_turned_sb[b], i + 1)
                            apply_bd(nc, pe, g.ps[:, 6 + b, :], xturned[:, b], g.bdel, 2 * H).then_inc(s.x_product[b], 1)

            @block.scalar
            def _(act):
                with act.Fori(0, GROUPS // 2) as i:
                    for b in range(2):
                        act.wait_ge(s.turned[b], i + 1)
                        copy_turned(nc, turned[:, b], g.ps[:, b, :]).then_inc(s.turned_sb[b], 1)
                        layernorm_sqrt(nc, act, s, i, b, stat)
                        if layer == 0:
                            act.wait_ge(s.x_turned[b], i + 1)
                            copy_turned(nc, xturned[:, b], g.ps[:, 4 + b, :]).then_inc(s.x_turned_sb[b], 1)
                        node_stores(nc, g, act, s, i, b, None, [(bufs[k], d) for k, d in dests])

            @block.vector
            def _(dve):
                v = nc.vector
                with dve.Fori(0, GROUPS // 2) as i:
                    for b in range(2):
                        cols = bass.ds(i * (2 * G) + b * G, G)
                        dve.wait_ge(s.gathered[b], 16 * G * i + 16 * G)
                        if layer == 2:
                            v.tensor_tensor(r[:, b], agg[:, b], bcast(g.norm[:, 1, cols], 2, D), ALU.mult)\
                                .then_inc(s.agg_ready[b], 1)
                            v.tensor_tensor(t[:, b], xg[:, b], bcast(g.b2row[:, :], 1, G), ALU.add)
                        if layer == 3:
                            v.tensor_tensor(t[:, b], xg[:, b], agg[:, b], ALU.add)
                        if layer != 0:
                            dve.drain()
                        dve.wait_ge(s.product[b], i + 1)
                        v.tensor_tensor(r[:, b], xg[:, b] if layer == 0 else t[:, b],
                                        g.ps[0:NP_, 2 + b, 0:G * D].rearrange("p (j f) -> p j f", f=D), ALU.add)
                        dve.drain()
                        dve.wait_ge(s.stored[b], 16 * n_dest * i + 16 * n_dest)
                        layernorm(nc, g, dve, s, i, b, r[:, b], t[:, b], stat, new[:, b])
                        if layer == 0:
                            dve.drain().then_inc(s.agg_ready[b], 1)
                            v.tensor_copy(t1[:, b, :, 0:D], new[:, b])
                            dve.wait_ge(s.x_product[b], i + 1)
                            el_er = g.ps[0:NP_, 6 + b, 0:G * 2 * H].rearrange("p (j h) -> p j h", h=2 * H)
                            v.tensor_copy(t1[:, b, :, D:T1W], el_er)
                            v.tensor_copy(g.er_nodes[:, cols, :], el_er[:, :, H:2 * H])
                        dve.drain().then_inc(s.new_ready[b], 1)
                        dve.sem_inc(s.free[b], 1)


def spread_er_stage(nc, g):
    put, got = g.gather_sem(0), g.gather_sem(1)
    with nc.Block() as block:
        @block.gpsimd
        def _(pool):
            for c in range(NC_):
                pool.indirect_dma_start(g.er_edges[:, :], bass.IndirectOffsetOnAxis(g.first_i[:, c:c + 1], 0),
                                        g.er_nodes[:, c, :], None).then_inc(put, 16)
            pool.indirect_dma_start(g.row_dst0[:, :], None, g.table1[:, :],
                                    bass.IndirectOffsetOnAxis(g.dst0_i[:, 0:1], 0)).then_inc(got, 16)
            pool.wait_ge(put, 16 * NC_)
            pool.wait_ge(got, 16)


def edge_stage_attention(nc, g):
    with ExitStack() as ph:
        sb = lambda n, s_, d=F32: ph.enter_context(nc.sbuf_tensor(f"e1_{n}", s_, d))
        s = EdgeSems(g.sem, g.gather_sem, "e1")
        gat = sb("gat", [P, 2, J, T1W])
        er0 = sb("er0", [P, 2, J, H])
        er = sb("er", [P, J, H])
        er_carry = sb("er_carry", [P, H])
        e = sb("e", [P, J, H])
        e2 = sb("e2", [P, J, H])
        neg = sb("neg", [P, J])
        expo = sb("expo", [P, 2, J, H])
        wexp = sb("wexp", [P, 2, J, H])
        acc = sb("acc", [P, 2, J, ROW1])
        er_in = [g.sem(f"e1_er_in{b}") for b in range(2)]
        gat_free = [g.sem(f"e1_gat_free{b}") for b in range(2)]
        expo_ready, wexp_ready = g.sem("e1_expo"), g.sem("e1_wexp")
        with nc.Block() as block:
            @block.gpsimd
            def _(pool):
                for b in range(2):
                    pool.sem_inc(gat_free[b], 1)
                    pool.sem_inc(s.buf_free[b], 16)
                with pool.Fori(0, PAIRS) as i:
                    for b in range(2):
                        pool.wait_ge(s.idx_in[b], 16 * i + 16)
                        pool.wait_ge(gat_free[b], i + 1)
                        pool.nop(nofuse=True)
                        for j in range(J):
                            pool.indirect_dma_start(gat[:, b, j, :], None, g.table1[:, :],
                                                    bass.IndirectOffsetOnAxis(g.idx[:, b, j:j + 1], 0)).then_inc(s.rows_in[b], 16)

            @block.sync
            def _(sp):
                er_v = g.er_edges[0:EROWS, :].rearrange("(p c) h -> p (c h)", p=P)
                chunk = lambda i, b, width: bass.ds(i * (2 * J * width) + b * J * width, J * width)
                for b in range(2):
                    sp.dma_start(g.idx[:, b, :], g.src_cols[:, b * J:(b + 1) * J]).then_inc(s.idx_in[b], 16)
                    sp.dma_start(er0[:, b].rearrange("p j h -> p (j h)"), er_v[:, b * J * H:(b + 1) * J * H]).then_inc(er_in[b], 16)
                with sp.Fori(0, PAIRS - 1) as i:
                    for b in range(2):
                        sp.wait_ge(s.rows_in[b], (16 * J) * i + 16 * J)
                        sp.dma_start(g.idx[:, b, :], g.src_cols[:, chunk(i, b + 2, 1)]).then_inc(s.idx_in[b], 16)
                        sp.wait_ge(gat_free[b], i + 2)
                        sp.dma_start(er0[:, b].rearrange("p j h -> p (j h)"), er_v[:, chunk(i, b + 2, H)]).then_inc(er_in[b], 16)
                for b in range(2):
                    sp.wait_ge(s.buf_free[b], 16 * PAIRS + 16)

            @block.scalar
            def _(act):
                rows_v = g.rows1[0:EROWS, :].rearrange("(p c) f -> p (c f)", p=P)
                with act.Fori(0, PAIRS) as i:
                    for b in range(2):
                        act.wait_ge(expo_ready, i * 2 + (b + 1))
                        nc.scalar.activation(wexp[:, :, :, :], expo[:, :, :, :], ACT.Exp).then_inc(wexp_ready, 1)
                        act.wait_ge(s.scanned[b], i + 1)
                        act.dma_start(rows_v[:, chunk_cols(i, b, ROW1)], acc[:, b].rearrange("p j f -> p (j f)"))\
                           .then_inc(s.buf_free[b], 16)

            @block.vector
            def _(dve):
                v = nc.vector
                v.memset(g.carry[:, 0:H], -BIG)
                v.memset(g.carry[:, H:ROW1], 0.0)
                v.tensor_copy(er_carry[:, :], g.row_dst0[:, D + H:T1W])
                dve.drain()
                with dve.Fori(0, PAIRS) as i:
                    for b in range(2):
                        cont = g.cont[:, chunk_cols(i, b)]
                        v.tensor_scalar(neg[:, :], cont, BIG, BIG, ALU.mult, ALU.subtract)
                        dve.wait_ge(er_in[b], 16 * i + 16)
                        for h in range(H):
                            v.tensor_tensor_scan(er[:, :, h], cont, er0[:, b, :, h], er_carry[:, h:h + 1], ALU.mult, ALU.add)
                        dve.drain()
                        v.tensor_copy(er_carry[:, :], er[:, J - 1, :])
                        dve.wait_ge(s.rows_in[b], (16 * J) * i + 16 * J)
                        v.tensor_tensor(e2[:, :, :], gat[:, b, :, D:D + H], er[:, :, :], ALU.add)
                        dve.drain()
                        v.scalar_tensor_tensor(e[:, :, :], e2[:, :, :], 0.2, e2[:, :, :], ALU.mult, ALU.max)
                        dve.drain()
                        dve.wait_ge(s.buf_free[b], 16 * i + 16)
                        for h in range(H):
                            v.tensor_tensor_scan(acc[:, b, :, h], neg[:, :], e[:, :, h], g.carry[:, h:h + 1], ALU.add, ALU.max)
                        dve.drain()
                        v.tensor_tensor(expo[:, 1], e[:, :, :], acc[:, b, :, 0:H], ALU.subtract)
                        v.tensor_tensor(e2[:, 0:1, :], bcast(neg[:, 0:1], 2, H), g.carry[:, 0:H].unsqueeze(1), ALU.add)
                        v.tensor_tensor(e2[:, 1:J, :], bcast(neg[:, 1:J], 2, H), acc[:, b, 0:J - 1, 0:H], ALU.add)
                        dve.drain()
                        v.tensor_tensor(expo[:, 0], e2[:, :, :], acc[:, b, :, 0:H], ALU.subtract)
                        dve.drain().then_inc(expo_ready, 1)
                        dve.wait_ge(wexp_ready, i * 2 + (b + 1))
                        v.tensor_copy(acc[:, b, :, H:2 * H], wexp[:, 1])
                        for h in range(H):
                            v.tensor_tensor(acc[:, b, :, 2 * H + h * D:2 * H + (h + 1) * D], gat[:, b, :, 0:D],
                                            bcast(wexp[:, 1, :, h], 2, D), ALU.mult)
                        dve.drain().then_inc(gat_free[b], 1)
                        for h in range(H):
                            for c in [H + h] + list(range(2 * H + h * D, 2 * H + (h + 1) * D)):
                                v.tensor_tensor_scan(acc[:, b, :, c], wexp[:, 0, :, h], acc[:, b, :, c],
                                                     g.carry[:, c:c + 1], ALU.mult, ALU.add)
                        dve.drain()
                        v.tensor_copy(g.carry[:, 0:ROW1], acc[:, b, J - 1, :])
                        dve.drain().then_inc(s.scanned[b], 1)


def border_stage_attention(nc, g):
    with ExitStack() as ph:
        sb = lambda n, s_, d=F32: ph.enter_context(nc.sbuf_tensor(f"b1_{n}", s_, d))
        K = H * D
        patch = sb("patch", [P, ROW1])
        wide = sb("wide", [P, 2, P])
        item_m = sb("item_m", [P, P])
        into_m = sb("into_m", [P, P])
        expo = sb("expo", [P, 2, P])
        fac = sb("fac", [P, 2, P])
        neg_link = sb("neg_link", [P, P])
        neg_c0 = sb("neg_c0", [P, P])
        item_v = sb("item_v", [P, P])
        into_v = sb("into_v", [P, P])
        new_m = sb("new_m", [P, H])
        m_all = sb("m_all", [P, 2, P])
        names = ("wide", "turned", "expo", "fac", "into", "back", "expo2", "fac2", "patched")
        wide_ready, turned, expo_ready, fac_ready, into_ready, back, expo2, fac2, patched = (
            g.sem(f"b1_{n}") for n in names)
        fetched, put = g.gather_sem(0), g.gather_sem(1)
        with nc.Block() as block:
            @block.gpsimd
            def _(pool):
                pool.indirect_dma_start(patch[:, :], None, g.rows1[:, :], bass.IndirectOffsetOnAxis(g.border_idx[:, 0:1], 0))\
                    .then_inc(fetched, 16)
                pool.wait_ge(patched, 1)
                pool.indirect_dma_start(g.rows1[:, :], bass.IndirectOffsetOnAxis(g.border_idx[:, 0:1], 0), patch[:, :], None)\
                    .then_inc(put, 16)
                pool.wait_ge(put, 16)

            @block.tensor
            def _(pe):
                for n in range(2):
                    pe.wait_ge(wide_ready, n + 1)
                    for k in range(2):
                        last = nc.tensor.transpose(g.ps[:, k, 0:P], wide[:, k, :], g.ident[:, :])
                    last.then_inc(turned, 1)
                    pe.wait_ge(into_ready, n + 1)
                    nc.tensor.transpose(g.ps[:, 2, 0:P], into_m[:, :], g.ident[:, :])
                    nc.tensor.transpose(g.ps[:, 3, 0:P], into_v[:, :], g.ident[:, :]).then_inc(back, 1)

            @block.scalar
            def _(act):
                for n in range(2):
                    act.wait_ge(expo_ready, n + 1)
                    nc.scalar.activation(fac[:, :, :], expo[:, :, :], ACT.Exp).then_inc(fac_ready, 1)
                    act.wait_ge(expo2, n + 1)
                    nc.scalar.activation(fac[:, :, :], m_all[:, :, :], ACT.Exp).then_inc(fac2, 1)

            @block.vector
            def _(dve):
                v = nc.vector
                v.tensor_scalar(neg_link[:, :], g.link[:, :], BIG, BIG, ALU.mult, ALU.subtract)
                v.tensor_scalar(neg_c0[:, :], g.cont0[:, :], BIG, BIG, ALU.mult, ALU.subtract)
                v.memset(item_m[:, :], -BIG)
                v.memset(item_v[:, :], 0.0)
                v.memset(expo[:, :, :], 0.0)
                dve.drain()
                dve.wait_ge(fetched, 16)
                for n in range(2):
                    v.tensor_copy(wide[:, 0, :].rearrange("p (h f) -> p h f", h=H), bcast(g.carry[:, 0:H], 2, D))
                    if n == 0:
                        v.tensor_copy(wide[:, 1, :], g.carry[:, 2 * H:ROW1])
                    else:
                        v.tensor_copy(wide[:, 1, :].rearrange("p (h f) -> p h f", h=H), bcast(g.carry[:, H:2 * H], 2, D))
                    dve.drain().then_inc(wide_ready, 1)
                    dve.wait_ge(turned, n + 1)
                    v.tensor_tensor(item_m[:, 1:P], g.cont0[:, 1:P], g.ps[:, 0, 0:P - 1], ALU.mult)
                    dve.drain()
                    v.tensor_tensor(item_m[:, 1:P], item_m[:, 1:P], neg_c0[:, 1:P], ALU.add)
                    dve.drain()
                    v.tensor_tensor_scan(into_m[:, :], neg_link[:, :], item_m[:, :], -BIG, ALU.add, ALU.max)
                    dve.drain()
                    v.tensor_tensor(expo[:, 0, 1:P], into_m[:, 0:P - 1], neg_link[:, 1:P], ALU.add)
                    v.tensor_tensor(expo[:, 1, 1:P], item_m[:, 1:P], into_m[:, 1:P], ALU.subtract)
                    dve.drain()
                    v.tensor_tensor(expo[:, 0, 1:P], expo[:, 0, 1:P], into_m[:, 1:P], ALU.subtract)
                    dve.drain().then_inc(expo_ready, 1)
                    dve.wait_ge(fac_ready, n + 1)
                    v.tensor_tensor(fac[:, 0, :], fac[:, 0, :], g.link[:, :], ALU.mult)
                    v.tensor_tensor(item_v[:, 1:P], fac[:, 1, 1:P], g.ps[:, 1, 0:P - 1], ALU.mult)
                    dve.drain()
                    v.tensor_tensor(item_v[:, 1:P], item_v[:, 1:P], g.cont0[:, 1:P], ALU.mult)
                    dve.drain()
                    v.tensor_tensor_scan(into_v[:, :], fac[:, 0, :], item_v[:, :], 0.0, ALU.mult, ALU.add)
                    dve.drain().then_inc(into_ready, 1)
                    dve.wait_ge(back, n + 1)
                    v.tensor_copy(m_all[:, 1, :], g.ps[:, 2, 0:P])
                    v.tensor_copy(m_all[:, 0, :].rearrange("p (h f) -> p h f", h=H), bcast(patch[:, 0:H], 2, D))
                    dve.drain()
                    v.tensor_tensor(item_m[:, :], m_all[:, 0, :], m_all[:, 1, :], ALU.max)
                    dve.drain()
                    v.tensor_tensor(m_all[:, 0, :], m_all[:, 0, :], item_m[:, :], ALU.subtract)
                    v.tensor_tensor(m_all[:, 1, :], m_all[:, 1, :], item_m[:, :], ALU.subtract)
                    if n == 1:
                        v.tensor_copy(new_m[:, :], item_m[:, :].rearrange("p (h f) -> p h f", h=H)[:, :, 0])
                    dve.drain().then_inc(expo2, 1)
                    dve.wait_ge(fac2, n + 1)
                    v.tensor_tensor(fac[:, 1, :], fac[:, 1, :], g.ps[:, 3, 0:P], ALU.mult)
                    if n == 0:
                        v.tensor_tensor(patch[:, 2 * H:ROW1], patch[:, 2 * H:ROW1], fac[:, 0, :], ALU.mult)
                        dve.drain()
                        v.tensor_tensor(patch[:, 2 * H:ROW1], patch[:, 2 * H:ROW1], fac[:, 1, :], ALU.add)
                        v.memset(item_m[:, 0:1], -BIG)
                        dve.drain()
                    else:
                        one = lambda k: fac[:, k, :].rearrange("p (h f) -> p h f", h=H)[:, :, 0]
                        v.tensor_tensor(patch[:, H:2 * H], patch[:, H:2 * H], one(0), ALU.mult)
                        dve.drain()
                        v.tensor_tensor(patch[:, H:2 * H], patch[:, H:2 * H], one(1), ALU.add)
                        v.tensor_copy(patch[:, 0:H], new_m[:, :])
                        dve.drain().then_inc(patched, 1)


def node_stage_gru(nc, g):
    with ExitStack() as ph:
        name = "n1"
        sb = lambda n, s_, d=F32: ph.enter_context(nc.sbuf_tensor(f"{name}_{n}", s_, d))
        s = NodeSems(g.sem, g.gather_sem, name)
        nidx = sb("nidx", [NP_, 2, G], I32)
        xg = sb("xg", [NP_, 2, G, D])
        agg = sb("agg", [NP_, 2, G, ROW1])
        rden = sb("rden", [NP_, 2, G, H])
        alpha = sb("alpha", [NP_, 2, G, H * D])
        aturned = sb("aturned", [P, 2, G, P])
        xturned = sb("xturned", [P, 2, 3, P])
        rz = sb("rz", [NP_, 2, G, 2 * D])
        hid = sb("hid", [NP_, 2, G, D])
        low = sb("low", [NP_, 2, G, D])
        r = sb("r", [NP_, 2, G, D])
        t = sb("t", [NP_, 2, G, D])
        stat = sb("stat", [NP_, 2, 5, G])
        new = sb("new", [NP_, 2, G, D])
        scaled = sb("scaled", [NP_, 2, G, D])
        tp = g.ps[:, 4:7, :]
        xp = g.ps[:, 7, :]
        gates_ps = g.ps[0:NP_, 0:3, :]
        gflat = gates_ps.rearrange("p q c -> p (q c)")[:, 0:G * P].rearrange("p (j c) -> p j c", c=P)
        with nc.Block() as block:
            @block.sync
            def _(sp):
                node_loads(nc, g, sp, s, nidx, xg, g.x1)
                for b in range(2):
                    sp.wait_ge(s.stored[b], 32 * (GROUPS // 2 + 1))

            @block.gpsimd
            def _(pool):
                for b in range(2):
                    pool.sem_inc(s.free[b], 1)
                    pool.sem_inc(s.stored[b], 32)
                pool.sem_inc(s.prods_used[0], 1)
                node_gathers(nc, g, pool, s, nidx, agg, g.rows1)

            @block.tensor
            def _(pe):
                with pe.Fori(0, GROUPS // 2) as i:
                    for b in range(2):
                        pe.wait_ge(s.loaded[b], 32 * i + 32)
                        turn_group(nc, g, pe, xg[:, b], xp).then_inc(s.x_turned[b], 1)
                        pe.wait_ge(s.agg_ready[b], i + 1)
                        for c in range(G):
                            last = nc.tensor.transpose(tp[:, c // 4, (c % 4) * P:(c % 4) * P + NP_], alpha[:, b, c, :],
                                                       g.ident[0:NP_, 0:NP_])
                        last.then_inc(s.turned[b], 1)
                        pe.wait_ge(s.x_turned_sb[b], i + 1)
                        pe.wait_ge(s.prods_used[0], i * 2 + (b + 1))
                        for q, (c, k) in enumerate(QUADS):
                            nc.tensor.matmul(gates_ps[:, q, 0:k * P], xturned[0:k * D, b, q, 0:NP_],
                                             g.bdhh[0:k * D, 0:k, :].rearrange("p k c -> p (k c)"), start=True, stop=False)
                            nc.tensor.matmul(gates_ps[:, q, 0:k * P], g.ones_row[0:1, 0:NP_],
                                             g.bias_quads[0:1, 0:k, :].rearrange("p k c -> p (k c)"), start=False, stop=True)
                        pe.wait_ge(s.turned_sb[b], i + 1)
                        for c in range(G):
                            last = nc.tensor.matmul(gates_ps[:, c // 4, (c % 4) * P:(c % 4 + 1) * P], aturned[:, b, c, 0:NP_],
                                                    g.wc[:, :], start=False, stop=True, skip_group_check=True)
                        last.then_inc(s.product[b], 1)

            @block.scalar
            def _(act):
                a = nc.scalar
                with act.Fori(0, GROUPS // 2) as i:
                    for b in range(2):
                        act.wait_ge(s.x_turned[b], i + 1)
                        copy_turned(nc, xturned[:, b], xp).then_inc(s.x_turned_sb[b], 1)
                        act.wait_ge(s.turned[b], i + 1)
                        for q, (c, k) in enumerate(QUADS):
                            last = a.activation(aturned[:, b, c:c + k, 0:NP_],
                                                tp[:, q, 0:k * P].rearrange("p (k n) -> p k n", k=k)[:, :, 0:NP_], ACT.Copy)
                        last.then_inc(s.turned_sb[b], 1)
                        act.wait_ge(s.product[b], i + 1)
                        a.activation(rz[:, b], gflat[:, :, 0:2 * D], ACT.Tanh, scale=0.5).then_inc(s.gates_act[b], 1)
                        act.wait_ge(s.hidden[b], i + 1)
                        a.activation(hid[:, b], hid[:, b], ACT.Tanh).then_inc(s.hidden_act[b], 1)
                        act.wait_ge(s.low[b], i + 1)
                        a.activation(low[:, b], low[:, b], ACT.Exp).then_inc(s.low_act[b], 1)
                        layernorm_sqrt(nc, act, s, i, b, stat)
                        node_stores(nc, g, act, s, i, b, None, [(new, g.x2), (scaled, g.table2)])

            @block.vector
            def _(dve):
                v = nc.vector
                with dve.Fori(0, GROUPS // 2) as i:
                    for b in range(2):
                        cols = bass.ds(i * (2 * G) + b * G, G)
                        dve.wait_ge(s.gathered[b], 16 * G * i + 16 * G)
                        v.tensor_scalar(rden[:, b], agg[:, b, :, H:2 * H], 1e-30, None, ALU.max)
                        dve.drain()
                        v.reciprocal(rden[:, b], rden[:, b])
                        dve.drain()
                        for h in range(H):
                            v.tensor_tensor(alpha[:, b, :, h * D:(h + 1) * D], agg[:, b, :, 2 * H + h * D:2 * H + (h + 1) * D],
                                            bcast(rden[:, b, :, h], 2, D), ALU.mult)
                        dve.drain().then_inc(s.agg_ready[b], 1)
                        dve.wait_ge(s.gates_act[b], i + 1)
                        v.tensor_scalar(rz[:, b], rz[:, b], 0.5, 0.5, ALU.mult, ALU.add)
                        dve.drain()
                        v.tensor_tensor(t[:, b], rz[:, b, :, 0:D], gflat[:, :, 3 * D:4 * D], ALU.mult)
                        dve.drain()
                        v.tensor_tensor(hid[:, b], t[:, b], gflat[:, :, 2 * D:3 * D], ALU.add).then_inc(s.hidden[b], 1)
                        dve.drain().then_inc(s.prods_used[0], 1)
                        dve.wait_ge(s.hidden_act[b], i + 1)
                        v.tensor_tensor(t[:, b], xg[:, b], hid[:, b], ALU.subtract)
                        dve.drain()
                        v.tensor_tensor(t[:, b], t[:, b], rz[:, b, :, D:2 * D], ALU.mult)
                        dve.drain()
                        v.tensor_tensor(r[:, b], t[:, b], hid[:, b], ALU.add)
                        dve.drain()
                        v.tensor_scalar(low[:, b], r[:, b], 0.0, None, ALU.min).then_inc(s.low[b], 1)
                        v.tensor_scalar(r[:, b], r[:, b], 0.0, -1.0, ALU.max, ALU.add)
                        dve.drain()
                        v.tensor_tensor(r[:, b], r[:, b], xg[:, b], ALU.add)
                        dve.drain()
                        dve.wait_ge(s.low_act[b], i + 1)
                        v.tensor_tensor(r[:, b], r[:, b], low[:, b], ALU.add)
                        dve.drain()
                        dve.wait_ge(s.stored[b], 32 * i + 32)
                        layernorm(nc, g, dve, s, i, b, r[:, b], t[:, b], stat, new[:, b])
                        dve.drain()
                        v.tensor_tensor(scaled[:, b], new[:, b], bcast(g.norm[:, 0, cols], 2, D), ALU.mult)
                        dve.drain().then_inc(s.new_ready[b], 1)
                        dve.sem_inc(s.free[b], 1)


def edge_stage_tensor_product(nc, g):
    with ExitStack() as ph:
        sb = lambda n, s_, d=F32: ph.enter_context(nc.sbuf_tensor(f"e3_{n}", s_, d))
        s = EdgeSems(g.sem, g.gather_sem, "e3")
        STEPS = J // SC
        W = SC * P
        gat = sb("gat", [P, 2, J, D])
        sh = sb("sh", [P, 2, J, 4])
        h2 = sb("h2", [HR + 1, 2, J * P])
        vs = sb("vs", [P, J, MUL, 3])
        fac = sb("fac", [P, J, 3, MUL])
        cv = sb("cv", [P, J, 3, MUL])
        prod = sb("prod", [P, 2, SC, 6, MUL, MUL])
        red = sb("red", [P, J, 6, MUL])
        msg = sb("msg", [P, 2, J, D])
        tp_made, tp_used = ([g.sem(f"e3_{n}{k}") for k in range(2)] for n in ("tp", "tp_used"))
        sh_in, h2_in, h2_free, gat_free = ([g.sem(f"e3_{n}{b}") for b in range(2)] for n in ("sh_in", "h2_in", "h2_free", "gat_free"))
        ones_set, hs_copied = g.sem("e3_ones"), g.sem("e3_hs")
        with nc.Block() as block:
            @block.gpsimd
            def _(pool):
                for b in range(2):
                    pool.sem_inc(gat_free[b], 1)
                    pool.sem_inc(s.buf_free[b], 16)
                with pool.Fori(0, PAIRS) as i:
                    for b in range(2):
                        pool.wait_ge(s.idx_in[b], 16 * i + 16)
                        pool.wait_ge(gat_free[b], i + 1)
                        pool.nop(nofuse=True)
                        for j in range(J):
                            pool.indirect_dma_start(gat[:, b, j, :], None, g.x3[:, :],
                                                    bass.IndirectOffsetOnAxis(g.idx[:, b, j:j + 1], 0)).then_inc(s.rows_in[b], 16)

            @block.sync
            def _(sp):
                sh_v = g.edge_sh.rearrange("(p c) h -> p (c h)", p=P)
                chunk = lambda i, b, width: bass.ds(i * (2 * J * width) + b * J * width, J * width)
                for b in range(2):
                    sp.dma_start(g.idx[:, b, :], g.src_cols[:, b * J:(b + 1) * J]).then_inc(s.idx_in[b], 16)
                    sp.dma_start(h2[0:HR, b, :], g.hidden[:, b * J * P:(b + 1) * J * P]).then_inc(h2_in[b], 16)
                    sp.dma_start(sh[:, b].rearrange("p j h -> p (j h)"), sh_v[:, b * J * 4:(b + 1) * J * 4]).then_inc(sh_in[b], 16)
                with sp.Fori(0, PAIRS - 1) as i:
                    for b in range(2):
                        sp.wait_ge(s.rows_in[b], (16 * J) * i + 16 * J)
                        sp.dma_start(g.idx[:, b, :], g.src_cols[:, chunk(i, b + 2, 1)]).then_inc(s.idx_in[b], 16)
                        sp.wait_ge(h2_free[b], i + 1)
                        sp.dma_start(h2[0:HR, b, :], g.hidden[:, chunk(i, b + 2, P)]).then_inc(h2_in[b], 16)
                        sp.wait_ge(gat_free[b], i + 2)
                        sp.dma_start(sh[:, b].rearrange("p j h -> p (j h)"), sh_v[:, chunk(i, b + 2, 4)]).then_inc(sh_in[b], 16)
                for b in range(2):
                    sp.wait_ge(s.buf_free[b], 16 * PAIRS + 16)

            @block.tensor
            def _(pe):
                pe.wait_ge(ones_set, 1)
                for k in range(2):
                    pe.sem_inc(tp_used[k], 1)
                with pe.Fori(0, PAIRS) as i:
                    for b in range(2):
                        pe.wait_ge(h2_in[b], 16 * i + 16)
                        for m in range(STEPS):
                            n = b * STEPS + m
                            k = n % 2
                            pe.wait_ge(tp_used[k], i * STEPS + n // 2 + 1)
                            for c in range(SC):
                                at = (m * SC + c) * P
                                last = nc.tensor.matmul(g.ps[:, 4 * k + c // 2, (c % 2) * NTP:(c % 2 + 1) * NTP],
                                                        h2[:, b, at:at + P], g.w3p[:, :], start=True, stop=True)
                            last.then_inc(tp_made[k], 1)
                        pe.drain().then_inc(h2_free[b], 1)

            @block.scalar
            def _(act):
                rows_v = g.rows3[0:EROWS, :].rearrange("(p c) f -> p (c f)", p=P)
                with act.Fori(0, PAIRS) as i:
                    for b in range(2):
                        act.wait_ge(s.rows_in[b], (16 * J) * i + 16 * J)
                        act.wait_ge(gat_free[1 - b], i + 1 + b)
                        nc.scalar.activation(fac[:, :, 2, :], gat[:, b, :, 0:MUL], ACT.Copy).then_inc(hs_copied, 1)
                        act.wait_ge(s.scanned[b], i + 1)
                        act.dma_start(rows_v[:, chunk_cols(i, b, D)], msg[:, b].rearrange("p j f -> p (j f)"))\
                           .then_inc(s.buf_free[b], 16)

            @block.vector
            def _(dve):
                v = nc.vector
                v.memset(h2[HR:HR + 1, :, :], 1.0)
                v.memset(g.carry[:, :], 0.0)
                dve.drain().then_inc(ones_set, 1)
                with dve.Fori(0, PAIRS) as i:
                    for b in range(2):
                        dve.wait_ge(sh_in[b], 16 * i + 16)
                        dve.wait_ge(s.rows_in[b], (16 * J) * i + 16 * J)
                        hv = gat[:, b, :, MUL:D].rearrange("p j (u i) -> p j u i", i=3)
                        sh0 = sh[:, b, :, 0]
                        sh1 = sh[:, b, :, 1:4]
                        v.tensor_tensor(vs[:, :, :, :], hv, bcast(sh1, 2, MUL), ALU.mult)
                        v.tensor_tensor(fac[:, :, 0, :], gat[:, b, :, 0:MUL], bcast(sh0, 2, MUL), ALU.mult)
                        v.tensor_tensor(cv[:, :, :, :], hv.rearrange("p j u i -> p j i u"),
                                        bcast(bcast(sh0, 2, 3), 3, MUL), ALU.mult)
                        dve.drain()
                        v.tensor_reduce(fac[:, :, 1, :], vs[:, :, :, :], AX.X, ALU.add)
                        dve.drain()
                        dve.wait_ge(hs_copied, i * 2 + (b + 1))
                        for m in range(STEPS):
                            n = b * STEPS + m
                            k = n % 2
                            c0, c1 = m * SC, (m + 1) * SC
                            dve.wait_ge(tp_made[k], i * STEPS + n // 2 + 1)
                            tp = g.ps[:, 4 * k:4 * k + 4, :].rearrange("p a (c x) -> p (a c) x", x=NTP)
                            v.tensor_tensor(prod[:, k, :, 0:3], tp[:, :, 0:192].rearrange("p c (f w u) -> p c f w u", f=3, w=MUL),
                                            bcast(fac[:, c0:c1], 3, MUL), ALU.mult)
                            v.tensor_tensor(prod[:, k, :, 3:6], bcast(tp[:, :, 192:256].rearrange("p c (w u) -> p c w u", w=MUL), 2, 3),
                                            bcast(cv[:, c0:c1], 3, MUL), ALU.mult)
                            dve.drain().then_inc(tp_used[k], 1)
                            v.tensor_reduce(red[:, c0:c1].rearrange("p c f w -> p (c f w)"),
                                            prod[:, k].rearrange("p c f w u -> p (c f w) u"), AX.X, ALU.add)
                        dve.drain()
                        dve.wait_ge(s.buf_free[b], 16 * i + 16)
                        v.tensor_tensor(msg[:, b, :, 0:MUL], red[:, :, 0, :], red[:, :, 1, :], ALU.add)
                        v.tensor_tensor(vs[:, :, :, :], bcast(red[:, :, 2, :], 3, 3), bcast(sh1, 2, MUL), ALU.mult)
                        dve.drain().then_inc(gat_free[b], 1)
                        v.tensor_tensor(msg[:, b, :, MUL:D].rearrange("p j (w i) -> p j w i", i=3), vs[:, :, :, :],
                                        red[:, :, 3:6, :].rearrange("p j i w -> p j w i"), ALU.add)
                        dve.drain()
                        scan_rows(nc, g, dve, i, b, msg, g.carry, D)
                        dve.drain().then_inc(s.scanned[b], 1)


def program(nc, x, src_cols, dst_flat, edge_sh, edge_rad, w, out):
    with ExitStack() as ctx:
        g = Graph()
        g.sem_for_good, g.gather_count = (lambda n: ctx.enter_context(nc.semaphore(n))), count()
        sb = lambda n, s, d=F32: ctx.enter_context(nc.sbuf_tensor(n, s, d))
        dram = lambda n, s, d=F32: nc.dram_tensor(n, s, d, kind="Internal").ap()
        g.src_cols, g.dst_flat, g.edge_sh, g.edge_rad = src_cols, dst_flat, edge_sh, edge_rad
        g.rows0 = dram("rows0", (EROWS + 1, D))
        g.rows1 = dram("rows1", (EROWS + 1, ROW1))
        g.rows2 = dram("rows2", (EROWS + 1, D))
        g.rows3 = dram("rows3", (EROWS + 1, D))
        g.er_edges = dram("er_edges", (EROWS + N, H))
        g.table1 = dram("table1", (N, T1W))
        g.table2 = dram("table2", (N, D))
        g.x1, g.x2, g.x3 = (dram(f"x{k}", (N, D)) for k in (1, 2, 3))
        g.hidden = dram("hidden", (HR, EROWS))
        g.last_cols = dram("last_cols", (NP_, NC_), I32)

        g.ps = ctx.enter_context(nc.psum_tensor("ps", [P, 8, 512], F32))
        g.idx = sb("idx", [P, 2, J], I32)
        g.cont = sb("cont", [P, EC])
        g.carry = sb("carry", [P, ROW1])
        g.ident = sb("ident", [P, P])
        g.ltri = sb("ltri", [P, P])
        g.iota_i = sb("iota_i", [P, P], I32)
        g.node_i = sb("node_i", [P, NC_], I32)
        g.first_edge_i = sb("first_edge_i", [P, 1], I32)
        g.dst0_f, g.dst0_i = sb("dst0_f", [P, 1]), sb("dst0_i", [P, 1], I32)
        g.row_dst0 = sb("row_dst0", [P, T1W])
        g.border_idx = sb("border_idx", [P, 1], I32)
        g.cont0, g.linked, g.link = sb("cont0", [P, P]), sb("linked", [P, P]), sb("link", [P, P])
        g.deg, g.norm = sb("deg", [NP_, 2, NC_]), sb("norm", [NP_, 2, NC_])
        g.last_i, g.first_i = sb("last_i", [NP_, NC_], I32), sb("first_i", [NP_, NC_], I32)
        g.er_nodes = sb("er_nodes", [NP_, NC_, H])
        g.bd0, g.bd2, g.bdself = sb("bd0", [P, P]), sb("bd2", [P, P]), sb("bdself", [P, P])
        g.bdel = sb("bdel", [P, 8 * H])
        g.bdhh = sb("bdhh", [P, 4, P])
        g.wc = sb("wc", [P, P])
        g.gate_bias, g.bias_quads, g.ones_row = sb("gate_bias", [1, P]), sb("bias_quads", [1, 4, P]), sb("ones_row", [1, P])
        g.w1, g.w2, g.w3p = sb("w1", [8, HR]), sb("w2", [HR, HR]), sb("w3p", [HR + 1, NTP])
        g.b1, g.b2, g.b2row = sb("b1", [HR, 1]), sb("b2", [HR, 1]), sb("b2row", [NP_, D])

        with stage(nc, g):
            load_weights(nc, g, w)
        with stage(nc, g):
            edge_stage_plain(nc, g, "e0", x[:, :], g.rows0, first=True)
        with stage(nc, g):
            index_stage(nc, g)
        with stage(nc, g):
            border_stage_plain(nc, g, "b0", g.rows0)
        with stage(nc, g):
            node_stage_plain(nc, g, "n0", 0, g.rows0, x, [("x", g.x1), ("t1", g.table1)])
        with stage(nc, g):
            spread_er_stage(nc, g)
        with stage(nc, g):
            edge_stage_attention(nc, g)
        with stage(nc, g):
            border_stage_attention(nc, g)
        with stage(nc, g):
            node_stage_gru(nc, g)
        with stage(nc, g):
            edge_stage_plain(nc, g, "e2", g.table2[:, :], g.rows2, first=False)
        with stage(nc, g):
            border_stage_plain(nc, g, "b2", g.rows2)
        with stage(nc, g):
            node_stage_plain(nc, g, "n2", 2, g.rows2, g.x2, [("x", g.x3)])
        with stage(nc, g):
            edge_stage_tensor_product(nc, g)
        with stage(nc, g):
            border_stage_plain(nc, g, "b3", g.rows3)
        with stage(nc, g):
            node_stage_plain(nc, g, "n3", 3, g.rows3, g.x3, [("x", out)])


def kernel(x, src, dst, edge_attr_4, edge_attr_8, L0_gnn_W, L1_gnn_W_gat, L1_gnn_attn_l, L1_gnn_attn_r, L1_gnn_W_ih,
           L1_gnn_W_hh, L1_gnn_b_ih, L1_gnn_b_hh, L2_gnn_W, L2_gnn_b, L3_gnn_W1, L3_gnn_b1, L3_gnn_W2, L3_gnn_b2,
           L3_gnn_W3, L3_gnn_b3, L3_gnn_Ws, L3_gnn_Wv):
    import concourse.bacc as bacc
    from concourse.bass_utils import run_bass_kernel_spmd

    a = np.ascontiguousarray
    pad = EROWS - E
    src_cols = np.pad(np.pad(np.asarray(src), (0, pad)).reshape(P, EC), ((0, 0), (0, 2 * J)))
    dst_flat = np.concatenate([np.full(1, -1, np.int32), np.asarray(dst), np.full(pad, N, np.int32)]).reshape(1, -1)
    rad = np.pad(np.asarray(edge_attr_8), ((0, pad), (0, 0))).reshape(P, EC, 8).transpose(2, 1, 0)
    rad = np.pad(rad, ((0, 0), (0, 2 * J), (0, 0))).reshape(8, -1)
    data = {
        "x": np.asarray(x),
        "src_cols": src_cols,
        "dst_flat": dst_flat,
        "edge_sh": np.pad(np.asarray(edge_attr_4), ((0, pad), (0, 0))),
        "edge_rad": rad,
    }
    attn = np.zeros((H * D, 2 * H), np.float32)
    for h in range(H):
        attn[h * D:(h + 1) * D, h] = np.asarray(L1_gnn_attn_l)[h]
        attn[h * D:(h + 1) * D, H + h] = np.asarray(L1_gnn_attn_r)[h]
    self_w = np.zeros((D, D), np.float32)
    self_w[:MUL, :MUL] = np.asarray(L3_gnn_Ws)
    for i in range(3):
        self_w[MUL + i::3, MUL + i::3] = np.asarray(L3_gnn_Wv)
    weights = {
        "W0": np.asarray(L0_gnn_W), "gatT": np.asarray(L1_gnn_W_gat).T, "attn": attn,
        "wihT": np.asarray(L1_gnn_W_ih).T, "whhT": np.asarray(L1_gnn_W_hh).T,
        "b_ih": np.asarray(L1_gnn_b_ih).reshape(1, -1), "b_hh": np.asarray(L1_gnn_b_hh).reshape(1, -1),
        "W2g": np.asarray(L2_gnn_W), "b2g": np.tile(np.asarray(L2_gnn_b).reshape(1, -1), (NP_, 1)),
        "W1": np.asarray(L3_gnn_W1), "b1": np.asarray(L3_gnn_b1).reshape(-1, 1),
        "W2": np.asarray(L3_gnn_W2), "b2": np.asarray(L3_gnn_b2).reshape(-1, 1),
        "W3": np.asarray(L3_gnn_W3), "b3": np.asarray(L3_gnn_b3).reshape(1, -1),
        "self": self_w,
    }
    nc = bacc.Bacc("TRN2", target_bir_lowering=False, num_devices=1)
    arrays = {f"in_{n}": a(v) for n, v in {**data, **weights}.items()}
    aps = {n: nc.dram_tensor(n, v.shape, mybir.dt.from_np(v.dtype), kind="ExternalInput").ap() for n, v in arrays.items()}
    out = nc.dram_tensor("out", (N, D), F32, kind="ExternalOutput").ap()
    program(nc, *(aps[f"in_{n}"] for n in data), {n: aps[f"in_{n}"] for n in weights}, out)
    r = run_bass_kernel_spmd(nc, [arrays], core_ids=[0])
    return r.results[0]["out"]
```

```python
import concourse.bass as bass
from concourse import mybir
from contextlib import ExitStack, contextmanager
from itertools import count
import numpy as np

F32 = mybir.dt.float32
BF16 = mybir.dt.bfloat16
I32 = mybir.dt.int32
ALU = mybir.AluOpType
ACT = mybir.ActivationFunctionType
AX = mybir.AxisListType

P = 128
N = 12500
E = 212500
D = 32
H = 4
J = 32
EC = 1664
CHUNKS = EC // J
PAIRS = CHUNKS // 2
EROWS = P * EC
NP_ = 125
NC_ = 100
G = 10
GROUPS = NC_ // G
QUADS = [(0, 4), (4, 4), (8, 2)]
OH = 8
ROW1 = 2 * H + H * D
T1W = D + 2 * H
BIG = 1e30
EPS = 1e-5
ROUND = 12582912.0
HR = 64
NTP = 256
MUL = 8
ALPHA = 1.0 / np.sqrt(2.0 * MUL)
INV_SQRT3 = 1.0 / np.sqrt(3.0)
NBRS = float(np.sqrt(16.0))
SC = 8
RC = 4
RW = RC * P
RSTEPS = J // RC

assert EC % (2 * J) == 0 and P * EC >= E and NP_ * NC_ == N and NC_ % (2 * G) == 0


class Graph:
    pass


@contextmanager
def stage(nc, g):
    with ExitStack() as ph:
        used = []

        def sem(name):
            used.append(ph.enter_context(nc.semaphore(name)))
            return used[-1]

        def gather_sem(k):
            return g.sem_for_good(f"gathered{next(g.gather_count)}_{k}")
        g.sem, g.gather_sem = sem, gather_sem
        yield
        with nc.Block() as block:
            @block.gpsimd
            def _(pool):
                for one in used:
                    pool.sem_clear(one)


def bcast(ap, axis, count):
    ap = ap.unsqueeze(axis)
    return ap.broadcast_to([count if k == axis else n for k, n in enumerate(ap.shape)])



def load_weights(nc, g, w):
    with ExitStack() as ph:
        sb = lambda n, s, d=F32: ph.enter_context(nc.sbuf_tensor(n, s, d))
        sem = g.sem
        cleared, loaded, made, ids, trans = sem("w_cleared"), sem("w_loaded"), sem("w_made"), sem("w_ids"), sem("w_mm")
        gatT_bd = sb("gatT_bd", [P, P])
        gatT_rep = sb("gatT_rep", [P, P])
        attn = sb("attn", [P, 2 * H])
        ihT = sb("ihT", [P, 96])
        whh = sb("whh_rows", [P, 96])
        w3raw = sb("w3raw", [HR + 1, NTP])
        bih = sb("bih", [2 * D + 1, 96])
        bhh = sb("bhh", [2 * D + 1, 96])
        psA = g.ps[:, 0, :]
        psB = g.ps[:, 1, :]
        n_load = [0]
        with nc.Block() as block:
            @block.sync
            def _(sp):
                def load(dst, src):
                    n_load[0] += 1
                    sp.dma_start(dst, src).then_inc(loaded, 16)
                sp.wait_ge(cleared, 1)
                for c in range(4):
                    r = slice(D * c, D * c + D)
                    load(g.bd0[r, D * c:D * c + D], w["W0"][:, :])
                    load(g.bd2[r, D * c:D * c + D], w["W2g"][:, :])
                    load(gatT_bd[r, D * c:D * c + D], w["gatT"][r, :])
                    load(gatT_rep[:, D * c:D * c + D], w["gatT"][:, :])
                    load(whh[r, :], w["whhT"][:, :])
                    load(g.bdself[r, D * c:D * c + D], w["self"][:, :])
                load(attn[:, :], w["attn"][:, :])
                load(ihT[:, :], w["wihT"][:, :])
                load(bih[2 * D:2 * D + 1, :], w["b_ih"])
                load(bhh[2 * D:2 * D + 1, :], w["b_hh"])
                load(g.w1[:, :], w["W1"][:, :])
                load(g.w2[:, :], w["W2"][:, :])
                load(g.b1[:, :], w["b1"])
                load(g.b2[:, :], w["b2"])
                load(w3raw[0:HR, :], w["W3"][:, :])
                load(w3raw[HR:HR + 1, :], w["b3"])
                load(g.b2row[:, :], w["b2g"])

            @block.vector
            def _(dve):
                for t in (gatT_bd, g.bd0, g.bd2, g.bdself, g.bdel):
                    nc.vector.memset(t[:, :], 0.0)
                nc.vector.memset(g.bdhh[:, :, :], 0.0)
                nc.vector.memset(g.wc[:, :], 0.0)
                dve.drain().then_inc(cleared, 1)
                dve.wait_ge(loaded, 16 * n_load[0])
                for c in range(2):
                    r = slice(D * c, D * c + D)
                    nc.vector.tensor_copy(g.bdhh[r, c, 0:64], whh[r, 0:64])
                    nc.vector.tensor_copy(g.bdhh[r, c, 96:128], whh[r, 64:96])
                    bias = g.bdhh[2 * D:2 * D + 1, c, :]
                    nc.vector.tensor_tensor(bias[:, 0:64], bih[64:65, 0:64], bhh[64:65, 0:64], ALU.add)
                    nc.vector.tensor_copy(bias[:, 64:96], bih[64:65, 64:96])
                    nc.vector.tensor_copy(bias[:, 96:128], bhh[64:65, 64:96])
                nc.vector.tensor_scalar(g.bdself[:, :], g.bdself[:, :], float(1.0 / np.sqrt(MUL)), None, ALU.mult)
                k = float(ALPHA / NBRS)
                src = w3raw[:, :].rearrange("r (b u w) -> r b w u", b=4, u=MUL)
                dst = g.w3p[:, :].rearrange("r (b w u) -> r b w u", b=4, u=MUL)
                for block_, factor in enumerate((k, k * INV_SQRT3, k, k)):
                    nc.vector.tensor_scalar(dst[:, block_], src[:, block_], float(factor), None, ALU.mult)
                dve.wait_ge(trans, 2)
                nc.vector.tensor_copy(g.wc[:, 0:96], psA[:, 0:96])
                for c in range(4):
                    r = slice(D * c, D * c + D)
                    nc.vector.tensor_copy(g.bdel[r, 8 * c:8 * c + 8], psB[r, 0:8])
                dve.drain().then_inc(made, 1)

            @block.gpsimd
            def _(pool):
                nc.gpsimd.memset(g.ident[:, :], 0.0)
                nc.gpsimd.memset(g.ltri[:, :], 1.0)
                nc.gpsimd.iota(g.iota_i[:, :], pattern=[[1, P]], base=0, channel_multiplier=0)
                nc.gpsimd.iota(g.node_i[:, :], pattern=[[1, NC_]], base=0, channel_multiplier=NC_)
                nc.gpsimd.iota(g.first_edge_i[:, :], pattern=[[1, 1]], base=0, channel_multiplier=EC)
                pool.drain()
                nc.gpsimd.affine_select(out=g.ident[:, :], in_=g.ident[:, :], compare_op=ALU.not_equal, fill=1.0,
                                        base=0, pattern=[[-1, P]], channel_multiplier=1)
                nc.gpsimd.affine_select(out=g.ltri[:, :], in_=g.ltri[:, :], compare_op=ALU.is_gt, fill=0.0,
                                        base=0, pattern=[[1, P]], channel_multiplier=-1)
                pool.drain().then_inc(ids, 1)

            @block.tensor
            def _(pe):
                pe.wait_ge(loaded, 16 * n_load[0])
                nc.tensor.matmul(psA[:, 0:96], gatT_bd[:, :], ihT[:, :], start=True, stop=True).then_inc(trans, 1)
                nc.tensor.matmul(psB[:, 0:8], gatT_rep[:, :], attn[:, :], start=True, stop=True).then_inc(trans, 1)



def gather_chunks(nc, g, pool, table, buf, s):
    for b in range(2):
        pool.sem_inc(s.buf_free[b], 16)
    with pool.Fori(0, PAIRS) as i:
        for b in range(2):
            pool.wait_ge(s.idx_in[b], 16 * i + 16)
            pool.wait_ge(s.buf_free[b], 16 * i + 16)
            pool.nop(nofuse=True)
            for j in range(J):
                pool.indirect_dma_start(buf[:, b, j, :], None, table,
                                        bass.IndirectOffsetOnAxis(g.idx[:, b, j:j + 1], 0)).then_inc(s.rows_in[b], 16)


def chunk_cols(i, b, width=1):
    return bass.ds(i * (2 * J * width) + b * J * width, J * width)


class EdgeSems:

    def __init__(self, sem, gather_sem, name):
        self.idx_in = [sem(f"{name}_idx_in{b}") for b in range(2)]
        self.rows_in = [gather_sem(b) for b in range(2)]
        self.buf_free = [sem(f"{name}_buf_free{b}") for b in range(2)]
        self.scanned = [sem(f"{name}_scanned{b}") for b in range(2)]


def scan_rows(nc, g, dve, i, b, buf, carry, width):
    cont = g.cont[:, chunk_cols(i, b)]
    for f in range(width):
        nc.vector.tensor_tensor_scan(buf[:, b, :, f], cont, buf[:, b, :, f], carry[:, f:f + 1], ALU.mult, ALU.add)
    dve.drain()
    nc.vector.tensor_copy(carry[:, 0:width], buf[:, b, J - 1, :])
    

def radial_tensor(nc, g, pe, rad, h1, r):
    def second_layer(i, n):
        k = n % 2
        pe.wait_ge(r.h1_out[k], i * RSTEPS + n // 2 + 1)
        pe.nop(nofuse=True)
        nc.tensor.matmul(g.ps[0:HR, 4 + k, :], g.w2[:, :], h1[:, k, :], start=True, stop=True).then_inc(r.h2_in[k], 1)

    with pe.Fori(0, PAIRS) as i:
        for b in range(2):
            pe.wait_ge(r.rad_in[b], 16 * i + 16)
            for m in range(RSTEPS):
                n = b * RSTEPS + m
                k = n % 2
                nc.tensor.matmul(g.ps[0:HR, 2 + k, :], g.w1[:, :], rad[:, b, m * RW:(m + 1) * RW], start=True, stop=True)\
                    .then_inc(r.h1_in[k], 1)
                if m == RSTEPS - 1:
                    pe.drain().then_inc(r.rad_free[b], 1)
                if n > 0:
                    second_layer(i, n - 1)
        second_layer(i, 2 * RSTEPS - 1)


def radial_scalar(nc, g, act, rad, h1, h2, r):
    def second_layer(i, n):
        k, b, m = n % 2, n // RSTEPS, n % RSTEPS
        if m == 0:
            act.wait_ge(r.h2_free[b], 16 * i + 16)
        act.wait_ge(r.h2_in[k], i * RSTEPS + n // 2 + 1)
        nc.scalar.activation(h2[:, b, m * RW:(m + 1) * RW], g.ps[0:HR, 4 + k, :], ACT.Silu, bias=g.b2[:, 0:1])
        if m == RSTEPS - 1:
            act.drain().then_inc(r.h2_made[b], 1)
            act.wait_ge(r.h2_made[b], i + 1)
            act.dma_start(g.hidden[:, chunk_cols(i, b, P)], h2[:, b, :]).then_inc(r.h2_free[b], 16)
            act.wait_ge(r.rad_free[b], i + 1)
            act.dma_start(rad[:, b, :], g.edge_rad[:, bass.ds(i * (2 * J * P) + (b + 2) * J * P, J * P)])\
               .then_inc(r.rad_in[b], 16)

    with act.Fori(0, PAIRS) as i:
        for n in range(2 * RSTEPS):
            k = n % 2
            act.wait_ge(r.h1_in[k], i * RSTEPS + n // 2 + 1)
            nc.scalar.activation(h1[:, k, :], g.ps[0:HR, 2 + k, :], ACT.Silu, bias=g.b1[:, 0:1]).then_inc(r.h1_out[k], 1)
            if n > 0:
                second_layer(i, n - 1)
        second_layer(i, 2 * RSTEPS - 1)
    for b in range(2):
        act.wait_ge(r.h2_free[b], 16 * PAIRS + 16)
        act.wait_ge(r.rad_in[b], 16 * PAIRS + 16)


class RadialSems:
    def __init__(self, sem):
        pair = lambda n: [sem(f"radial_{n}{b}") for b in range(2)]
        self.rad_in, self.rad_free, self.h1_in, self.h1_out = pair("in"), pair("free"), pair("h1_in"), pair("h1_out")
        self.h2_in, self.h2_made, self.h2_free = pair("h2_in"), pair("h2_made"), pair("h2_free")


def edge_stage_plain(nc, g, name, table, rows, first):
    with ExitStack() as ph:
        sb = lambda n, s, d=F32: ph.enter_context(nc.sbuf_tensor(f"{name}_{n}", s, d))
        s = EdgeSems(g.sem, g.gather_sem, name)
        buf = sb("rows", [P, 2, J, D])
        if first:
            dst_i = sb("dst_i", [P, EC], I32)
            prev_i = sb("prev_i", [P, EC], I32)
            src_i = sb("src_i", [P, EC], I32)
            dst_f = sb("dst_f", [P, EC])
            src_f = sb("src_f", [P, EC])
            tmp_f = sb("tmp_f", [P, EC])
            hi = sb("hi", [P, 2, EC], BF16)
            lo = sb("lo", [P, 2, EC], BF16)
            iota_b = sb("iota_b", [P, P], BF16)
            onehot_hi = sb("onehot_hi", [P, 2, 2, OH, NP_], BF16)
            onehot_lo = sb("onehot_lo", [P, 2, 2, OH, NC_], BF16)
            zero_b = sb("zero_b", [P, P], BF16)
            graph_in, oh_used, oh_made, hist_zero, hist_done = (
                g.sem("graph_in"), [g.sem(f"oh_used{b}") for b in range(2)], [g.sem(f"oh_made{b}") for b in range(2)],
                g.sem("hist_zero"), g.sem("hist_done"))
            er_zero = g.sem("er_zero")
            zeroed = g.sem("zeroed")
        else:
            rs = RadialSems(g.sem)
            rad = sb("rad", [8, 2, J * P])
            h1 = sb("h1", [HR, 2, RW])
            h2 = sb("h2", [HR, 2, J * P])
        with nc.Block() as block:
            @block.gpsimd
            def _(pool):
                if not first:
                    for b in range(2):
                        pool.sem_inc(rs.h2_free[b], 16)
                gather_chunks(nc, g, pool, table, buf, s)

            @block.sync
            def _(sp):
                if first:
                    dst_cols = lambda o: g.dst_flat[0:1, o:o + EROWS].rearrange("a (p c) -> (a p) c", c=EC)
                    for b in range(2):
                        sp.dma_start(g.idx[:, b, :], g.src_cols[:, b * J:(b + 1) * J]).then_inc(s.idx_in[b], 16)
                    sp.dma_start(dst_i[:, :], dst_cols(1)).then_inc(graph_in, 16)
                    sp.dma_start(prev_i[:, :], dst_cols(0)).then_inc(graph_in, 16)
                    sp.dma_start(src_i[:, :], g.src_cols[:, 0:EC]).then_inc(graph_in, 16)
                    sp.wait_ge(zeroed, 1)
                    for k in range(4):
                        sp.dma_start(g.er_edges[0:EROWS, :].rearrange("(p c) h -> p (c h)", p=P)[:, k * EC:(k + 1) * EC],
                                     tmp_f[:, :]).then_inc(er_zero, 16)
                    for r, width in ((g.rows0, D), (g.rows1, ROW1), (g.rows2, D), (g.rows3, D)):
                        sp.dma_start(r[EROWS:EROWS + 1, :], tmp_f[0:1, 0:width]).then_inc(er_zero, 16)
                else:
                    for b in range(2):
                        sp.dma_start(g.idx[:, b, :], g.src_cols[:, b * J:(b + 1) * J]).then_inc(s.idx_in[b], 16)
                        sp.dma_start(rad[:, b, :], g.edge_rad[:, b * J * P:(b + 1) * J * P]).then_inc(rs.rad_in[b], 16)
                rows_v = rows[0:EROWS, :].rearrange("(p c) f -> p (c f)", p=P)
                with sp.Fori(0, PAIRS) as i:
                    for b in range(2):
                        sp.wait_ge(s.rows_in[b], (16 * J) * i + 16 * J)
                        sp.dma_start(g.idx[:, b, :], g.src_cols[:, bass.ds(i * (2 * J) + (b + 2) * J, J)])\
                          .then_inc(s.idx_in[b], 16)
                        sp.wait_ge(s.scanned[b], i + 1)
                        sp.dma_start(rows_v[:, chunk_cols(i, b, D)], buf[:, b].rearrange("p j f -> p (j f)"))\
                          .then_inc(s.buf_free[b], 16)
                for b in range(2):
                    sp.wait_ge(s.buf_free[b], 16 * PAIRS + 16)
                    sp.wait_ge(s.idx_in[b], 16 * PAIRS + 16)
                if first:
                    sp.wait_ge(er_zero, 16 * 8)

            @block.vector
            def _(dve):
                if first:
                    nc.vector.memset(tmp_f[:, :], 0.0)
                    nc.vector.memset(zero_b[:, :], 0.0)
                    dve.drain().then_inc(zeroed, 1)
                    nc.vector.tensor_copy(iota_b[:, :], g.iota_i[:, :])
                    dve.wait_ge(graph_in, 48)
                    nc.vector.tensor_tensor(g.cont[:, :], dst_i[:, :], prev_i[:, :], ALU.is_equal)
                    nc.vector.tensor_copy(dst_f[:, :], dst_i[:, :])
                    nc.vector.tensor_copy(src_f[:, :], src_i[:, :])
                    dve.drain()
                    dve.wait_ge(er_zero, 16 * 8)
                    nc.vector.tensor_scalar(g.dst0_f[:, :], dst_f[:, 0:1], float(N - 1), None, ALU.min)
                    for k, n_f in enumerate((src_f, dst_f)):
                        nc.vector.tensor_scalar(tmp_f[:, :], n_f[:, :], 1.0 / NC_, -0.495, ALU.mult, ALU.add)
                        dve.drain()
                        nc.vector.tensor_scalar(tmp_f[:, :], tmp_f[:, :], ROUND, ROUND, ALU.add, ALU.subtract)
                        dve.drain()
                        nc.vector.scalar_tensor_tensor(lo[:, k, :], tmp_f[:, :], -float(NC_), n_f[:, :], ALU.mult, ALU.add)
                        nc.vector.tensor_copy(hi[:, k, :], tmp_f[:, :])
                        dve.drain()
                    nc.vector.tensor_scalar(tmp_f[:, :], dst_f[:, :], float(N), 2.0 * NP_, ALU.is_ge, ALU.mult)
                    nc.vector.tensor_copy(g.dst0_i[:, :], g.dst0_f[:, :])
                    dve.drain()
                    nc.vector.tensor_tensor(hi[:, 0, :], hi[:, 0, :], tmp_f[:, :], ALU.add)
                nc.vector.memset(g.carry[:, :], 0.0)
                dve.drain()
                with dve.Fori(0, PAIRS) as i:
                    for b in range(2):
                        if first:
                            for k in range(J // OH):
                                h = k % 2
                                dve.wait_ge(oh_used[h], i * (J // OH) + (b * (J // OH) + k) // 2 + 1)
                                cols = bass.ds(i * (2 * J) + (b * J + k * OH), OH)
                                for e in range(2):
                                    nc.vector.tensor_tensor(
                                        onehot_hi[:, h, e], bcast(iota_b[:, 0:NP_], 1, OH),
                                        bcast(hi[:, e, cols], 2, NP_), ALU.is_equal)
                                    last = nc.vector.tensor_tensor(
                                        onehot_lo[:, h, e], bcast(iota_b[:, 0:NC_], 1, OH),
                                        bcast(lo[:, e, cols], 2, NC_), ALU.is_equal)
                                dve.drain().then_inc(oh_made[h], 1)
                        dve.wait_ge(s.rows_in[b], (16 * J) * i + 16 * J)
                        scan_rows(nc, g, dve, i, b, buf, g.carry, D)
                        dve.drain().then_inc(s.scanned[b], 1)
                if first:
                    dve.wait_ge(hist_done, 1)
                    nc.vector.tensor_copy(g.deg[:, 0, :], g.ps[0:NP_, 0, 0:NC_])
                    nc.vector.tensor_copy(g.deg[:, 1, :], g.ps[0:NP_, 1, 0:NC_])
                    dve.drain()

            if not first:
                @block.tensor
                def _(pe):
                    radial_tensor(nc, g, pe, rad, h1, rs)

                @block.scalar
                def _(act):
                    radial_scalar(nc, g, act, rad, h1, h2, rs)
            else:
                @block.tensor
                def _(pe):
                    pe.wait_ge(zeroed, 1)
                    for e in range(2):
                        nc.tensor.matmul(g.ps[0:NP_, e, 0:NC_], zero_b[:, 0:NP_], zero_b[:, 0:NC_], start=True, stop=False)
                    for h in range(2):
                        pe.sem_inc(oh_used[h], 1)
                    with pe.Fori(0, CHUNKS) as i:
                        for k in range(J // OH):
                            h = k % 2
                            pe.wait_ge(oh_made[h], i * (J // OH // 2) + k // 2 + 1)
                            for e in range(2):
                                for c in range(OH):
                                    last = nc.tensor.matmul(g.ps[0:NP_, e, 0:NC_], onehot_hi[:, h, e, c, :],
                                                            onehot_lo[:, h, e, c, :], start=False, stop=False)
                            last.then_inc(oh_used[h], 1)
                    for e in range(2):
                        last = nc.tensor.matmul(g.ps[0:NP_, e, 0:NC_], zero_b[:, 0:NP_], zero_b[:, 0:NC_],
                                                start=False, stop=True)
                    last.then_inc(hist_done, 1)


def index_stage(nc, g):
    with ExitStack() as ph:
        sb = lambda n, s, d=F32: ph.enter_context(nc.sbuf_tensor(f"ix_{n}", s, d))
        run = sb("run", [NP_, NC_])
        ones = sb("ones", [NP_, NC_])
        node = sb("node", [NP_, NC_])
        last_e = sb("last_e", [NP_, NC_])
        first_e = sb("first_e", [NP_, NC_])
        alt = sb("alt", [NP_, NC_])
        empty = sb("empty", [NP_, NC_])
        base = sb("base", [NP_, 1])
        prod = sb("prod", [P, EC])
        lead = sb("lead", [P, 1])
        fe = sb("fe", [P, 1])
        flag = sb("flag", [P, 1])
        whole = sb("whole", [P, 1])
        flags_wide = sb("flags_wide", [P, 2, P])
        run_made, base_made, flags_made, flags_turned = (g.sem("ix_run"), g.sem("ix_base"), g.sem("ix_flags"), g.sem("ix_turned"))
        norm_in, norm_out = g.sem("ix_norm_in"), g.sem("ix_norm_out")
        with nc.Block() as block:
            @block.vector
            def _(dve):
                v = nc.vector
                v.memset(ones[:, :], 1.0)
                v.tensor_copy(node[:, :], g.node_i[0:NP_, :])
                v.tensor_scalar(g.norm[:, :, :], g.deg[:, :, :], 1.0, None, ALU.max)
                dve.drain().then_inc(norm_in, 1)
                v.tensor_tensor_scan(run[:, :], ones[:, :], g.deg[:, 1, :], 0.0, ALU.mult, ALU.add)
                dve.drain().then_inc(run_made, 1)
                v.tensor_tensor_scan(prod[:, 0:EC - 1], g.cont[:, 1:EC], g.cont[:, 1:EC], 1.0, ALU.mult, ALU.min)
                v.tensor_copy(fe[:, :], g.first_edge_i[:, :])
                dve.drain()
                v.reduce_sum(lead[:, :], prod[:, 0:EC - 1], axis=AX.X)
                v.tensor_tensor(whole[:, :], prod[:, EC - 2:EC - 1], g.cont[:, 0:1], ALU.mult)
                dve.drain()
                v.tensor_tensor(fe[:, :], fe[:, :], lead[:, :], ALU.add)
                v.tensor_copy(flags_wide[:, 0, :], g.cont[:, 0:1].broadcast_to([P, P]))
                v.tensor_copy(flags_wide[:, 1, :], whole[:, 0:1].broadcast_to([P, P]))
                dve.drain().then_inc(flags_made, 1)
                v.tensor_copy(g.border_idx[:, :], fe[:, :])
                dve.wait_ge(base_made, 1)
                v.tensor_copy(base[:, :], g.ps[0:NP_, 2, 0:1])
                v.tensor_scalar(empty[:, :], g.deg[:, 1, :], 0.0, None, ALU.is_equal)
                dve.drain()
                v.tensor_scalar(last_e[:, :], run[:, :], base[:, 0:1], -1.0, ALU.add, ALU.add)
                dve.drain()
                v.tensor_tensor(first_e[:, :], last_e[:, :], g.deg[:, 1, :], ALU.subtract)
                v.tensor_scalar(alt[:, :], last_e[:, :], -1.0, float(EROWS), ALU.mult, ALU.add)
                dve.drain()
                v.tensor_scalar(first_e[:, :], first_e[:, :], 1.0, None, ALU.add)
                v.tensor_tensor(alt[:, :], alt[:, :], empty[:, :], ALU.mult)
                dve.drain()
                v.tensor_tensor(last_e[:, :], last_e[:, :], alt[:, :], ALU.add)
                dve.drain()
                v.tensor_scalar(node[:, :], node[:, :], float(EROWS), None, ALU.add)
                dve.drain()
                v.tensor_tensor(node[:, :], node[:, :], first_e[:, :], ALU.subtract)
                dve.drain()
                v.tensor_tensor(node[:, :], node[:, :], empty[:, :], ALU.mult)
                dve.drain()
                v.tensor_tensor(first_e[:, :], first_e[:, :], node[:, :], ALU.add)
                v.memset(g.last_i[:, NC_:NC_ + 2 * G], 0)
                v.tensor_copy(g.last_i[:, 0:NC_], last_e[:, :])
                dve.drain()
                v.tensor_copy(g.first_i[:, :], first_e[:, :])
                dve.wait_ge(norm_out, 1)
                v.reciprocal(g.norm[:, :, :], g.norm[:, :, :])
                dve.wait_ge(flags_turned, 1)
                v.tensor_copy(g.cont0[:, :], g.ps[:, 3, 0:P])
                v.tensor_copy(g.linked[:, :], g.ps[:, 3, P:2 * P])
                v.memset(g.link[:, :], 0.0)
                dve.drain()
                v.tensor_tensor(g.link[:, 1:P], g.cont0[:, 1:P], g.linked[:, 0:P - 1], ALU.mult)
                dve.drain()

            @block.scalar
            def _(act):
                act.wait_ge(norm_in, 1)
                nc.scalar.activation(g.norm[:, :, :], g.norm[:, :, :], ACT.Sqrt).then_inc(norm_out, 1)

            @block.tensor
            def _(pe):
                pe.wait_ge(run_made, 1)
                nc.tensor.matmul(g.ps[0:NP_, 2, 0:1], g.ltri[0:NP_, 0:NP_], run[:, NC_ - 1:NC_],
                                 start=True, stop=True).then_inc(base_made, 1)
                pe.wait_ge(flags_made, 1)
                nc.tensor.transpose(g.ps[:, 3, 0:P], flags_wide[:, 0, :], g.ident[:, :])
                nc.tensor.transpose(g.ps[:, 3, P:2 * P], flags_wide[:, 1, :], g.ident[:, :]).then_inc(flags_turned, 1)


def border_stage_plain(nc, g, name, rows):
    with ExitStack() as ph:
        sb = lambda n, s, d=F32: ph.enter_context(nc.sbuf_tensor(f"{name}_{n}", s, d))
        patch = sb("patch", [P, D])
        item = sb("item", [D, P])
        into = sb("into", [D, P])
        turned, into_made, back, patched = (g.sem(f"{name}_{n}") for n in ("turned", "into", "back", "patched"))
        fetched, put = g.gather_sem(0), g.gather_sem(1)
        with nc.Block() as block:
            @block.tensor
            def _(pe):
                nc.tensor.transpose(g.ps[0:D, 0, 0:P], g.carry[:, 0:D], g.ident[:, :]).then_inc(turned, 1)
                pe.wait_ge(into_made, 1)
                nc.tensor.transpose(g.ps[:, 1, 0:D], into[:, :], g.ident[0:D, 0:D]).then_inc(back, 1)

            @block.vector
            def _(dve):
                nc.vector.memset(item[:, :], 0.0)
                dve.drain()
                dve.wait_ge(turned, 1)
                nc.vector.tensor_tensor(item[:, 1:P], g.cont0[0:D, 1:P], g.ps[0:D, 0, 0:P - 1], ALU.mult)
                dve.drain()
                nc.vector.tensor_tensor_scan(into[:, :], g.link[0:D, :], item[:, :], 0.0, ALU.mult, ALU.add)\
                    .then_inc(into_made, 1)
                dve.wait_ge(back, 1)
                dve.wait_ge(fetched, 16)
                nc.vector.tensor_tensor(patch[:, :], patch[:, :], g.ps[:, 1, 0:D], ALU.add).then_inc(patched, 1)

            @block.gpsimd
            def _(pool):
                pool.indirect_dma_start(patch[:, :], None, rows[:, :], bass.IndirectOffsetOnAxis(g.border_idx[:, 0:1], 0))\
                    .then_inc(fetched, 16)
                pool.wait_ge(patched, 1)
                pool.indirect_dma_start(rows[:, :], bass.IndirectOffsetOnAxis(g.border_idx[:, 0:1], 0), patch[:, :], None)\
                    .then_inc(put, 16)
                pool.wait_ge(put, 16)



class NodeSems:

    def __init__(self, sem, gather_sem, name):
        pair = lambda n: [sem(f"{name}_{n}{b}") for b in range(2)]
        self.gathered = [gather_sem(b) for b in range(2)]
        self.idx_ready, self.x_in, self.free = pair("idx_ready"), pair("x_in"), pair("free")
        self.stored, self.new_ready = pair("stored"), pair("new_ready")
        self.turned, self.turned_sb, self.product = pair("turned"), pair("turned_sb"), pair("product")
        self.x_turned, self.x_turned_sb, self.x_product = pair("x_turned"), pair("x_turned_sb"), pair("x_product")
        self.agg_ready, self.var, self.std, self.prods_used = pair("agg_ready"), pair("var"), pair("std"), pair("prods_used")
        self.gates_act, self.hidden, self.hidden_act = pair("gates_act"), pair("hidden"), pair("hidden_act")
        self.low, self.low_act = pair("low"), pair("low_act")


def load_residual(nc, g, sp, s, xg, x_rows):
    x_v = x_rows.rearrange("(p j) f -> p (j f)", p=NP_)

    def load(i, b):
        sp.dma_start(xg[:, b].rearrange("p j f -> p (j f)"), x_v[:, bass.ds(i * (2 * G * D) + b * G * D, G * D)])\
          .then_inc(s.x_in[b], 16)
    for b in range(2):
        load(0, b)
    with sp.Fori(0, GROUPS // 2 - 1) as i:
        for b in range(2):
            sp.wait_ge(s.free[b], i + 1)
            load(i + 1, b)


def group_cols(i, b):
    return bass.ds(i * (2 * G) + b * G, G)


def next_index(nc, g, dve, s, nidx, i, b):
    nc.vector.tensor_copy(nidx[:, b, :], g.last_i[:, group_cols(i, b)])
    dve.drain().then_inc(s.idx_ready[b], 1)


def node_gathers(nc, g, pool, s, nidx, agg, rows):
    with pool.Fori(0, GROUPS // 2) as i:
        for b in range(2):
            pool.wait_ge(s.idx_ready[b], i + 1)
            pool.nop(nofuse=True)
            for j in range(G):
                pool.indirect_dma_start(agg[:, b, j, :], None, rows[:, :],
                                        bass.IndirectOffsetOnAxis(nidx[:, b, j:j + 1], 0)).then_inc(s.gathered[b], 16)


def node_stores(nc, g, eng, s, i, b, new, dests):
    eng.wait_ge(s.new_ready[b], i + 1)
    for buf, rows in dests:
        width = rows.shape[1]
        eng.dma_start(rows.rearrange("(p j) f -> p (j f)", p=NP_)[:, bass.ds(i * (2 * G * width) + b * G * width, G * width)],
                      buf[:, b].rearrange("p j f -> p (j f)")).then_inc(s.stored[b], 16)


def turn_group(nc, g, pe, src, psum):
    for q, (c, k) in enumerate(QUADS):
        last = nc.tensor.transpose(psum[0:k * D, q * P:q * P + NP_], src[:, c:c + k, :].rearrange("p j f -> p (j f)"),
                                   g.ident[0:NP_, 0:NP_])
    return last


def copy_turned(nc, turned, psum):
    nc.scalar.activation(turned[:, 0:2, 0:NP_], psum[:, 0:2 * P].rearrange("p (q n) -> p q n", q=2)[:, :, 0:NP_], ACT.Copy)
    return nc.scalar.activation(turned[0:2 * D, 2, 0:NP_], psum[0:2 * D, 2 * P:2 * P + NP_], ACT.Copy)


def apply_bd(nc, pe, psum, turned, weight, width):
    for q, (c, k) in enumerate(QUADS):
        last = nc.tensor.matmul(psum[0:NP_, c * width:(c + k) * width], turned[0:k * D, q, 0:NP_],
                                weight[0:k * D, 0:k * width], start=True, stop=True)
    return last


def layernorm_moments(nc, dve, s, b, r, t, stat):
    v = nc.vector
    v.reduce_sum(stat[:, b, 0, :], r, axis=AX.X)
    dve.drain()
    v.tensor_scalar(stat[:, b, 1, :], stat[:, b, 0, :], 1.0 / D, None, ALU.mult)
    dve.drain()
    v.tensor_tensor(r, r, bcast(stat[:, b, 1, :], 2, D), ALU.subtract)
    dve.drain()
    v.tensor_tensor(t, r, r, ALU.mult)
    dve.drain()
    v.reduce_sum(stat[:, b, 0, :], t, axis=AX.X)
    dve.drain()
    v.tensor_scalar(stat[:, b, 2, :], stat[:, b, 0, :], 1.0 / D, EPS, ALU.mult, ALU.add).then_inc(s.var[b], 1)


def layernorm_scale(nc, dve, s, i, b, r, stat, out):
    dve.wait_ge(s.std[b], i + 1)
    nc.vector.reciprocal(stat[:, b, 4, :], stat[:, b, 3, :])
    dve.drain()
    return nc.vector.tensor_tensor(out, r, bcast(stat[:, b, 4, :], 2, D), ALU.mult)


def layernorm_sqrt(nc, act, s, i, b, stat):
    act.wait_ge(s.var[b], i + 1)
    nc.scalar.activation(stat[:, b, 3, :], stat[:, b, 2, :], ACT.Sqrt).then_inc(s.std[b], 1)


def node_stage_plain(nc, g, name, layer, rows, x_in, dests):
    with ExitStack() as ph:
        sb = lambda n, s_, d=F32: ph.enter_context(nc.sbuf_tensor(f"{name}_{n}", s_, d))
        s = NodeSems(g.sem, g.gather_sem, name)
        nidx = sb("nidx", [NP_, 2, G], I32)
        xg = sb("xg", [NP_, 2, G, D])
        agg = sb("agg", [NP_, 2, G, D])
        turned = sb("turned", [P, 2, 3, P])
        xturned = sb("xturned", [P, 2, 3, P])
        r = sb("r", [NP_, 2, G, D])
        t = sb("t", [NP_, 2, G, D])
        stat = sb("stat", [NP_, 2, 5, G])
        new = sb("new", [NP_, 2, G, D])
        t1 = sb("t1", [NP_, 2, G, T1W])
        bd = {0: g.bd0, 2: g.bd2, 3: g.bdself}[layer]
        bufs = {"x": new, "t1": t1}
        n_dest = len(dests)
        with nc.Block() as block:
            @block.sync
            def _(sp):
                load_residual(nc, g, sp, s, xg, x_in)
                for b in range(2):
                    sp.wait_ge(s.stored[b], 16 * n_dest * (GROUPS // 2 + 1))

            @block.gpsimd
            def _(pool):
                for b in range(2):
                    pool.sem_inc(s.stored[b], 16 * n_dest)
                node_gathers(nc, g, pool, s, nidx, agg, rows)

            @block.tensor
            def _(pe):
                with pe.Fori(0, GROUPS // 2) as i:
                    for b in range(2):
                        if layer == 3:
                            pe.wait_ge(s.x_in[b], 16 * i + 16)
                            turn_group(nc, g, pe, xg[:, b], g.ps[:, b, :]).then_inc(s.turned[b], 1)
                        elif layer == 2:
                            pe.wait_ge(s.agg_ready[b], i + 1)
                            turn_group(nc, g, pe, r[:, b], g.ps[:, b, :]).then_inc(s.turned[b], 1)
                        else:
                            pe.wait_ge(s.gathered[b], 16 * G * i + 16 * G)
                            turn_group(nc, g, pe, agg[:, b], g.ps[:, b, :]).then_inc(s.turned[b], 1)
                        pe.wait_ge(s.turned_sb[b], i + 1)
                        apply_bd(nc, pe, g.ps[:, 2 + b, :], turned[:, b], bd, D).then_inc(s.product[b], 1)
                        if layer == 0:
                            pe.wait_ge(s.agg_ready[b], i + 1)
                            turn_group(nc, g, pe, new[:, b], g.ps[:, 4 + b, :]).then_inc(s.x_turned[b], 1)
                            pe.wait_ge(s.x_turned_sb[b], i + 1)
                            apply_bd(nc, pe, g.ps[:, 6 + b, :], xturned[:, b], g.bdel, 2 * H).then_inc(s.x_product[b], 1)

            @block.scalar
            def _(act):
                with act.Fori(0, GROUPS // 2) as i:
                    for b in range(2):
                        act.wait_ge(s.turned[b], i + 1)
                        copy_turned(nc, turned[:, b], g.ps[:, b, :]).then_inc(s.turned_sb[b], 1)
                        layernorm_sqrt(nc, act, s, i, b, stat)
                        if layer == 0:
                            act.wait_ge(s.x_turned[b], i + 1)
                            copy_turned(nc, xturned[:, b], g.ps[:, 4 + b, :]).then_inc(s.x_turned_sb[b], 1)
                        node_stores(nc, g, act, s, i, b, None, [(bufs[k], d) for k, d in dests])

            @block.vector
            def _(dve):
                v = nc.vector
                for b in range(2):
                    next_index(nc, g, dve, s, nidx, 0, b)
                with dve.Fori(0, GROUPS // 2) as i:
                    for b in range(2):
                        cols = group_cols(i, b)
                        dve.wait_ge(s.x_in[b], 16 * i + 16)
                        dve.wait_ge(s.gathered[b], 16 * G * i + 16 * G)
                        if layer == 2:
                            v.tensor_tensor(r[:, b], agg[:, b], bcast(g.norm[:, 1, cols], 2, D), ALU.mult)\
                                .then_inc(s.agg_ready[b], 1)
                            v.tensor_tensor(t[:, b], xg[:, b], bcast(g.b2row[:, :], 1, G), ALU.add)
                        if layer == 3:
                            v.tensor_tensor(t[:, b], xg[:, b], agg[:, b], ALU.add)
                        if layer != 0:
                            dve.drain()
                            next_index(nc, g, dve, s, nidx, i + 1, b)
                        dve.wait_ge(s.product[b], i + 1)
                        v.tensor_tensor(r[:, b], xg[:, b] if layer == 0 else t[:, b],
                                        g.ps[0:NP_, 2 + b, 0:G * D].rearrange("p (j f) -> p j f", f=D), ALU.add)
                        if layer == 0:
                            next_index(nc, g, dve, s, nidx, i + 1, b)
                        dve.drain().then_inc(s.free[b], 1)
                        dve.wait_ge(s.stored[b], 16 * n_dest * i + 16 * n_dest)
                        layernorm_moments(nc, dve, s, b, r[:, b], t[:, b], stat)
                        layernorm_scale(nc, dve, s, i, b, r[:, b], stat, new[:, b])
                        if layer == 0:
                            dve.drain().then_inc(s.agg_ready[b], 1)
                            v.tensor_copy(t1[:, b, :, 0:D], new[:, b])
                            dve.wait_ge(s.x_product[b], i + 1)
                            el_er = g.ps[0:NP_, 6 + b, 0:G * 2 * H].rearrange("p (j h) -> p j h", h=2 * H)
                            v.tensor_copy(t1[:, b, :, D:T1W], el_er)
                            v.tensor_copy(g.er_nodes[:, cols, :], el_er[:, :, H:2 * H])
                        dve.drain().then_inc(s.new_ready[b], 1)


def spread_er_stage(nc, g):
    put, got = g.gather_sem(0), g.gather_sem(1)
    with nc.Block() as block:
        @block.gpsimd
        def _(pool):
            for c in range(NC_):
                pool.indirect_dma_start(g.er_edges[:, :], bass.IndirectOffsetOnAxis(g.first_i[:, c:c + 1], 0),
                                        g.er_nodes[:, c, :], None).then_inc(put, 16)
            pool.indirect_dma_start(g.row_dst0[:, :], None, g.table1[:, :],
                                    bass.IndirectOffsetOnAxis(g.dst0_i[:, 0:1], 0)).then_inc(got, 16)
            pool.wait_ge(put, 16 * NC_)
            pool.wait_ge(got, 16)


def edge_stage_attention(nc, g):
    with ExitStack() as ph:
        sb = lambda n, s_, d=F32: ph.enter_context(nc.sbuf_tensor(f"e1_{n}", s_, d))
        s = EdgeSems(g.sem, g.gather_sem, "e1")
        gat = sb("gat", [P, 2, J, T1W])
        er0 = sb("er0", [P, 2, J, H])
        er = sb("er", [P, J, H])
        er_carry = sb("er_carry", [P, H])
        e = sb("e", [P, J, H])
        e2 = sb("e2", [P, J, H])
        neg = sb("neg", [P, J])
        expo = sb("expo", [P, 2, J, H])
        wexp = sb("wexp", [P, 2, J, H])
        acc = sb("acc", [P, 2, J, ROW1])
        er_in = [g.sem(f"e1_er_in{b}") for b in range(2)]
        gat_free = [g.sem(f"e1_gat_free{b}") for b in range(2)]
        expo_ready, wexp_ready = g.sem("e1_expo"), g.sem("e1_wexp")
        with nc.Block() as block:
            @block.gpsimd
            def _(pool):
                for b in range(2):
                    pool.sem_inc(gat_free[b], 1)
                    pool.sem_inc(s.buf_free[b], 16)
                with pool.Fori(0, PAIRS) as i:
                    for b in range(2):
                        pool.wait_ge(s.idx_in[b], 16 * i + 16)
                        pool.wait_ge(gat_free[b], i + 1)
                        pool.nop(nofuse=True)
                        for j in range(J):
                            pool.indirect_dma_start(gat[:, b, j, :], None, g.table1[:, :],
                                                    bass.IndirectOffsetOnAxis(g.idx[:, b, j:j + 1], 0)).then_inc(s.rows_in[b], 16)

            @block.sync
            def _(sp):
                er_v = g.er_edges[0:EROWS, :].rearrange("(p c) h -> p (c h)", p=P)
                chunk = lambda i, b, width: bass.ds(i * (2 * J * width) + b * J * width, J * width)
                for b in range(2):
                    sp.dma_start(g.idx[:, b, :], g.src_cols[:, b * J:(b + 1) * J]).then_inc(s.idx_in[b], 16)
                    sp.dma_start(er0[:, b].rearrange("p j h -> p (j h)"), er_v[:, b * J * H:(b + 1) * J * H]).then_inc(er_in[b], 16)
                with sp.Fori(0, PAIRS - 1) as i:
                    for b in range(2):
                        sp.wait_ge(s.rows_in[b], (16 * J) * i + 16 * J)
                        sp.dma_start(g.idx[:, b, :], g.src_cols[:, chunk(i, b + 2, 1)]).then_inc(s.idx_in[b], 16)
                        sp.wait_ge(gat_free[b], i + 2)
                        sp.dma_start(er0[:, b].rearrange("p j h -> p (j h)"), er_v[:, chunk(i, b + 2, H)]).then_inc(er_in[b], 16)
                for b in range(2):
                    sp.wait_ge(s.buf_free[b], 16 * PAIRS + 16)

            @block.scalar
            def _(act):
                rows_v = g.rows1[0:EROWS, :].rearrange("(p c) f -> p (c f)", p=P)
                with act.Fori(0, PAIRS) as i:
                    for b in range(2):
                        act.wait_ge(expo_ready, i * 2 + (b + 1))
                        nc.scalar.activation(wexp[:, :, :, :], expo[:, :, :, :], ACT.Exp).then_inc(wexp_ready, 1)
                        act.wait_ge(s.scanned[b], i + 1)
                        act.dma_start(rows_v[:, chunk_cols(i, b, ROW1)], acc[:, b].rearrange("p j f -> p (j f)"))\
                           .then_inc(s.buf_free[b], 16)

            @block.vector
            def _(dve):
                v = nc.vector
                v.memset(g.carry[:, 0:H], -BIG)
                v.memset(g.carry[:, H:ROW1], 0.0)
                v.tensor_copy(er_carry[:, :], g.row_dst0[:, D + H:T1W])
                dve.drain()
                with dve.Fori(0, PAIRS) as i:
                    for b in range(2):
                        cont = g.cont[:, chunk_cols(i, b)]
                        v.tensor_scalar(neg[:, :], cont, BIG, BIG, ALU.mult, ALU.subtract)
                        dve.wait_ge(er_in[b], 16 * i + 16)
                        for h in range(H):
                            v.tensor_tensor_scan(er[:, :, h], cont, er0[:, b, :, h], er_carry[:, h:h + 1], ALU.mult, ALU.add)
                        dve.drain()
                        v.tensor_copy(er_carry[:, :], er[:, J - 1, :])
                        dve.wait_ge(s.rows_in[b], (16 * J) * i + 16 * J)
                        v.tensor_tensor(e2[:, :, :], gat[:, b, :, D:D + H], er[:, :, :], ALU.add)
                        dve.drain()
                        v.scalar_tensor_tensor(e[:, :, :], e2[:, :, :], 0.2, e2[:, :, :], ALU.mult, ALU.max)
                        dve.drain()
                        dve.wait_ge(s.buf_free[b], 16 * i + 16)
                        for h in range(H):
                            v.tensor_tensor_scan(acc[:, b, :, h], neg[:, :], e[:, :, h], g.carry[:, h:h + 1], ALU.add, ALU.max)
                        dve.drain()
                        v.tensor_tensor(expo[:, 1], e[:, :, :], acc[:, b, :, 0:H], ALU.subtract)
                        v.tensor_tensor(e2[:, 0:1, :], bcast(neg[:, 0:1], 2, H), g.carry[:, 0:H].unsqueeze(1), ALU.add)
                        v.tensor_tensor(e2[:, 1:J, :], bcast(neg[:, 1:J], 2, H), acc[:, b, 0:J - 1, 0:H], ALU.add)
                        dve.drain()
                        v.tensor_tensor(expo[:, 0], e2[:, :, :], acc[:, b, :, 0:H], ALU.subtract)
                        dve.drain().then_inc(expo_ready, 1)
                        dve.wait_ge(wexp_ready, i * 2 + (b + 1))
                        v.tensor_copy(acc[:, b, :, H:2 * H], wexp[:, 1])
                        for h in range(H):
                            v.tensor_tensor(acc[:, b, :, 2 * H + h * D:2 * H + (h + 1) * D], gat[:, b, :, 0:D],
                                            bcast(wexp[:, 1, :, h], 2, D), ALU.mult)
                        dve.drain().then_inc(gat_free[b], 1)
                        for h in range(H):
                            for c in [H + h] + list(range(2 * H + h * D, 2 * H + (h + 1) * D)):
                                v.tensor_tensor_scan(acc[:, b, :, c], wexp[:, 0, :, h], acc[:, b, :, c],
                                                     g.carry[:, c:c + 1], ALU.mult, ALU.add)
                        dve.drain()
                        v.tensor_copy(g.carry[:, 0:ROW1], acc[:, b, J - 1, :])
                        dve.drain().then_inc(s.scanned[b], 1)


def border_stage_attention(nc, g):
    with ExitStack() as ph:
        sb = lambda n, s_, d=F32: ph.enter_context(nc.sbuf_tensor(f"b1_{n}", s_, d))
        K = H * D
        patch = sb("patch", [P, ROW1])
        wide = sb("wide", [P, 2, P])
        item_m = sb("item_m", [P, P])
        into_m = sb("into_m", [P, P])
        expo = sb("expo", [P, 2, P])
        fac = sb("fac", [P, 2, P])
        neg_link = sb("neg_link", [P, P])
        neg_c0 = sb("neg_c0", [P, P])
        item_v = sb("item_v", [P, P])
        into_v = sb("into_v", [P, P])
        new_m = sb("new_m", [P, H])
        m_all = sb("m_all", [P, 2, P])
        names = ("wide", "turned", "expo", "fac", "into", "back", "expo2", "fac2", "patched")
        wide_ready, turned, expo_ready, fac_ready, into_ready, back, expo2, fac2, patched = (
            g.sem(f"b1_{n}") for n in names)
        fetched, put = g.gather_sem(0), g.gather_sem(1)
        with nc.Block() as block:
            @block.gpsimd
            def _(pool):
                pool.indirect_dma_start(patch[:, :], None, g.rows1[:, :], bass.IndirectOffsetOnAxis(g.border_idx[:, 0:1], 0))\
                    .then_inc(fetched, 16)
                pool.wait_ge(patched, 1)
                pool.indirect_dma_start(g.rows1[:, :], bass.IndirectOffsetOnAxis(g.border_idx[:, 0:1], 0), patch[:, :], None)\
                    .then_inc(put, 16)
                pool.wait_ge(put, 16)

            @block.tensor
            def _(pe):
                for n in range(2):
                    pe.wait_ge(wide_ready, n + 1)
                    for k in range(2):
                        last = nc.tensor.transpose(g.ps[:, k, 0:P], wide[:, k, :], g.ident[:, :])
                    last.then_inc(turned, 1)
                    pe.wait_ge(into_ready, n + 1)
                    nc.tensor.transpose(g.ps[:, 2, 0:P], into_m[:, :], g.ident[:, :])
                    nc.tensor.transpose(g.ps[:, 3, 0:P], into_v[:, :], g.ident[:, :]).then_inc(back, 1)

            @block.scalar
            def _(act):
                for n in range(2):
                    act.wait_ge(expo_ready, n + 1)
                    nc.scalar.activation(fac[:, :, :], expo[:, :, :], ACT.Exp).then_inc(fac_ready, 1)
                    act.wait_ge(expo2, n + 1)
                    nc.scalar.activation(fac[:, :, :], m_all[:, :, :], ACT.Exp).then_inc(fac2, 1)

            @block.vector
            def _(dve):
                v = nc.vector
                v.tensor_scalar(neg_link[:, :], g.link[:, :], BIG, BIG, ALU.mult, ALU.subtract)
                v.tensor_scalar(neg_c0[:, :], g.cont0[:, :], BIG, BIG, ALU.mult, ALU.subtract)
                v.memset(item_m[:, :], -BIG)
                v.memset(item_v[:, :], 0.0)
                v.memset(expo[:, :, :], 0.0)
                dve.drain()
                dve.wait_ge(fetched, 16)
                for n in range(2):
                    v.tensor_copy(wide[:, 0, :].rearrange("p (h f) -> p h f", h=H), bcast(g.carry[:, 0:H], 2, D))
                    if n == 0:
                        v.tensor_copy(wide[:, 1, :], g.carry[:, 2 * H:ROW1])
                    else:
                        v.tensor_copy(wide[:, 1, :].rearrange("p (h f) -> p h f", h=H), bcast(g.carry[:, H:2 * H], 2, D))
                    dve.drain().then_inc(wide_ready, 1)
                    dve.wait_ge(turned, n + 1)
                    v.tensor_tensor(item_m[:, 1:P], g.cont0[:, 1:P], g.ps[:, 0, 0:P - 1], ALU.mult)
                    dve.drain()
                    v.tensor_tensor(item_m[:, 1:P], item_m[:, 1:P], neg_c0[:, 1:P], ALU.add)
                    dve.drain()
                    v.tensor_tensor_scan(into_m[:, :], neg_link[:, :], item_m[:, :], -BIG, ALU.add, ALU.max)
                    dve.drain()
                    v.tensor_tensor(expo[:, 0, 1:P], into_m[:, 0:P - 1], neg_link[:, 1:P], ALU.add)
                    v.tensor_tensor(expo[:, 1, 1:P], item_m[:, 1:P], into_m[:, 1:P], ALU.subtract)
                    dve.drain()
                    v.tensor_tensor(expo[:, 0, 1:P], expo[:, 0, 1:P], into_m[:, 1:P], ALU.subtract)
                    dve.drain().then_inc(expo_ready, 1)
                    dve.wait_ge(fac_ready, n + 1)
                    v.tensor_tensor(fac[:, 0, :], fac[:, 0, :], g.link[:, :], ALU.mult)
                    v.tensor_tensor(item_v[:, 1:P], fac[:, 1, 1:P], g.ps[:, 1, 0:P - 1], ALU.mult)
                    dve.drain()
                    v.tensor_tensor(item_v[:, 1:P], item_v[:, 1:P], g.cont0[:, 1:P], ALU.mult)
                    dve.drain()
                    v.tensor_tensor_scan(into_v[:, :], fac[:, 0, :], item_v[:, :], 0.0, ALU.mult, ALU.add)
                    dve.drain().then_inc(into_ready, 1)
                    dve.wait_ge(back, n + 1)
                    v.tensor_copy(m_all[:, 1, :], g.ps[:, 2, 0:P])
                    v.tensor_copy(m_all[:, 0, :].rearrange("p (h f) -> p h f", h=H), bcast(patch[:, 0:H], 2, D))
                    dve.drain()
                    v.tensor_tensor(item_m[:, :], m_all[:, 0, :], m_all[:, 1, :], ALU.max)
                    dve.drain()
                    v.tensor_tensor(m_all[:, 0, :], m_all[:, 0, :], item_m[:, :], ALU.subtract)
                    v.tensor_tensor(m_all[:, 1, :], m_all[:, 1, :], item_m[:, :], ALU.subtract)
                    if n == 1:
                        v.tensor_copy(new_m[:, :], item_m[:, :].rearrange("p (h f) -> p h f", h=H)[:, :, 0])
                    dve.drain().then_inc(expo2, 1)
                    dve.wait_ge(fac2, n + 1)
                    v.tensor_tensor(fac[:, 1, :], fac[:, 1, :], g.ps[:, 3, 0:P], ALU.mult)
                    if n == 0:
                        v.tensor_tensor(patch[:, 2 * H:ROW1], patch[:, 2 * H:ROW1], fac[:, 0, :], ALU.mult)
                        dve.drain()
                        v.tensor_tensor(patch[:, 2 * H:ROW1], patch[:, 2 * H:ROW1], fac[:, 1, :], ALU.add)
                        v.memset(item_m[:, 0:1], -BIG)
                        dve.drain()
                    else:
                        one = lambda k: fac[:, k, :].rearrange("p (h f) -> p h f", h=H)[:, :, 0]
                        v.tensor_tensor(patch[:, H:2 * H], patch[:, H:2 * H], one(0), ALU.mult)
                        dve.drain()
                        v.tensor_tensor(patch[:, H:2 * H], patch[:, H:2 * H], one(1), ALU.add)
                        v.tensor_copy(patch[:, 0:H], new_m[:, :])
                        dve.drain().then_inc(patched, 1)


def pipelined(loop, step):
    def fixed(n):
        return lambda k: ((n + k) // 2, (n + k) % 2) if 0 <= n + k < GROUPS else None
    pairs = (GROUPS - 4) // 2
    step(fixed(0))
    with loop(0, pairs) as i:
        for o in (1, 2):
            step(lambda k, o=o: (i + (o + k) // 2, (o + k) % 2))
    for n in range(2 * pairs + 1, GROUPS + 1):
        step(fixed(n))


def node_stage_gru(nc, g):
    with ExitStack() as ph:
        name = "n1"
        sb = lambda n, s_, d=F32: ph.enter_context(nc.sbuf_tensor(f"{name}_{n}", s_, d))
        s = NodeSems(g.sem, g.gather_sem, name)
        nidx = sb("nidx", [NP_, 2, G], I32)
        xg = sb("xg", [NP_, 2, G, D])
        xt = sb("xt", [NP_, 2, G, D])
        agg = sb("agg", [NP_, 2, G, ROW1])
        rden = sb("rden", [NP_, 2, G, H])
        alpha = sb("alpha", [NP_, 2, G, H * D])
        aturned = sb("aturned", [P, 2, G, P])
        xturned = sb("xturned", [2 * D + 1, 2, G // 2, P])
        rz = sb("rz", [NP_, 2, G, 2 * D])
        hid = sb("hid", [NP_, 2, G, D])
        low = sb("low", [NP_, 2, G, D])
        r = sb("r", [NP_, 2, G, D])
        t = sb("t", [NP_, 2, G, D])
        stat = sb("stat", [NP_, 2, 5, G])
        new = sb("new", [NP_, 2, G, D])
        scaled = sb("scaled", [NP_, 2, G, D])
        tp = g.ps[:, 4:7, :]
        xp = g.ps[0:2 * D, 7, :]
        xp_last = g.ps[0:2 * D, 3, 0:NP_]
        gates_ps = g.ps[0:NP_, 0:3, :].rearrange("p q c -> p (q c)")
        gflat = gates_ps[:, 0:G * P].rearrange("p (j c) -> p j c", c=P)
        ones_set = g.sem("n1_ones")
        with nc.Block() as block:
            @block.sync
            def _(sp):
                x_v = g.x1.rearrange("(p j) f -> p (j f)", p=NP_)

                def load(buf, arrived, i, b):
                    sp.dma_start(buf[:, b].rearrange("p j f -> p (j f)"), x_v[:, bass.ds(i * (2 * G * D) + b * G * D, G * D)])\
                      .then_inc(arrived[b], 16)
                for b in range(2):
                    load(xt, s.x_product, 0, b)
                    load(xg, s.x_in, 0, b)
                with sp.Fori(0, GROUPS // 2 - 1) as i:
                    for b in range(2):
                        sp.wait_ge(s.x_turned[b], i + 1)
                        load(xt, s.x_product, i + 1, b)
                        sp.wait_ge(s.free[b], i + 1)
                        load(xg, s.x_in, i + 1, b)
                for b in range(2):
                    sp.wait_ge(s.stored[b], 32 * (GROUPS // 2 + 1))

            @block.gpsimd
            def _(pool):
                for b in range(2):
                    pool.sem_inc(s.stored[b], 32)
                pool.sem_inc(s.prods_used[0], 1)
                node_gathers(nc, g, pool, s, nidx, agg, g.rows1)

            @block.tensor
            def _(pe):
                def turn(i, b, before):
                    if before:
                        pe.wait_ge(s.x_turned_sb[before[1]], before[0] + 1)
                        pe.wait_ge(s.turned_sb[before[1]], before[0] + 1)
                    pe.wait_ge(s.x_product[b], 16 * i + 16)
                    pe.nop(nofuse=True)
                    for q in range(G // 2):
                        last = nc.tensor.transpose(xp[:, q * P:q * P + NP_] if q < 4 else xp_last,
                                                   xt[:, b, 2 * q:2 * q + 2, :].rearrange("p j f -> p (j f)"),
                                                   g.ident[0:NP_, 0:NP_])
                    last.then_inc(s.x_turned[b], 1)
                    pe.wait_ge(s.agg_ready[b], i + 1)
                    for c in range(G):
                        last = nc.tensor.transpose(tp[:, c // 4, (c % 4) * P:(c % 4) * P + NP_], alpha[:, b, c, :],
                                                   g.ident[0:NP_, 0:NP_])
                    last.then_inc(s.turned[b], 1)

                def gates(i, b):
                    pe.wait_ge(s.x_turned_sb[b], i + 1)
                    pe.wait_ge(s.turned_sb[b], i + 1)
                    pe.wait_ge(s.prods_used[0], i * 2 + (b + 1))
                    for q in range(G // 2):
                        nc.tensor.matmul(gates_ps[:, q * 2 * P:(q + 1) * 2 * P], xturned[:, b, q, 0:NP_],
                                         g.bdhh[:, :, :].rearrange("p k c -> p (k c)"), start=(q % 2 == 0), stop=True,
                                         skip_group_check=True)
                    for c in range(G):
                        last = nc.tensor.matmul(gates_ps[:, c * P:(c + 1) * P], aturned[:, b, c, 0:NP_],
                                                g.wc[:, :], start=False, stop=True, skip_group_check=True)
                    last.then_inc(s.product[b], 1)

                def step(at):
                    if at(2):
                        turn(*at(2), at(1))
                    if at(1):
                        gates(*at(1))

                pe.wait_ge(ones_set, 1)
                turn(0, 0, None)
                turn(0, 1, (0, 0))
                gates(0, 0)
                pipelined(pe.Fori, step)

            @block.scalar
            def _(act):
                a = nc.scalar

                def copy(i, b):
                    act.wait_ge(s.x_turned[b], i + 1)
                    a.activation(xturned[0:2 * D, b, 0:4, 0:NP_], xp.rearrange("p (q n) -> p q n", q=4)[:, :, 0:NP_], ACT.Copy)
                    a.activation(xturned[0:2 * D, b, 4, 0:NP_], xp_last, ACT.Copy).then_inc(s.x_turned_sb[b], 1)
                    act.wait_ge(s.turned[b], i + 1)
                    for q, (c, k) in enumerate(QUADS):
                        last = a.activation(aturned[:, b, c:c + k, 0:NP_],
                                            tp[:, q, 0:k * P].rearrange("p (k n) -> p k n", k=k)[:, :, 0:NP_], ACT.Copy)
                    last.then_inc(s.turned_sb[b], 1)

                def nonlinear(i, b):
                    act.wait_ge(s.product[b], i + 1)
                    a.activation(rz[:, b], gflat[:, :, 0:2 * D], ACT.Tanh, scale=0.5).then_inc(s.gates_act[b], 1)
                    act.wait_ge(s.hidden[b], i + 1)
                    a.activation(hid[:, b], hid[:, b], ACT.Tanh).then_inc(s.hidden_act[b], 1)
                    act.wait_ge(s.low[b], i + 1)
                    a.activation(low[:, b], low[:, b], ACT.Exp).then_inc(s.low_act[b], 1)

                def root(i, b):
                    layernorm_sqrt(nc, act, s, i, b, stat)

                def store(i, b):
                    node_stores(nc, g, act, s, i, b, None, [(new, g.x2), (scaled, g.table2)])

                def step(at):
                    if at(-1):
                        root(*at(-1))
                    if at(0):
                        nonlinear(*at(0))
                    if at(-1):
                        store(*at(-1))
                    if at(2):
                        copy(*at(2))

                copy(0, 0)
                copy(0, 1)
                pipelined(act.Fori, step)

            @block.vector
            def _(dve):
                v = nc.vector

                def means(i, b):
                    dve.wait_ge(s.gathered[b], 16 * G * i + 16 * G)
                    v.tensor_scalar(rden[:, b], agg[:, b, :, H:2 * H], 1e-30, None, ALU.max)
                    dve.drain()
                    v.reciprocal(rden[:, b], rden[:, b])
                    dve.drain()
                    if not isinstance(i, int) or i > 0:
                        dve.wait_ge(s.turned[b], i)
                    for h in range(H):
                        v.tensor_tensor(alpha[:, b, :, h * D:(h + 1) * D], agg[:, b, :, 2 * H + h * D:2 * H + (h + 1) * D],
                                        bcast(rden[:, b, :, h], 2, D), ALU.mult)
                    dve.drain().then_inc(s.agg_ready[b], 1)
                    next_index(nc, g, dve, s, nidx, i + 1, b)

                def cell(i, b):
                    dve.wait_ge(s.gates_act[b], i + 1)
                    v.tensor_scalar(rz[:, b], rz[:, b], 0.5, 0.5, ALU.mult, ALU.add)
                    dve.drain()
                    v.tensor_tensor(t[:, b], rz[:, b, :, 0:D], gflat[:, :, 3 * D:4 * D], ALU.mult)
                    dve.drain()
                    v.tensor_tensor(hid[:, b], t[:, b], gflat[:, :, 2 * D:3 * D], ALU.add).then_inc(s.hidden[b], 1)
                    dve.drain().then_inc(s.prods_used[0], 1)
                    dve.wait_ge(s.hidden_act[b], i + 1)
                    dve.wait_ge(s.x_in[b], 16 * i + 16)
                    v.tensor_tensor(t[:, b], xg[:, b], hid[:, b], ALU.subtract)
                    dve.drain()
                    v.tensor_tensor(t[:, b], t[:, b], rz[:, b, :, D:2 * D], ALU.mult)
                    dve.drain()
                    v.tensor_tensor(r[:, b], t[:, b], hid[:, b], ALU.add)
                    dve.drain()
                    v.tensor_scalar(low[:, b], r[:, b], 0.0, None, ALU.min).then_inc(s.low[b], 1)
                    v.tensor_scalar(r[:, b], r[:, b], 0.0, -1.0, ALU.max, ALU.add)
                    dve.drain()
                    v.tensor_tensor(r[:, b], r[:, b], xg[:, b], ALU.add)
                    dve.drain().then_inc(s.free[b], 1)
                    dve.wait_ge(s.low_act[b], i + 1)
                    v.tensor_tensor(r[:, b], r[:, b], low[:, b], ALU.add)
                    dve.drain()
                    layernorm_moments(nc, dve, s, b, r[:, b], t[:, b], stat)

                def finish(i, b):
                    cols = group_cols(i, b)
                    dve.wait_ge(s.stored[b], 32 * i + 32)
                    layernorm_scale(nc, dve, s, i, b, r[:, b], stat, new[:, b])
                    dve.drain()
                    v.tensor_tensor(scaled[:, b], new[:, b], bcast(g.norm[:, 0, cols], 2, D), ALU.mult)
                    dve.drain().then_inc(s.new_ready[b], 1)

                v.memset(xturned[2 * D:2 * D + 1, :, :, :], 1.0)
                for b in range(2):
                    next_index(nc, g, dve, s, nidx, 0, b)
                dve.drain().then_inc(ones_set, 1)

                def step(at):
                    if at(2):
                        means(*at(2))
                    if at(-1):
                        finish(*at(-1))
                    if at(0):
                        cell(*at(0))

                means(0, 0)
                means(0, 1)
                pipelined(dve.Fori, step)


def edge_stage_tensor_product(nc, g):
    with ExitStack() as ph:
        sb = lambda n, s_, d=F32: ph.enter_context(nc.sbuf_tensor(f"e3_{n}", s_, d))
        s = EdgeSems(g.sem, g.gather_sem, "e3")
        STEPS = J // SC
        W = SC * P
        gat = sb("gat", [P, 2, J, D])
        sh = sb("sh", [P, 2, J, 4])
        h2 = sb("h2", [HR + 1, 2, J * P])
        vs = sb("vs", [P, J, MUL, 3])
        fac = sb("fac", [P, 2, J, 3, MUL])
        cv = sb("cv", [P, 2, J, 3, MUL])
        prod = sb("prod", [P, 2, SC, 6, MUL, MUL])
        half = sb("half", [P, J * 6 * MUL, 4])
        quarter = sb("quarter", [P, J * 6 * MUL, 2])
        red = sb("red", [P, J, 6, MUL])
        msg = sb("msg", [P, 2, D, J])
        out = sb("out", [P, 2, J, D])
        contw = sb("contw", [P, 2, D, J])
        cont_first = sb("cont_first", [P, 2, 1])
        tp_made, tp_used = ([g.sem(f"e3_{n}{k}") for k in range(2)] for n in ("tp", "tp_used"))
        sh_in, h2_in, h2_free, gat_free, factored, used = (
            [g.sem(f"e3_{n}{b}") for b in range(2)] for n in ("sh_in", "h2_in", "h2_free", "gat_free", "factored", "used"))
        ones_set = g.sem("e3_ones")
        turned = [g.sem(f"e3_turned{b}") for b in range(2)]
        with nc.Block() as block:
            @block.gpsimd
            def _(pool):
                for b in range(2):
                    pool.sem_inc(gat_free[b], 1)
                    pool.sem_inc(used[b], 1)
                    pool.sem_inc(turned[b], 1)
                    pool.sem_inc(s.buf_free[b], 16)
                with pool.Fori(0, PAIRS) as i:
                    for b in range(2):
                        pool.wait_ge(s.idx_in[b], 16 * i + 16)
                        pool.wait_ge(gat_free[b], i + 1)
                        pool.nop(nofuse=True)
                        for j in range(J):
                            pool.indirect_dma_start(gat[:, b, j, :], None, g.x3[:, :],
                                                    bass.IndirectOffsetOnAxis(g.idx[:, b, j:j + 1], 0)).then_inc(s.rows_in[b], 16)

            @block.sync
            def _(sp):
                sh_v = g.edge_sh.rearrange("(p c) h -> p (c h)", p=P)
                chunk = lambda i, b, width: bass.ds(i * (2 * J * width) + b * J * width, J * width)
                for b in range(2):
                    sp.dma_start(g.idx[:, b, :], g.src_cols[:, b * J:(b + 1) * J]).then_inc(s.idx_in[b], 16)
                    sp.dma_start(h2[0:HR, b, :], g.hidden[:, b * J * P:(b + 1) * J * P]).then_inc(h2_in[b], 16)
                    sp.dma_start(sh[:, b].rearrange("p j h -> p (j h)"), sh_v[:, b * J * 4:(b + 1) * J * 4]).then_inc(sh_in[b], 16)
                with sp.Fori(0, PAIRS - 1) as i:
                    for b in range(2):
                        sp.wait_ge(s.rows_in[b], (16 * J) * i + 16 * J)
                        sp.dma_start(g.idx[:, b, :], g.src_cols[:, chunk(i, b + 2, 1)]).then_inc(s.idx_in[b], 16)
                        sp.wait_ge(h2_free[b], i + 1)
                        sp.dma_start(h2[0:HR, b, :], g.hidden[:, chunk(i, b + 2, P)]).then_inc(h2_in[b], 16)
                        sp.wait_ge(used[b], i + 2)
                        sp.dma_start(sh[:, b].rearrange("p j h -> p (j h)"), sh_v[:, chunk(i, b + 2, 4)]).then_inc(sh_in[b], 16)
                for b in range(2):
                    sp.wait_ge(s.buf_free[b], 16 * PAIRS + 16)

            @block.tensor
            def _(pe):
                pe.wait_ge(ones_set, 1)
                for k in range(2):
                    pe.sem_inc(tp_used[k], 1)
                with pe.Fori(0, PAIRS) as i:
                    for b in range(2):
                        pe.wait_ge(h2_in[b], 16 * i + 16)
                        for m in range(STEPS):
                            n = b * STEPS + m
                            k = n % 2
                            pe.wait_ge(tp_used[k], i * STEPS + n // 2 + 1)
                            for c in range(SC):
                                at = (m * SC + c) * P
                                last = nc.tensor.matmul(g.ps[:, 4 * k + c // 2, (c % 2) * NTP:(c % 2 + 1) * NTP],
                                                        h2[:, b, at:at + P], g.w3p[:, :], start=True, stop=True)
                            last.then_inc(tp_made[k], 1)
                        pe.drain().then_inc(h2_free[b], 1)

            @block.scalar
            def _(act):
                rows_v = g.rows3[0:EROWS, :].rearrange("(p c) f -> p (c f)", p=P)

                def factors(i, b):
                    act.wait_ge(s.rows_in[b], (16 * J) * i + 16 * J)
                    act.wait_ge(sh_in[b], 16 * i + 16)
                    act.wait_ge(used[b], i + 1)
                    cols = i * (2 * J) + b * J
                    nc.scalar.activation(contw[:, b, :, 1:J], bcast(g.cont[:, bass.ds(cols + 1, J - 1)], 1, D), ACT.Copy)
                    nc.scalar.activation(cont_first[:, b, :], g.cont[:, bass.ds(cols, 1)], ACT.Copy)
                    nc.scalar.activation(fac[:, b, :, 2, :], gat[:, b, :, 0:MUL], ACT.Copy)
                    for j in range(J):
                        nc.scalar.mul(fac[:, b, j, 0, :], gat[:, b, j, 0:MUL], sh[:, b, j, 0:1])
                        last = nc.scalar.mul(cv[:, b, j], gat[:, b, j, MUL:D].rearrange("p (u i) -> p i u", i=3),
                                             sh[:, b, j, 0:1])
                    last.then_inc(factored[b], 1)

                def store(i, b):
                    act.wait_ge(s.scanned[b], i + 1)
                    act.wait_ge(s.buf_free[b], 16 * i + 16)
                    nc.scalar.activation(out[:, b], msg[:, b].rearrange("p f j -> p j f"), ACT.Copy).then_inc(turned[b], 1)
                    act.wait_ge(turned[b], i + 2)
                    act.dma_start(rows_v[:, chunk_cols(i, b, D)], out[:, b].rearrange("p j f -> p (j f)"))\
                       .then_inc(s.buf_free[b], 16)

                factors(0, 0)
                with act.Fori(0, PAIRS - 1) as i:
                    factors(i, 1)
                    store(i, 0)
                    factors(i + 1, 0)
                    store(i, 1)
                factors(PAIRS - 1, 1)
                store(PAIRS - 1, 0)
                store(PAIRS - 1, 1)

            @block.vector
            def _(dve):
                v = nc.vector
                v.memset(h2[HR:HR + 1, :, :], 1.0)
                v.memset(g.carry[:, :], 0.0)
                v.memset(contw[:, :, :, 0:1], 0.0)
                dve.drain().then_inc(ones_set, 1)
                with dve.Fori(0, PAIRS) as i:
                    for b in range(2):
                        dve.wait_ge(sh_in[b], 16 * i + 16)
                        dve.wait_ge(s.rows_in[b], (16 * J) * i + 16 * J)
                        hv = gat[:, b, :, MUL:D].rearrange("p j (u i) -> p j u i", i=3)
                        sh1 = sh[:, b, :, 1:4]
                        v.tensor_tensor(vs[:, :, :, :], hv, bcast(sh1, 2, MUL), ALU.mult)
                        dve.wait_ge(factored[b], i + 1)
                        dve.nop(nofuse=True)
                        dve.drain().then_inc(gat_free[b], 1)
                        v.tensor_reduce(fac[:, b, :, 1, :], vs[:, :, :, :], AX.X, ALU.add)
                        dve.drain()
                        for m in range(STEPS):
                            n = b * STEPS + m
                            k = n % 2
                            c0, c1 = m * SC, (m + 1) * SC
                            dve.wait_ge(tp_made[k], i * STEPS + n // 2 + 1)
                            tp = g.ps[:, 4 * k:4 * k + 4, :].rearrange("p a (c x) -> p (a c) x", x=NTP)
                            v.tensor_tensor(prod[:, k, :, 0:3], tp[:, :, 0:192].rearrange("p c (f w u) -> p c f w u", f=3, w=MUL),
                                            bcast(fac[:, b, c0:c1], 3, MUL), ALU.mult)
                            v.tensor_tensor(prod[:, k, :, 3:6], bcast(tp[:, :, 192:256].rearrange("p c (w u) -> p c w u", w=MUL), 2, 3),
                                            bcast(cv[:, b, c0:c1], 3, MUL), ALU.mult)
                            dve.drain().then_inc(tp_used[k], 1)
                            by_u = prod[:, k].rearrange("p c f w u -> p (c f w) u")
                            v.tensor_tensor(half[:, c0 * 6 * MUL:c1 * 6 * MUL, :], by_u[:, :, 0:4], by_u[:, :, 4:8], ALU.add)
                        dve.drain()
                        v.tensor_tensor(quarter[:, :, :], half[:, :, 0:2], half[:, :, 2:4], ALU.add)
                        dve.drain()
                        v.tensor_tensor(red[:, :, :, :].rearrange("p c f w -> p (c f w)"), quarter[:, :, 0], quarter[:, :, 1],
                                        ALU.add)
                        dve.drain()
                        dve.wait_ge(turned[b], i + 1)
                        by_j = msg[:, b].rearrange("p f j -> p j f")
                        v.tensor_tensor(by_j[:, :, 0:MUL], red[:, :, 0, :], red[:, :, 1, :], ALU.add)
                        v.tensor_tensor(vs[:, :, :, :], bcast(red[:, :, 2, :], 3, 3), bcast(sh1, 2, MUL), ALU.mult)
                        dve.drain()
                        v.tensor_tensor(by_j[:, :, MUL:D].rearrange("p j (w i) -> p j w i", i=3), vs[:, :, :, :],
                                        red[:, :, 3:6, :].rearrange("p j i w -> p j w i"), ALU.add)
                        dve.drain()
                        v.scalar_tensor_tensor(msg[:, b, :, 0], g.carry[:, 0:D], cont_first[:, b, 0:1], msg[:, b, :, 0],
                                               ALU.mult, ALU.add)
                        dve.drain()
                        flat = msg[:, b].rearrange("p f j -> p (f j)")
                        v.tensor_tensor_scan(flat, contw[:, b].rearrange("p f j -> p (f j)"), flat, 0.0, ALU.mult, ALU.add)
                        dve.drain().then_inc(used[b], 1)
                        v.tensor_copy(g.carry[:, 0:D], msg[:, b, :, J - 1])
                        dve.drain().then_inc(s.scanned[b], 1)


def program(nc, x, src_cols, dst_flat, edge_sh, edge_rad, w, out):
    with ExitStack() as ctx:
        g = Graph()
        g.sem_for_good, g.gather_count = (lambda n: ctx.enter_context(nc.semaphore(n))), count()
        sb = lambda n, s, d=F32: ctx.enter_context(nc.sbuf_tensor(n, s, d))
        dram = lambda n, s, d=F32: nc.dram_tensor(n, s, d, kind="Internal").ap()
        g.src_cols, g.dst_flat, g.edge_sh, g.edge_rad = src_cols, dst_flat, edge_sh, edge_rad
        g.rows0 = dram("rows0", (EROWS + 1, D))
        g.rows1 = dram("rows1", (EROWS + 1, ROW1))
        g.rows2 = dram("rows2", (EROWS + 1, D))
        g.rows3 = dram("rows3", (EROWS + 1, D))
        g.er_edges = dram("er_edges", (EROWS + N, H))
        g.table1 = dram("table1", (N, T1W))
        g.table2 = dram("table2", (N, D))
        g.x1, g.x2, g.x3 = (dram(f"x{k}", (N, D)) for k in (1, 2, 3))
        g.hidden = dram("hidden", (HR, EROWS))

        g.ps = ctx.enter_context(nc.psum_tensor("ps", [P, 8, 512], F32))
        g.idx = sb("idx", [P, 2, J], I32)
        g.cont = sb("cont", [P, EC])
        g.carry = sb("carry", [P, ROW1])
        g.ident = sb("ident", [P, P])
        g.ltri = sb("ltri", [P, P])
        g.iota_i = sb("iota_i", [P, P], I32)
        g.node_i = sb("node_i", [P, NC_], I32)
        g.first_edge_i = sb("first_edge_i", [P, 1], I32)
        g.dst0_f, g.dst0_i = sb("dst0_f", [P, 1]), sb("dst0_i", [P, 1], I32)
        g.row_dst0 = sb("row_dst0", [P, T1W])
        g.border_idx = sb("border_idx", [P, 1], I32)
        g.cont0, g.linked, g.link = sb("cont0", [P, P]), sb("linked", [P, P]), sb("link", [P, P])
        g.deg, g.norm = sb("deg", [NP_, 2, NC_]), sb("norm", [NP_, 2, NC_])
        g.last_i, g.first_i = sb("last_i", [NP_, NC_ + 2 * G], I32), sb("first_i", [NP_, NC_], I32)
        g.er_nodes = sb("er_nodes", [NP_, NC_, H])
        g.bd0, g.bd2, g.bdself = sb("bd0", [P, P]), sb("bd2", [P, P]), sb("bdself", [P, P])
        g.bdel = sb("bdel", [P, 8 * H])
        g.bdhh = sb("bdhh", [2 * D + 1, 2, P])
        g.wc = sb("wc", [P, P])
        g.w1, g.w2, g.w3p = sb("w1", [8, HR]), sb("w2", [HR, HR]), sb("w3p", [HR + 1, NTP])
        g.b1, g.b2, g.b2row = sb("b1", [HR, 1]), sb("b2", [HR, 1]), sb("b2row", [NP_, D])

        with stage(nc, g):
            load_weights(nc, g, w)
        with stage(nc, g):
            edge_stage_plain(nc, g, "e0", x[:, :], g.rows0, first=True)
        with stage(nc, g):
            index_stage(nc, g)
        with stage(nc, g):
            border_stage_plain(nc, g, "b0", g.rows0)
        with stage(nc, g):
            node_stage_plain(nc, g, "n0", 0, g.rows0, x, [("x", g.x1), ("t1", g.table1)])
        with stage(nc, g):
            spread_er_stage(nc, g)
        with stage(nc, g):
            edge_stage_attention(nc, g)
        with stage(nc, g):
            border_stage_attention(nc, g)
        with stage(nc, g):
            node_stage_gru(nc, g)
        with stage(nc, g):
            edge_stage_plain(nc, g, "e2", g.table2[:, :], g.rows2, first=False)
        with stage(nc, g):
            border_stage_plain(nc, g, "b2", g.rows2)
        with stage(nc, g):
            node_stage_plain(nc, g, "n2", 2, g.rows2, g.x2, [("x", g.x3)])
        with stage(nc, g):
            edge_stage_tensor_product(nc, g)
        with stage(nc, g):
            border_stage_plain(nc, g, "b3", g.rows3)
        with stage(nc, g):
            node_stage_plain(nc, g, "n3", 3, g.rows3, g.x3, [("x", out)])


def kernel(x, src, dst, edge_attr_4, edge_attr_8, L0_gnn_W, L1_gnn_W_gat, L1_gnn_attn_l, L1_gnn_attn_r, L1_gnn_W_ih,
           L1_gnn_W_hh, L1_gnn_b_ih, L1_gnn_b_hh, L2_gnn_W, L2_gnn_b, L3_gnn_W1, L3_gnn_b1, L3_gnn_W2, L3_gnn_b2,
           L3_gnn_W3, L3_gnn_b3, L3_gnn_Ws, L3_gnn_Wv):
    import concourse.bacc as bacc
    from concourse.bass_utils import run_bass_kernel_spmd

    a = np.ascontiguousarray
    pad = EROWS - E
    src_cols = np.pad(np.pad(np.asarray(src), (0, pad)).reshape(P, EC), ((0, 0), (0, 2 * J)))
    dst_flat = np.concatenate([np.full(1, -1, np.int32), np.asarray(dst), np.full(pad, N, np.int32)]).reshape(1, -1)
    rad = np.pad(np.asarray(edge_attr_8), ((0, pad), (0, 0))).reshape(P, EC, 8).transpose(2, 1, 0)
    rad = np.pad(rad, ((0, 0), (0, 2 * J), (0, 0))).reshape(8, -1)
    data = {
        "x": np.asarray(x),
        "src_cols": src_cols,
        "dst_flat": dst_flat,
        "edge_sh": np.pad(np.asarray(edge_attr_4), ((0, pad), (0, 0))),
        "edge_rad": rad,
    }
    attn = np.zeros((H * D, 2 * H), np.float32)
    for h in range(H):
        attn[h * D:(h + 1) * D, h] = np.asarray(L1_gnn_attn_l)[h]
        attn[h * D:(h + 1) * D, H + h] = np.asarray(L1_gnn_attn_r)[h]
    self_w = np.zeros((D, D), np.float32)
    self_w[:MUL, :MUL] = np.asarray(L3_gnn_Ws)
    for i in range(3):
        self_w[MUL + i::3, MUL + i::3] = np.asarray(L3_gnn_Wv)
    weights = {
        "W0": np.asarray(L0_gnn_W), "gatT": np.asarray(L1_gnn_W_gat).T, "attn": attn,
        "wihT": np.asarray(L1_gnn_W_ih).T, "whhT": np.asarray(L1_gnn_W_hh).T,
        "b_ih": np.asarray(L1_gnn_b_ih).reshape(1, -1), "b_hh": np.asarray(L1_gnn_b_hh).reshape(1, -1),
        "W2g": np.asarray(L2_gnn_W), "b2g": np.tile(np.asarray(L2_gnn_b).reshape(1, -1), (NP_, 1)),
        "W1": np.asarray(L3_gnn_W1), "b1": np.asarray(L3_gnn_b1).reshape(-1, 1),
        "W2": np.asarray(L3_gnn_W2), "b2": np.asarray(L3_gnn_b2).reshape(-1, 1),
        "W3": np.asarray(L3_gnn_W3), "b3": np.asarray(L3_gnn_b3).reshape(1, -1),
        "self": self_w,
    }
    nc = bacc.Bacc("TRN2", target_bir_lowering=False, num_devices=1)
    arrays = {f"in_{n}": a(v) for n, v in {**data, **weights}.items()}
    aps = {n: nc.dram_tensor(n, v.shape, mybir.dt.from_np(v.dtype), kind="ExternalInput").ap() for n, v in arrays.items()}
    out = nc.dram_tensor("out", (N, D), F32, kind="ExternalOutput").ap()
    program(nc, *(aps[f"in_{n}"] for n in data), {n: aps[f"in_{n}"] for n in weights}, out)
    r = run_bass_kernel_spmd(nc, [arrays], core_ids=[0])
    return r.results[0]["out"]
```

```python
import concourse.bass as bass
from concourse import mybir
from contextlib import ExitStack, contextmanager
from itertools import count
import numpy as np

F32 = mybir.dt.float32
BF16 = mybir.dt.bfloat16
I32 = mybir.dt.int32
ALU = mybir.AluOpType
ACT = mybir.ActivationFunctionType
AX = mybir.AxisListType

P = 128
N = 12500
E = 212500
D = 32
H = 4
J = 32
EC = 1664
CHUNKS = EC // J
PAIRS = CHUNKS // 2
EROWS = P * EC
NP_ = 125
NC_ = 100
G = 10
GROUPS = NC_ // G
QUADS = [(0, 4), (4, 4), (8, 2)]
OH = 8
ROW1 = 2 * H + H * D
T1W = D + 2 * H
BIG = 1e30
EPS = 1e-5
ROUND = 12582912.0
HR = 64
NTP = 256
MUL = 8
ALPHA = 1.0 / np.sqrt(2.0 * MUL)
INV_SQRT3 = 1.0 / np.sqrt(3.0)
NBRS = float(np.sqrt(16.0))
SC = 8
RC = 4
RW = RC * P
RSTEPS = J // RC

assert EC % (2 * J) == 0 and P * EC >= E and NP_ * NC_ == N and NC_ % (2 * G) == 0


class Graph:
    pass


@contextmanager
def stage(nc, g):
    held = ExitStack()
    used = []

    def sem(name):
        used.append(held.enter_context(nc.semaphore(name)))
        return used[-1]

    def gather_sem(k):
        return g.sem_for_good(f"gathered{next(g.gather_count)}_{k}")
    g.sem, g.gather_sem = sem, gather_sem
    yield
    g.past_held.close()
    g.past_held, g.past_sems = held, used


def clear_past(g, pool):
    for one in g.past_sems:
        pool.sem_clear(one)


def bcast(ap, axis, count):
    ap = ap.unsqueeze(axis)
    return ap.broadcast_to([count if k == axis else n for k, n in enumerate(ap.shape)])



class WeightLoad:

    def __init__(self, nc, g, w, ph):
        sb = lambda n, s, d=F32: ph.enter_context(nc.sbuf_tensor(n, s, d))
        self.nc, self.g, self.w = nc, g, w
        self.cleared, self.loaded, self.ids, self.product = g.sem("w_cleared"), g.sem("w_loaded"), g.sem("w_ids"), g.sem("w_mm")
        self.gatT_bd = sb("gatT_bd", [P, P])
        self.gatT_rep = sb("gatT_rep", [P, P])
        self.attn = sb("attn", [P, 2 * H])
        self.ihT = sb("ihT", [P, 96])
        self.whh = sb("whh_rows", [P, 96])
        self.w3raw = sb("w3raw", [HR + 1, NTP])
        self.bih = sb("bih", [2 * D + 1, 96])
        self.bhh = sb("bhh", [2 * D + 1, 96])
        self.ps_gates, self.ps_attn = g.ps[:, 2, :], g.ps[:, 3, :]

        w3 = ((self.w3raw[0:HR, :], w["W3"][:, :]), (self.w3raw[HR:HR + 1, :], w["b3"]))
        self.pieces = [(self.attn[:, :], w["attn"][:, :]), (self.ihT[:, :], w["wihT"][:, :]),
                       (self.bih[2 * D:2 * D + 1, :], w["b_ih"]), (self.bhh[2 * D:2 * D + 1, :], w["b_hh"]),
                       (g.w1[:, :], w["W1"][:, :]), (g.w2[:, :], w["W2"][:, :]), (g.b1[:, :], w["b1"]), (g.b2[:, :], w["b2"]),
                       (g.b2row[:, :], w["b2g"]), *w3]
        for c in range(4):
            r = slice(D * c, D * c + D)
            self.pieces += [(g.bd0[r, r], w["W0"][:, :]), (g.bd2[r, r], w["W2g"][:, :]), (g.bdself[r, r], w["self"][:, :]),
                            (self.gatT_bd[r, r], w["gatT"][r, :]), (self.gatT_rep[:, r], w["gatT"][:, :]),
                            (self.whh[r, :], w["whhT"][:, :])]

    def load(self, sp):
        sp.wait_ge(self.cleared, 1)
        for dst, src in self.pieces:
            sp.dma_start(dst, src).then_inc(self.loaded, 16)

    def clear(self, dve):
        g = self.g
        for t in (self.gatT_bd, g.bd0, g.bd2, g.bdself, g.bdel, g.wc):
            self.nc.vector.memset(t[:, :], 0.0)
        self.nc.vector.memset(g.bdhh[:, :, :], 0.0)
        dve.drain().then_inc(self.cleared, 1)

    def form(self, dve):
        v, g, whh, bih, bhh = self.nc.vector, self.g, self.whh, self.bih, self.bhh
        dve.wait_ge(self.loaded, 16 * len(self.pieces))
        for c in range(2):
            r = slice(D * c, D * c + D)
            v.tensor_copy(g.bdhh[r, c, 0:64], whh[r, 0:64])
            v.tensor_copy(g.bdhh[r, c, 96:128], whh[r, 64:96])
            bias = g.bdhh[2 * D:2 * D + 1, c, :]
            v.tensor_tensor(bias[:, 0:64], bih[64:65, 0:64], bhh[64:65, 0:64], ALU.add)
            v.tensor_copy(bias[:, 64:96], bih[64:65, 64:96])
            v.tensor_copy(bias[:, 96:128], bhh[64:65, 64:96])
        v.tensor_scalar(g.bdself[:, :], g.bdself[:, :], float(1.0 / np.sqrt(MUL)), None, ALU.mult)
        k = float(ALPHA / NBRS)
        src = self.w3raw[:, :].rearrange("r (b u w) -> r b w u", b=4, u=MUL)
        dst = g.w3p[:, :].rearrange("r (b w u) -> r b w u", b=4, u=MUL)
        for block_, factor in enumerate((k, k * INV_SQRT3, k, k)):
            v.tensor_scalar(dst[:, block_], src[:, block_], float(factor), None, ALU.mult)
        dve.wait_ge(self.product, 2)
        v.tensor_copy(g.wc[:, 0:96], self.ps_gates[:, 0:96])
        for c in range(4):
            r = slice(D * c, D * c + D)
            v.tensor_copy(g.bdel[r, 8 * c:8 * c + 8], self.ps_attn[r, 0:8])

    def constants(self, pool):
        gp, g = self.nc.gpsimd, self.g
        gp.memset(g.ident[:, :], 0.0)
        gp.memset(g.ltri[:, :], 1.0)
        gp.iota(g.iota_i[:, :], pattern=[[1, P]], base=0, channel_multiplier=0)
        gp.iota(g.node_i[:, :], pattern=[[1, NC_]], base=0, channel_multiplier=NC_)
        gp.iota(g.first_edge_i[:, :], pattern=[[1, 1]], base=0, channel_multiplier=EC)
        pool.drain()
        gp.affine_select(out=g.ident[:, :], in_=g.ident[:, :], compare_op=ALU.not_equal, fill=1.0,
                         base=0, pattern=[[-1, P]], channel_multiplier=1)
        gp.affine_select(out=g.ltri[:, :], in_=g.ltri[:, :], compare_op=ALU.is_gt, fill=0.0,
                         base=0, pattern=[[1, P]], channel_multiplier=-1)
        pool.drain().then_inc(self.ids, 1)

    def products(self, pe):
        pe.wait_ge(self.loaded, 16 * len(self.pieces))
        self.nc.tensor.matmul(self.ps_gates[:, 0:96], self.gatT_bd[:, :], self.ihT[:, :], start=True, stop=True)\
            .then_inc(self.product, 1)
        self.nc.tensor.matmul(self.ps_attn[:, 0:8], self.gatT_rep[:, :], self.attn[:, :], start=True, stop=True)\
            .then_inc(self.product, 1)



def gather_chunks(nc, g, pool, table, buf, s):
    for b in range(2):
        pool.sem_inc(s.buf_free[b], 16)
    with pool.Fori(0, PAIRS) as i:
        for b in range(2):
            pool.wait_ge(s.idx_in[b], 16 * i + 16)
            pool.wait_ge(s.buf_free[b], 16 * i + 16)
            pool.nop(nofuse=True)
            for j in range(J):
                pool.indirect_dma_start(buf[:, b, j, :], None, table,
                                        bass.IndirectOffsetOnAxis(g.idx[:, b, j:j + 1], 0)).then_inc(s.rows_in[b], 16)


def chunk_cols(i, b, width=1):
    return bass.ds(i * (2 * J * width) + b * J * width, J * width)


class EdgeSems:

    def __init__(self, sem, gather_sem, name):
        self.idx_in = [sem(f"{name}_idx_in{b}") for b in range(2)]
        self.rows_in = [gather_sem(b) for b in range(2)]
        self.buf_free = [sem(f"{name}_buf_free{b}") for b in range(2)]
        self.scanned = [sem(f"{name}_scanned{b}") for b in range(2)]


def scan_rows(nc, g, dve, i, b, buf, carry, width):
    cont = g.cont[:, chunk_cols(i, b)]
    for f in range(width):
        nc.vector.tensor_tensor_scan(buf[:, b, :, f], cont, buf[:, b, :, f], carry[:, f:f + 1], ALU.mult, ALU.add)
    dve.drain()
    nc.vector.tensor_copy(carry[:, 0:width], buf[:, b, J - 1, :])


def radial_tensor(nc, g, pe, rad, h1, r):
    def second_layer(i, n):
        k = n % 2
        pe.wait_ge(r.h1_out[k], i * RSTEPS + n // 2 + 1)
        pe.nop(nofuse=True)
        nc.tensor.matmul(g.ps[0:HR, 4 + k, :], g.w2[:, :], h1[:, k, :], start=True, stop=True).then_inc(r.h2_in[k], 1)

    with pe.Fori(0, PAIRS) as i:
        for b in range(2):
            pe.wait_ge(r.rad_in[b], 16 * i + 16)
            for m in range(RSTEPS):
                n = b * RSTEPS + m
                k = n % 2
                nc.tensor.matmul(g.ps[0:HR, 2 + k, :], g.w1[:, :], rad[:, b, m * RW:(m + 1) * RW], start=True, stop=True)\
                    .then_inc(r.h1_in[k], 1)
                if m == RSTEPS - 1:
                    pe.drain().then_inc(r.rad_free[b], 1)
                if n > 0:
                    second_layer(i, n - 1)
        second_layer(i, 2 * RSTEPS - 1)


def radial_scalar(nc, g, act, rad, h1, h2, r):
    def second_layer(i, n):
        k, b, m = n % 2, n // RSTEPS, n % RSTEPS
        if m == 0:
            act.wait_ge(r.h2_free[b], 16 * i + 16)
        act.wait_ge(r.h2_in[k], i * RSTEPS + n // 2 + 1)
        nc.scalar.activation(h2[:, b, m * RW:(m + 1) * RW], g.ps[0:HR, 4 + k, :], ACT.Silu, bias=g.b2[:, 0:1])
        if m == RSTEPS - 1:
            act.drain().then_inc(r.h2_made[b], 1)
            act.wait_ge(r.h2_made[b], i + 1)
            act.dma_start(g.hidden[:, chunk_cols(i, b, P)], h2[:, b, :]).then_inc(r.h2_free[b], 16)
            act.wait_ge(r.rad_free[b], i + 1)
            act.dma_start(rad[:, b, :], g.edge_rad[:, bass.ds(i * (2 * J * P) + (b + 2) * J * P, J * P)])\
               .then_inc(r.rad_in[b], 16)

    with act.Fori(0, PAIRS) as i:
        for n in range(2 * RSTEPS):
            k = n % 2
            act.wait_ge(r.h1_in[k], i * RSTEPS + n // 2 + 1)
            nc.scalar.activation(h1[:, k, :], g.ps[0:HR, 2 + k, :], ACT.Silu, bias=g.b1[:, 0:1]).then_inc(r.h1_out[k], 1)
            if n > 0:
                second_layer(i, n - 1)
        second_layer(i, 2 * RSTEPS - 1)
    for b in range(2):
        act.wait_ge(r.h2_free[b], 16 * PAIRS + 16)
        act.wait_ge(r.rad_in[b], 16 * PAIRS + 16)


class RadialSems:

    def __init__(self, sem):
        pair = lambda n: [sem(f"radial_{n}{b}") for b in range(2)]
        self.rad_in, self.rad_free, self.h1_in, self.h1_out = pair("in"), pair("free"), pair("h1_in"), pair("h1_out")
        self.h2_in, self.h2_made, self.h2_free = pair("h2_in"), pair("h2_made"), pair("h2_free")


def edge_stage_plain(nc, g, name, table, rows, weights=None):
    with ExitStack() as ph:
        sb = lambda n, s, d=F32: ph.enter_context(nc.sbuf_tensor(f"{name}_{n}", s, d))
        s = EdgeSems(g.sem, g.gather_sem, name)
        buf = sb("rows", [P, 2, J, D])
        first = weights is not None
        if first:
            wl = WeightLoad(nc, g, weights, ph)
            dst_i = sb("dst_i", [P, EC], I32)
            prev_i = sb("prev_i", [P, EC], I32)
            src_i = sb("src_i", [P, EC], I32)
            dst_f = sb("dst_f", [P, EC])
            src_f = sb("src_f", [P, EC])
            tmp_f = sb("tmp_f", [P, EC])
            hi = sb("hi", [P, 2, EC], BF16)
            lo = sb("lo", [P, 2, EC], BF16)
            iota_b = sb("iota_b", [P, P], BF16)
            onehot_hi = sb("onehot_hi", [P, 2, 2, OH, NP_], BF16)
            onehot_lo = sb("onehot_lo", [P, 2, 2, OH, NC_], BF16)
            zero_b = sb("zero_b", [P, P], BF16)
            graph_in, oh_used, oh_made, hist_zero, hist_done = (
                g.sem("graph_in"), [g.sem(f"oh_used{b}") for b in range(2)], [g.sem(f"oh_made{b}") for b in range(2)],
                g.sem("hist_zero"), g.sem("hist_done"))
            er_zero = g.sem("er_zero")
            zeroed = g.sem("zeroed")
        else:
            rs = RadialSems(g.sem)
            rad = sb("rad", [8, 2, J * P])
            h1 = sb("h1", [HR, 2, RW])
            h2 = sb("h2", [HR, 2, J * P])
        with nc.Block() as block:
            @block.gpsimd
            def _(pool):
                if not first:
                    for b in range(2):
                        pool.sem_inc(rs.h2_free[b], 16)
                if first:
                    wl.constants(pool)
                gather_chunks(nc, g, pool, table, buf, s)
                clear_past(g, pool)

            @block.sync
            def _(sp):
                if first:
                    dst_cols = lambda o: g.dst_flat[0:1, o:o + EROWS].rearrange("a (p c) -> (a p) c", c=EC)
                    for b in range(2):
                        sp.dma_start(g.idx[:, b, :], g.src_cols[:, b * J:(b + 1) * J]).then_inc(s.idx_in[b], 16)
                    sp.dma_start(dst_i[:, :], dst_cols(1)).then_inc(graph_in, 16)
                    sp.dma_start(prev_i[:, :], dst_cols(0)).then_inc(graph_in, 16)
                    sp.dma_start(src_i[:, :], g.src_cols[:, 0:EC]).then_inc(graph_in, 16)
                    wl.load(sp)
                    sp.wait_ge(zeroed, 1)
                    for k in range(4):
                        sp.dma_start(g.er_edges[0:EROWS, :].rearrange("(p c) h -> p (c h)", p=P)[:, k * EC:(k + 1) * EC],
                                     tmp_f[:, :]).then_inc(er_zero, 16)
                    for r, width in ((g.rows0, D), (g.rows1, ROW1), (g.rows2, D), (g.rows3, D)):
                        sp.dma_start(r[EROWS:EROWS + 1, :], tmp_f[0:1, 0:width]).then_inc(er_zero, 16)
                else:
                    for b in range(2):
                        sp.dma_start(g.idx[:, b, :], g.src_cols[:, b * J:(b + 1) * J]).then_inc(s.idx_in[b], 16)
                        sp.dma_start(rad[:, b, :], g.edge_rad[:, b * J * P:(b + 1) * J * P]).then_inc(rs.rad_in[b], 16)
                rows_v = rows[0:EROWS, :].rearrange("(p c) f -> p (c f)", p=P)
                with sp.Fori(0, PAIRS) as i:
                    for b in range(2):
                        sp.wait_ge(s.rows_in[b], (16 * J) * i + 16 * J)
                        sp.dma_start(g.idx[:, b, :], g.src_cols[:, bass.ds(i * (2 * J) + (b + 2) * J, J)])\
                          .then_inc(s.idx_in[b], 16)
                        sp.wait_ge(s.scanned[b], i + 1)
                        sp.dma_start(rows_v[:, chunk_cols(i, b, D)], buf[:, b].rearrange("p j f -> p (j f)"))\
                          .then_inc(s.buf_free[b], 16)
                for b in range(2):
                    sp.wait_ge(s.buf_free[b], 16 * PAIRS + 16)
                    sp.wait_ge(s.idx_in[b], 16 * PAIRS + 16)
                if first:
                    sp.wait_ge(er_zero, 16 * 8)

            @block.vector
            def _(dve):
                if first:
                    wl.clear(dve)
                    nc.vector.memset(tmp_f[:, :], 0.0)
                    nc.vector.memset(zero_b[:, :], 0.0)
                    dve.drain().then_inc(zeroed, 1)
                    dve.wait_ge(wl.ids, 1)
                    nc.vector.tensor_copy(iota_b[:, :], g.iota_i[:, :])
                    dve.wait_ge(graph_in, 48)
                    nc.vector.tensor_tensor(g.cont[:, :], dst_i[:, :], prev_i[:, :], ALU.is_equal)
                    nc.vector.tensor_copy(dst_f[:, :], dst_i[:, :])
                    nc.vector.tensor_copy(src_f[:, :], src_i[:, :])
                    dve.drain()
                    dve.wait_ge(er_zero, 16 * 8)
                    nc.vector.tensor_scalar(g.dst0_f[:, :], dst_f[:, 0:1], float(N - 1), None, ALU.min)
                    for k, n_f in enumerate((src_f, dst_f)):
                        nc.vector.tensor_scalar(tmp_f[:, :], n_f[:, :], 1.0 / NC_, -0.495, ALU.mult, ALU.add)
                        dve.drain()
                        nc.vector.tensor_scalar(tmp_f[:, :], tmp_f[:, :], ROUND, ROUND, ALU.add, ALU.subtract)
                        dve.drain()
                        nc.vector.scalar_tensor_tensor(lo[:, k, :], tmp_f[:, :], -float(NC_), n_f[:, :], ALU.mult, ALU.add)
                        nc.vector.tensor_copy(hi[:, k, :], tmp_f[:, :])
                        dve.drain()
                    nc.vector.tensor_scalar(tmp_f[:, :], dst_f[:, :], float(N), 2.0 * NP_, ALU.is_ge, ALU.mult)
                    nc.vector.tensor_copy(g.dst0_i[:, :], g.dst0_f[:, :])
                    dve.drain()
                    nc.vector.tensor_tensor(hi[:, 0, :], hi[:, 0, :], tmp_f[:, :], ALU.add)
                    wl.form(dve)
                nc.vector.memset(g.carry[:, :], 0.0)
                dve.drain()
                with dve.Fori(0, PAIRS) as i:
                    for b in range(2):
                        if first:
                            for k in range(J // OH):
                                h = k % 2
                                dve.wait_ge(oh_used[h], i * (J // OH) + (b * (J // OH) + k) // 2 + 1)
                                cols = bass.ds(i * (2 * J) + (b * J + k * OH), OH)
                                for e in range(2):
                                    nc.vector.tensor_tensor(
                                        onehot_hi[:, h, e], bcast(iota_b[:, 0:NP_], 1, OH),
                                        bcast(hi[:, e, cols], 2, NP_), ALU.is_equal)
                                    last = nc.vector.tensor_tensor(
                                        onehot_lo[:, h, e], bcast(iota_b[:, 0:NC_], 1, OH),
                                        bcast(lo[:, e, cols], 2, NC_), ALU.is_equal)
                                dve.drain().then_inc(oh_made[h], 1)
                        dve.wait_ge(s.rows_in[b], (16 * J) * i + 16 * J)
                        scan_rows(nc, g, dve, i, b, buf, g.carry, D)
                        dve.drain().then_inc(s.scanned[b], 1)
                if first:
                    dve.wait_ge(hist_done, 1)
                    nc.vector.tensor_copy(g.deg[:, 0, :], g.ps[0:NP_, 0, 0:NC_])
                    nc.vector.tensor_copy(g.deg[:, 1, :], g.ps[0:NP_, 1, 0:NC_])
                    dve.drain()

            if not first:
                @block.tensor
                def _(pe):
                    radial_tensor(nc, g, pe, rad, h1, rs)

                @block.scalar
                def _(act):
                    radial_scalar(nc, g, act, rad, h1, h2, rs)
            else:
                @block.tensor
                def _(pe):
                    wl.products(pe)
                    pe.wait_ge(zeroed, 1)
                    for e in range(2):
                        nc.tensor.matmul(g.ps[0:NP_, e, 0:NC_], zero_b[:, 0:NP_], zero_b[:, 0:NC_], start=True, stop=False)
                    for h in range(2):
                        pe.sem_inc(oh_used[h], 1)
                    with pe.Fori(0, CHUNKS) as i:
                        for k in range(J // OH):
                            h = k % 2
                            pe.wait_ge(oh_made[h], i * (J // OH // 2) + k // 2 + 1)
                            for e in range(2):
                                for c in range(OH):
                                    last = nc.tensor.matmul(g.ps[0:NP_, e, 0:NC_], onehot_hi[:, h, e, c, :],
                                                            onehot_lo[:, h, e, c, :], start=False, stop=False)
                            last.then_inc(oh_used[h], 1)
                    for e in range(2):
                        last = nc.tensor.matmul(g.ps[0:NP_, e, 0:NC_], zero_b[:, 0:NP_], zero_b[:, 0:NC_],
                                                start=False, stop=True)
                    last.then_inc(hist_done, 1)


def index_stage(nc, g):
    with ExitStack() as ph:
        sb = lambda n, s, d=F32: ph.enter_context(nc.sbuf_tensor(f"ix_{n}", s, d))
        run = sb("run", [NP_, NC_])
        ones = sb("ones", [NP_, NC_])
        node = sb("node", [NP_, NC_])
        last_e = sb("last_e", [NP_, NC_])
        first_e = sb("first_e", [NP_, NC_])
        alt = sb("alt", [NP_, NC_])
        empty = sb("empty", [NP_, NC_])
        base = sb("base", [NP_, 1])
        prod = sb("prod", [P, EC])
        lead = sb("lead", [P, 1])
        fe = sb("fe", [P, 1])
        flag = sb("flag", [P, 1])
        whole = sb("whole", [P, 1])
        flags_wide = sb("flags_wide", [P, 2, P])
        run_made, base_made, flags_made, flags_turned = (g.sem("ix_run"), g.sem("ix_base"), g.sem("ix_flags"), g.sem("ix_turned"))
        norm_in, norm_out = g.sem("ix_norm_in"), g.sem("ix_norm_out")
        with nc.Block() as block:
            @block.gpsimd
            def _(pool):
                clear_past(g, pool)

            @block.vector
            def _(dve):
                v = nc.vector
                v.memset(ones[:, :], 1.0)
                v.tensor_copy(node[:, :], g.node_i[0:NP_, :])
                v.tensor_scalar(g.norm[:, :, :], g.deg[:, :, :], 1.0, None, ALU.max)
                dve.drain().then_inc(norm_in, 1)
                v.tensor_tensor_scan(run[:, :], ones[:, :], g.deg[:, 1, :], 0.0, ALU.mult, ALU.add)
                dve.drain().then_inc(run_made, 1)
                v.tensor_tensor_scan(prod[:, 0:EC - 1], g.cont[:, 1:EC], g.cont[:, 1:EC], 1.0, ALU.mult, ALU.min)
                v.tensor_copy(fe[:, :], g.first_edge_i[:, :])
                dve.drain()
                v.reduce_sum(lead[:, :], prod[:, 0:EC - 1], axis=AX.X)
                v.tensor_tensor(whole[:, :], prod[:, EC - 2:EC - 1], g.cont[:, 0:1], ALU.mult)
                dve.drain()
                v.tensor_tensor(fe[:, :], fe[:, :], lead[:, :], ALU.add)
                v.tensor_copy(flags_wide[:, 0, :], g.cont[:, 0:1].broadcast_to([P, P]))
                v.tensor_copy(flags_wide[:, 1, :], whole[:, 0:1].broadcast_to([P, P]))
                dve.drain().then_inc(flags_made, 1)
                v.tensor_copy(g.border_idx[:, :], fe[:, :])
                dve.wait_ge(base_made, 1)
                v.tensor_copy(base[:, :], g.ps[0:NP_, 2, 0:1])
                v.tensor_scalar(empty[:, :], g.deg[:, 1, :], 0.0, None, ALU.is_equal)
                dve.drain()
                v.tensor_scalar(last_e[:, :], run[:, :], base[:, 0:1], -1.0, ALU.add, ALU.add)
                dve.drain()
                v.tensor_tensor(first_e[:, :], last_e[:, :], g.deg[:, 1, :], ALU.subtract)
                v.tensor_scalar(alt[:, :], last_e[:, :], -1.0, float(EROWS), ALU.mult, ALU.add)
                dve.drain()
                v.tensor_scalar(first_e[:, :], first_e[:, :], 1.0, None, ALU.add)
                v.tensor_tensor(alt[:, :], alt[:, :], empty[:, :], ALU.mult)
                dve.drain()
                v.tensor_tensor(last_e[:, :], last_e[:, :], alt[:, :], ALU.add)
                dve.drain()
                v.tensor_scalar(node[:, :], node[:, :], float(EROWS), None, ALU.add)
                dve.drain()
                v.tensor_tensor(node[:, :], node[:, :], first_e[:, :], ALU.subtract)
                dve.drain()
                v.tensor_tensor(node[:, :], node[:, :], empty[:, :], ALU.mult)
                dve.drain()
                v.tensor_tensor(first_e[:, :], first_e[:, :], node[:, :], ALU.add)
                v.memset(g.last_i[:, NC_:NC_ + 2 * G], 0)
                v.tensor_copy(g.last_i[:, 0:NC_], last_e[:, :])
                dve.drain()
                v.tensor_copy(g.first_i[:, :], first_e[:, :])
                dve.wait_ge(norm_out, 1)
                v.reciprocal(g.norm[:, :, :], g.norm[:, :, :])
                dve.wait_ge(flags_turned, 1)
                v.tensor_copy(g.cont0[:, :], g.ps[:, 3, 0:P])
                v.tensor_copy(g.linked[:, :], g.ps[:, 3, P:2 * P])
                v.memset(g.link[:, :], 0.0)
                dve.drain()
                v.tensor_tensor(g.link[:, 1:P], g.cont0[:, 1:P], g.linked[:, 0:P - 1], ALU.mult)
                dve.drain()

            @block.scalar
            def _(act):
                act.wait_ge(norm_in, 1)
                nc.scalar.activation(g.norm[:, :, :], g.norm[:, :, :], ACT.Sqrt).then_inc(norm_out, 1)

            @block.tensor
            def _(pe):
                pe.wait_ge(run_made, 1)
                nc.tensor.matmul(g.ps[0:NP_, 2, 0:1], g.ltri[0:NP_, 0:NP_], run[:, NC_ - 1:NC_],
                                 start=True, stop=True).then_inc(base_made, 1)
                pe.wait_ge(flags_made, 1)
                nc.tensor.transpose(g.ps[:, 3, 0:P], flags_wide[:, 0, :], g.ident[:, :])
                nc.tensor.transpose(g.ps[:, 3, P:2 * P], flags_wide[:, 1, :], g.ident[:, :]).then_inc(flags_turned, 1)


def border_stage_plain(nc, g, name, rows):
    with ExitStack() as ph:
        sb = lambda n, s, d=F32: ph.enter_context(nc.sbuf_tensor(f"{name}_{n}", s, d))
        patch = sb("patch", [P, D])
        item = sb("item", [D, P])
        into = sb("into", [D, P])
        turned, into_made, back, patched = (g.sem(f"{name}_{n}") for n in ("turned", "into", "back", "patched"))
        fetched, put = g.gather_sem(0), g.gather_sem(1)
        with nc.Block() as block:
            @block.tensor
            def _(pe):
                nc.tensor.transpose(g.ps[0:D, 0, 0:P], g.carry[:, 0:D], g.ident[:, :]).then_inc(turned, 1)
                pe.wait_ge(into_made, 1)
                nc.tensor.transpose(g.ps[:, 1, 0:D], into[:, :], g.ident[0:D, 0:D]).then_inc(back, 1)

            @block.vector
            def _(dve):
                nc.vector.memset(item[:, :], 0.0)
                dve.drain()
                dve.wait_ge(turned, 1)
                nc.vector.tensor_tensor(item[:, 1:P], g.cont0[0:D, 1:P], g.ps[0:D, 0, 0:P - 1], ALU.mult)
                dve.drain()
                nc.vector.tensor_tensor_scan(into[:, :], g.link[0:D, :], item[:, :], 0.0, ALU.mult, ALU.add)\
                    .then_inc(into_made, 1)
                dve.wait_ge(back, 1)
                dve.wait_ge(fetched, 16)
                nc.vector.tensor_tensor(patch[:, :], patch[:, :], g.ps[:, 1, 0:D], ALU.add).then_inc(patched, 1)

            @block.gpsimd
            def _(pool):
                pool.indirect_dma_start(patch[:, :], None, rows[:, :], bass.IndirectOffsetOnAxis(g.border_idx[:, 0:1], 0))\
                    .then_inc(fetched, 16)
                pool.wait_ge(patched, 1)
                pool.indirect_dma_start(rows[:, :], bass.IndirectOffsetOnAxis(g.border_idx[:, 0:1], 0), patch[:, :], None)\
                    .then_inc(put, 16)
                clear_past(g, pool)
                pool.wait_ge(put, 16)



class NodeSems:

    def __init__(self, sem, gather_sem, name):
        pair = lambda n: [sem(f"{name}_{n}{b}") for b in range(2)]
        self.gathered = [gather_sem(b) for b in range(2)]
        self.idx_ready, self.x_in, self.free = pair("idx_ready"), pair("x_in"), pair("free")
        self.stored, self.new_ready = pair("stored"), pair("new_ready")
        self.turned, self.turned_sb, self.product = pair("turned"), pair("turned_sb"), pair("product")
        self.x_turned, self.x_turned_sb, self.x_product = pair("x_turned"), pair("x_turned_sb"), pair("x_product")
        self.agg_ready, self.var, self.std, self.prods_used = pair("agg_ready"), pair("var"), pair("std"), pair("prods_used")
        self.gates_act, self.hidden, self.hidden_act = pair("gates_act"), pair("hidden"), pair("hidden_act")
        self.low, self.low_act = pair("low"), pair("low_act")


def load_residual(nc, g, sp, s, xg, x_rows):
    x_v = x_rows.rearrange("(p j) f -> p (j f)", p=NP_)

    def load(i, b):
        sp.dma_start(xg[:, b].rearrange("p j f -> p (j f)"), x_v[:, bass.ds(i * (2 * G * D) + b * G * D, G * D)])\
          .then_inc(s.x_in[b], 16)
    for b in range(2):
        load(0, b)
    with sp.Fori(0, GROUPS // 2 - 1) as i:
        for b in range(2):
            sp.wait_ge(s.free[b], i + 1)
            load(i + 1, b)


def group_cols(i, b):
    return bass.ds(i * (2 * G) + b * G, G)


def next_index(nc, g, dve, s, nidx, i, b):
    nc.vector.tensor_copy(nidx[:, b, :], g.last_i[:, group_cols(i, b)])
    dve.drain().then_inc(s.idx_ready[b], 1)


def node_gathers(nc, g, pool, s, nidx, agg, rows):
    with pool.Fori(0, GROUPS // 2) as i:
        for b in range(2):
            pool.wait_ge(s.idx_ready[b], i + 1)
            pool.nop(nofuse=True)
            for j in range(G):
                pool.indirect_dma_start(agg[:, b, j, :], None, rows[:, :],
                                        bass.IndirectOffsetOnAxis(nidx[:, b, j:j + 1], 0)).then_inc(s.gathered[b], 16)


def node_stores(nc, g, eng, s, i, b, new, dests):
    eng.wait_ge(s.new_ready[b], i + 1)
    for buf, rows in dests:
        width = rows.shape[1]
        eng.dma_start(rows.rearrange("(p j) f -> p (j f)", p=NP_)[:, bass.ds(i * (2 * G * width) + b * G * width, G * width)],
                      buf[:, b].rearrange("p j f -> p (j f)")).then_inc(s.stored[b], 16)


def turn_group(nc, g, pe, src, psum):
    for q, (c, k) in enumerate(QUADS):
        last = nc.tensor.transpose(psum[0:k * D, q * P:q * P + NP_], src[:, c:c + k, :].rearrange("p j f -> p (j f)"),
                                   g.ident[0:NP_, 0:NP_])
    return last


def copy_turned(nc, turned, psum):
    nc.scalar.activation(turned[:, 0:2, 0:NP_], psum[:, 0:2 * P].rearrange("p (q n) -> p q n", q=2)[:, :, 0:NP_], ACT.Copy)
    return nc.scalar.activation(turned[0:2 * D, 2, 0:NP_], psum[0:2 * D, 2 * P:2 * P + NP_], ACT.Copy)


def apply_bd(nc, pe, psum, turned, weight, width):
    for q, (c, k) in enumerate(QUADS):
        last = nc.tensor.matmul(psum[0:NP_, c * width:(c + k) * width], turned[0:k * D, q, 0:NP_],
                                weight[0:k * D, 0:k * width], start=True, stop=True)
    return last


def layernorm_moments(nc, dve, s, b, r, t, stat):
    v = nc.vector
    v.reduce_sum(stat[:, b, 0, :], r, axis=AX.X)
    dve.drain()
    v.scalar_tensor_tensor(r, bcast(stat[:, b, 0, :], 2, D), -1.0 / D, r, ALU.mult, ALU.add)
    dve.drain()
    v.tensor_tensor(t, r, r, ALU.mult)
    dve.drain()
    v.reduce_sum(stat[:, b, 0, :], t, axis=AX.X)
    dve.drain()
    v.tensor_scalar(stat[:, b, 2, :], stat[:, b, 0, :], 1.0 / D, EPS, ALU.mult, ALU.add).then_inc(s.var[b], 1)


def layernorm_scale(nc, dve, s, i, b, r, stat, out):
    dve.wait_ge(s.std[b], i + 1)
    nc.vector.reciprocal(stat[:, b, 4, :], stat[:, b, 3, :])
    dve.drain()
    return nc.vector.tensor_tensor(out, r, bcast(stat[:, b, 4, :], 2, D), ALU.mult)


def layernorm_sqrt(nc, act, s, i, b, stat):
    act.wait_ge(s.var[b], i + 1)
    nc.scalar.activation(stat[:, b, 3, :], stat[:, b, 2, :], ACT.Sqrt).then_inc(s.std[b], 1)


def node_stage_plain(nc, g, name, layer, rows, x_in, dests):
    with ExitStack() as ph:
        sb = lambda n, s_, d=F32: ph.enter_context(nc.sbuf_tensor(f"{name}_{n}", s_, d))
        s = NodeSems(g.sem, g.gather_sem, name)
        nidx = sb("nidx", [NP_, 2, G], I32)
        xg = sb("xg", [NP_, 2, G, D])
        agg = sb("agg", [NP_, 2, G, D])
        turned = sb("turned", [P, 2, 3, P])
        xturned = sb("xturned", [P, 2, 3, P])
        r = sb("r", [NP_, 2, G, D])
        t = sb("t", [NP_, 2, G, D])
        stat = sb("stat", [NP_, 2, 5, G])
        new = sb("new", [NP_, 2, G, D])
        t1 = sb("t1", [NP_, 2, G, T1W])
        bd = {0: g.bd0, 2: g.bd2, 3: g.bdself}[layer]
        bufs = {"x": new, "t1": t1}
        n_dest = len(dests)
        if layer == 0:
            er_put, dst0_got = g.gather_sem("er"), g.gather_sem("dst0")
        with nc.Block() as block:
            @block.sync
            def _(sp):
                load_residual(nc, g, sp, s, xg, x_in)
                for b in range(2):
                    sp.wait_ge(s.stored[b], 16 * n_dest * (GROUPS // 2 + 1))

            @block.gpsimd
            def _(pool):
                for b in range(2):
                    pool.sem_inc(s.stored[b], 16 * n_dest)
                node_gathers(nc, g, pool, s, nidx, agg, rows)
                if layer == 0:
                    for n in range(GROUPS):
                        pool.wait_ge(s.new_ready[n % 2], n // 2 + 1)
                        for c in range(n * G, (n + 1) * G):
                            pool.indirect_dma_start(g.er_edges[:, :], bass.IndirectOffsetOnAxis(g.first_i[:, c:c + 1], 0),
                                                    g.er_nodes[:, c, :], None).then_inc(er_put, 16)
                    for b in range(2):
                        pool.wait_ge(s.stored[b], 16 * n_dest * (GROUPS // 2 + 1))
                    pool.indirect_dma_start(g.row_dst0[:, :], None, g.table1[:, :],
                                            bass.IndirectOffsetOnAxis(g.dst0_i[:, 0:1], 0)).then_inc(dst0_got, 16)
                    pool.wait_ge(er_put, 16 * NC_)
                    pool.wait_ge(dst0_got, 16)
                clear_past(g, pool)

            @block.tensor
            def _(pe):
                with pe.Fori(0, GROUPS // 2) as i:
                    for b in range(2):
                        if layer == 3:
                            pe.wait_ge(s.x_in[b], 16 * i + 16)
                            turn_group(nc, g, pe, xg[:, b], g.ps[:, b, :]).then_inc(s.turned[b], 1)
                        elif layer == 2:
                            pe.wait_ge(s.agg_ready[b], i + 1)
                            turn_group(nc, g, pe, r[:, b], g.ps[:, b, :]).then_inc(s.turned[b], 1)
                        else:
                            pe.wait_ge(s.gathered[b], 16 * G * i + 16 * G)
                            turn_group(nc, g, pe, agg[:, b], g.ps[:, b, :]).then_inc(s.turned[b], 1)
                        pe.wait_ge(s.turned_sb[b], i + 1)
                        apply_bd(nc, pe, g.ps[:, 2 + b, :], turned[:, b], bd, D).then_inc(s.product[b], 1)
                        if layer == 0:
                            pe.wait_ge(s.agg_ready[b], i + 1)
                            turn_group(nc, g, pe, new[:, b], g.ps[:, 4 + b, :]).then_inc(s.x_turned[b], 1)
                            pe.wait_ge(s.x_turned_sb[b], i + 1)
                            apply_bd(nc, pe, g.ps[:, 6 + b, :], xturned[:, b], g.bdel, 2 * H).then_inc(s.x_product[b], 1)

            @block.scalar
            def _(act):
                with act.Fori(0, GROUPS // 2) as i:
                    for b in range(2):
                        act.wait_ge(s.turned[b], i + 1)
                        copy_turned(nc, turned[:, b], g.ps[:, b, :]).then_inc(s.turned_sb[b], 1)
                        layernorm_sqrt(nc, act, s, i, b, stat)
                        if layer == 0:
                            act.wait_ge(s.x_turned[b], i + 1)
                            copy_turned(nc, xturned[:, b], g.ps[:, 4 + b, :]).then_inc(s.x_turned_sb[b], 1)
                        node_stores(nc, g, act, s, i, b, None, [(bufs[k], d) for k, d in dests])

            @block.vector
            def _(dve):
                v = nc.vector
                for b in range(2):
                    next_index(nc, g, dve, s, nidx, 0, b)
                with dve.Fori(0, GROUPS // 2) as i:
                    for b in range(2):
                        cols = group_cols(i, b)
                        dve.wait_ge(s.x_in[b], 16 * i + 16)
                        dve.wait_ge(s.gathered[b], 16 * G * i + 16 * G)
                        if layer == 2:
                            v.tensor_tensor(r[:, b], agg[:, b], bcast(g.norm[:, 1, cols], 2, D), ALU.mult)\
                                .then_inc(s.agg_ready[b], 1)
                            v.tensor_tensor(t[:, b], xg[:, b], bcast(g.b2row[:, :], 1, G), ALU.add)
                        if layer == 3:
                            v.tensor_tensor(t[:, b], xg[:, b], agg[:, b], ALU.add)
                        if layer != 0:
                            dve.drain()
                            next_index(nc, g, dve, s, nidx, i + 1, b)
                        dve.wait_ge(s.product[b], i + 1)
                        v.tensor_tensor(r[:, b], xg[:, b] if layer == 0 else t[:, b],
                                        g.ps[0:NP_, 2 + b, 0:G * D].rearrange("p (j f) -> p j f", f=D), ALU.add)
                        if layer == 0:
                            next_index(nc, g, dve, s, nidx, i + 1, b)
                        dve.drain().then_inc(s.free[b], 1)
                        dve.wait_ge(s.stored[b], 16 * n_dest * i + 16 * n_dest)
                        layernorm_moments(nc, dve, s, b, r[:, b], t[:, b], stat)
                        layernorm_scale(nc, dve, s, i, b, r[:, b], stat, new[:, b])
                        if layer == 0:
                            dve.drain().then_inc(s.agg_ready[b], 1)
                            v.tensor_copy(t1[:, b, :, 0:D], new[:, b])
                            dve.wait_ge(s.x_product[b], i + 1)
                            el_er = g.ps[0:NP_, 6 + b, 0:G * 2 * H].rearrange("p (j h) -> p j h", h=2 * H)
                            v.tensor_copy(t1[:, b, :, D:T1W], el_er)
                            v.tensor_copy(g.er_nodes[:, cols, :], el_er[:, :, H:2 * H])
                        dve.drain().then_inc(s.new_ready[b], 1)


def edge_stage_attention(nc, g):
    with ExitStack() as ph:
        sb = lambda n, s_, d=F32: ph.enter_context(nc.sbuf_tensor(f"e1_{n}", s_, d))
        s = EdgeSems(g.sem, g.gather_sem, "e1")
        gat = sb("gat", [P, 2, J, T1W])
        er0 = sb("er0", [P, 2, J, H])
        er = sb("er", [P, J, H])
        er_carry = sb("er_carry", [P, H])
        e = sb("e", [P, J, H])
        e2 = sb("e2", [P, J, H])
        neg = sb("neg", [P, J])
        expo = sb("expo", [P, 2, J, H])
        wexp = sb("wexp", [P, 2, J, H])
        acc = sb("acc", [P, 2, J, ROW1])
        er_in = [g.sem(f"e1_er_in{b}") for b in range(2)]
        gat_free = [g.sem(f"e1_gat_free{b}") for b in range(2)]
        expo_ready, wexp_ready = g.sem("e1_expo"), g.sem("e1_wexp")
        with nc.Block() as block:
            @block.gpsimd
            def _(pool):
                for b in range(2):
                    pool.sem_inc(gat_free[b], 1)
                    pool.sem_inc(s.buf_free[b], 16)
                with pool.Fori(0, PAIRS) as i:
                    for b in range(2):
                        pool.wait_ge(s.idx_in[b], 16 * i + 16)
                        pool.wait_ge(gat_free[b], i + 1)
                        pool.nop(nofuse=True)
                        for j in range(J):
                            pool.indirect_dma_start(gat[:, b, j, :], None, g.table1[:, :],
                                                    bass.IndirectOffsetOnAxis(g.idx[:, b, j:j + 1], 0)).then_inc(s.rows_in[b], 16)
                clear_past(g, pool)

            @block.sync
            def _(sp):
                er_v = g.er_edges[0:EROWS, :].rearrange("(p c) h -> p (c h)", p=P)
                chunk = lambda i, b, width: bass.ds(i * (2 * J * width) + b * J * width, J * width)
                for b in range(2):
                    sp.dma_start(g.idx[:, b, :], g.src_cols[:, b * J:(b + 1) * J]).then_inc(s.idx_in[b], 16)
                    sp.dma_start(er0[:, b].rearrange("p j h -> p (j h)"), er_v[:, b * J * H:(b + 1) * J * H]).then_inc(er_in[b], 16)
                with sp.Fori(0, PAIRS - 1) as i:
                    for b in range(2):
                        sp.wait_ge(s.rows_in[b], (16 * J) * i + 16 * J)
                        sp.dma_start(g.idx[:, b, :], g.src_cols[:, chunk(i, b + 2, 1)]).then_inc(s.idx_in[b], 16)
                        sp.wait_ge(gat_free[b], i + 2)
                        sp.dma_start(er0[:, b].rearrange("p j h -> p (j h)"), er_v[:, chunk(i, b + 2, H)]).then_inc(er_in[b], 16)
                for b in range(2):
                    sp.wait_ge(s.buf_free[b], 16 * PAIRS + 16)

            @block.scalar
            def _(act):
                rows_v = g.rows1[0:EROWS, :].rearrange("(p c) f -> p (c f)", p=P)
                with act.Fori(0, PAIRS) as i:
                    for b in range(2):
                        act.wait_ge(expo_ready, i * 2 + (b + 1))
                        nc.scalar.activation(wexp[:, :, :, :], expo[:, :, :, :], ACT.Exp).then_inc(wexp_ready, 1)
                        act.wait_ge(s.scanned[b], i + 1)
                        act.dma_start(rows_v[:, chunk_cols(i, b, ROW1)], acc[:, b].rearrange("p j f -> p (j f)"))\
                           .then_inc(s.buf_free[b], 16)

            @block.vector
            def _(dve):
                v = nc.vector
                v.memset(g.carry[:, 0:H], -BIG)
                v.memset(g.carry[:, H:ROW1], 0.0)
                v.tensor_copy(er_carry[:, :], g.row_dst0[:, D + H:T1W])
                dve.drain()
                with dve.Fori(0, PAIRS) as i:
                    for b in range(2):
                        cont = g.cont[:, chunk_cols(i, b)]
                        v.tensor_scalar(neg[:, :], cont, BIG, BIG, ALU.mult, ALU.subtract)
                        dve.wait_ge(er_in[b], 16 * i + 16)
                        for h in range(H):
                            v.tensor_tensor_scan(er[:, :, h], cont, er0[:, b, :, h], er_carry[:, h:h + 1], ALU.mult, ALU.add)
                        dve.drain()
                        v.tensor_copy(er_carry[:, :], er[:, J - 1, :])
                        dve.wait_ge(s.rows_in[b], (16 * J) * i + 16 * J)
                        v.tensor_tensor(e2[:, :, :], gat[:, b, :, D:D + H], er[:, :, :], ALU.add)
                        dve.drain()
                        v.scalar_tensor_tensor(e[:, :, :], e2[:, :, :], 0.2, e2[:, :, :], ALU.mult, ALU.max)
                        dve.drain()
                        dve.wait_ge(s.buf_free[b], 16 * i + 16)
                        for h in range(H):
                            v.tensor_tensor_scan(acc[:, b, :, h], neg[:, :], e[:, :, h], g.carry[:, h:h + 1], ALU.add, ALU.max)
                        dve.drain()
                        v.tensor_tensor(expo[:, 1], e[:, :, :], acc[:, b, :, 0:H], ALU.subtract)
                        v.tensor_tensor(e2[:, 0:1, :], bcast(neg[:, 0:1], 2, H), g.carry[:, 0:H].unsqueeze(1), ALU.add)
                        v.tensor_tensor(e2[:, 1:J, :], bcast(neg[:, 1:J], 2, H), acc[:, b, 0:J - 1, 0:H], ALU.add)
                        dve.drain()
                        v.tensor_tensor(expo[:, 0], e2[:, :, :], acc[:, b, :, 0:H], ALU.subtract)
                        dve.drain().then_inc(expo_ready, 1)
                        dve.wait_ge(wexp_ready, i * 2 + (b + 1))
                        v.tensor_copy(acc[:, b, :, H:2 * H], wexp[:, 1])
                        for h in range(H):
                            v.tensor_tensor(acc[:, b, :, 2 * H + h * D:2 * H + (h + 1) * D], gat[:, b, :, 0:D],
                                            bcast(wexp[:, 1, :, h], 2, D), ALU.mult)
                        dve.drain().then_inc(gat_free[b], 1)
                        for h in range(H):
                            for c in [H + h] + list(range(2 * H + h * D, 2 * H + (h + 1) * D)):
                                v.tensor_tensor_scan(acc[:, b, :, c], wexp[:, 0, :, h], acc[:, b, :, c],
                                                     g.carry[:, c:c + 1], ALU.mult, ALU.add)
                        dve.drain()
                        v.tensor_copy(g.carry[:, 0:ROW1], acc[:, b, J - 1, :])
                        dve.drain().then_inc(s.scanned[b], 1)


def border_stage_attention(nc, g):
    with ExitStack() as ph:
        sb = lambda n, s_, d=F32: ph.enter_context(nc.sbuf_tensor(f"b1_{n}", s_, d))
        patch = sb("patch", [P, ROW1])
        wide = sb("wide", [P, 3, P])
        item_m = sb("item_m", [P, P])
        into_m = sb("into_m", [P, P])
        expo = sb("expo", [P, 2, P])
        fac = sb("fac", [P, 2, P])
        neg_link = sb("neg_link", [P, P])
        neg_c0 = sb("neg_c0", [P, P])
        item_v = sb("item_v", [P, 2, P])
        into_v = sb("into_v", [P, 2, P])
        joined = sb("joined", [P, 2, P])
        m_all = sb("m_all", [P, 2, P])
        names = ("wide", "turned", "expo", "fac", "into", "back", "expo2", "fac2", "patched")
        wide_ready, turned, expo_ready, fac_ready, into_ready, back, expo2, fac2, patched = (
            g.sem(f"b1_{n}") for n in names)
        fetched, put = g.gather_sem(0), g.gather_sem(1)
        with nc.Block() as block:
            @block.gpsimd
            def _(pool):
                pool.indirect_dma_start(patch[:, :], None, g.rows1[:, :], bass.IndirectOffsetOnAxis(g.border_idx[:, 0:1], 0))\
                    .then_inc(fetched, 16)
                pool.wait_ge(patched, 1)
                pool.indirect_dma_start(g.rows1[:, :], bass.IndirectOffsetOnAxis(g.border_idx[:, 0:1], 0), patch[:, :], None)\
                    .then_inc(put, 16)
                clear_past(g, pool)
                pool.wait_ge(put, 16)

            @block.tensor
            def _(pe):
                pe.wait_ge(wide_ready, 1)
                for k in range(3):
                    last = nc.tensor.transpose(g.ps[:, k, 0:P], wide[:, k, :], g.ident[:, :])
                last.then_inc(turned, 1)
                pe.wait_ge(into_ready, 1)
                nc.tensor.transpose(g.ps[:, 3, 0:P], into_m[:, :], g.ident[:, :])
                for k in range(2):
                    last = nc.tensor.transpose(g.ps[:, 4 + k, 0:P], into_v[:, k, :], g.ident[:, :])
                last.then_inc(back, 1)

            @block.scalar
            def _(act):
                act.wait_ge(expo_ready, 1)
                nc.scalar.activation(fac[:, :, :], expo[:, :, :], ACT.Exp).then_inc(fac_ready, 1)
                act.wait_ge(expo2, 1)
                nc.scalar.activation(fac[:, :, :], m_all[:, :, :], ACT.Exp).then_inc(fac2, 1)

            @block.vector
            def _(dve):
                v = nc.vector
                by_head = lambda ap: ap.rearrange("p (h f) -> p h f", h=H)
                v.tensor_copy(by_head(wide[:, 0, :]), bcast(g.carry[:, 0:H], 2, D))
                v.tensor_copy(wide[:, 1, :], g.carry[:, 2 * H:ROW1])
                v.tensor_copy(by_head(wide[:, 2, :]), bcast(g.carry[:, H:2 * H], 2, D))
                dve.drain().then_inc(wide_ready, 1)
                v.tensor_scalar(neg_link[:, :], g.link[:, :], BIG, BIG, ALU.mult, ALU.subtract)
                v.tensor_scalar(neg_c0[:, :], g.cont0[:, :], BIG, BIG, ALU.mult, ALU.subtract)
                v.memset(item_m[:, :], -BIG)
                v.memset(item_v[:, :, :], 0.0)
                v.memset(expo[:, :, :], 0.0)
                dve.drain()
                dve.wait_ge(turned, 1)
                v.tensor_tensor(item_m[:, 1:P], g.cont0[:, 1:P], g.ps[:, 0, 0:P - 1], ALU.mult)
                dve.drain()
                v.tensor_tensor(item_m[:, 1:P], item_m[:, 1:P], neg_c0[:, 1:P], ALU.add)
                dve.drain()
                v.tensor_tensor_scan(into_m[:, :], neg_link[:, :], item_m[:, :], -BIG, ALU.add, ALU.max)
                dve.drain()
                v.tensor_tensor(expo[:, 0, 1:P], into_m[:, 0:P - 1], neg_link[:, 1:P], ALU.add)
                v.tensor_tensor(expo[:, 1, 1:P], item_m[:, 1:P], into_m[:, 1:P], ALU.subtract)
                dve.drain()
                v.tensor_tensor(expo[:, 0, 1:P], expo[:, 0, 1:P], into_m[:, 1:P], ALU.subtract)
                dve.drain().then_inc(expo_ready, 1)
                dve.wait_ge(fac_ready, 1)
                v.tensor_tensor(fac[:, 0, :], fac[:, 0, :], g.link[:, :], ALU.mult)
                for k in range(2):
                    v.tensor_tensor(item_v[:, k, 1:P], fac[:, 1, 1:P], g.ps[:, 1 + k, 0:P - 1], ALU.mult)
                dve.drain()
                for k in range(2):
                    v.tensor_tensor(item_v[:, k, 1:P], item_v[:, k, 1:P], g.cont0[:, 1:P], ALU.mult)
                dve.drain()
                for k in range(2):
                    v.tensor_tensor_scan(into_v[:, k, :], fac[:, 0, :], item_v[:, k, :], 0.0, ALU.mult, ALU.add)
                dve.drain().then_inc(into_ready, 1)
                dve.wait_ge(fetched, 16)
                dve.wait_ge(back, 1)
                v.tensor_copy(m_all[:, 1, :], g.ps[:, 3, 0:P])
                v.tensor_copy(by_head(m_all[:, 0, :]), bcast(patch[:, 0:H], 2, D))
                dve.drain()
                v.tensor_tensor(item_m[:, :], m_all[:, 0, :], m_all[:, 1, :], ALU.max)
                dve.drain()
                v.tensor_tensor(m_all[:, 0, :], m_all[:, 0, :], item_m[:, :], ALU.subtract)
                v.tensor_tensor(m_all[:, 1, :], m_all[:, 1, :], item_m[:, :], ALU.subtract)
                v.tensor_copy(patch[:, 0:H], by_head(item_m[:, :])[:, :, 0])
                dve.drain().then_inc(expo2, 1)
                dve.wait_ge(fac2, 1)
                for k in range(2):
                    v.tensor_tensor(joined[:, k, :], fac[:, 1, :], g.ps[:, 4 + k, 0:P], ALU.mult)
                v.tensor_tensor(patch[:, 2 * H:ROW1], patch[:, 2 * H:ROW1], fac[:, 0, :], ALU.mult)
                v.tensor_tensor(patch[:, H:2 * H], patch[:, H:2 * H], by_head(fac[:, 0, :])[:, :, 0], ALU.mult)
                dve.drain()
                v.tensor_tensor(patch[:, 2 * H:ROW1], patch[:, 2 * H:ROW1], joined[:, 0, :], ALU.add)
                v.tensor_tensor(patch[:, H:2 * H], patch[:, H:2 * H], by_head(joined[:, 1, :])[:, :, 0], ALU.add)
                dve.drain().then_inc(patched, 1)


def pipelined(loop, step):
    def fixed(n):
        return lambda k: ((n + k) // 2, (n + k) % 2) if 0 <= n + k < GROUPS else None
    pairs = (GROUPS - 4) // 2
    step(fixed(0))
    with loop(0, pairs) as i:
        for o in (1, 2):
            step(lambda k, o=o: (i + (o + k) // 2, (o + k) % 2))
    for n in range(2 * pairs + 1, GROUPS + 1):
        step(fixed(n))


def node_stage_gru(nc, g):
    with ExitStack() as ph:
        name = "n1"
        sb = lambda n, s_, d=F32: ph.enter_context(nc.sbuf_tensor(f"{name}_{n}", s_, d))
        s = NodeSems(g.sem, g.gather_sem, name)
        nidx = sb("nidx", [NP_, 2, G], I32)
        xg = sb("xg", [NP_, 2, G, D])
        xt = sb("xt", [NP_, 2, G, D])
        agg = sb("agg", [NP_, 2, G, ROW1])
        rden = sb("rden", [NP_, 2, G, H])
        alpha = sb("alpha", [NP_, 2, G, H * D])
        aturned = sb("aturned", [P, 2, G, P])
        xturned = sb("xturned", [2 * D + 1, 2, G // 2, P])
        rz = sb("rz", [NP_, 2, G, 2 * D])
        hid = sb("hid", [NP_, 2, G, D])
        low = sb("low", [NP_, 2, G, D])
        r = sb("r", [NP_, 2, G, D])
        t = sb("t", [NP_, 2, G, D])
        stat = sb("stat", [NP_, 2, 5, G])
        new = sb("new", [NP_, 2, G, D])
        scaled = sb("scaled", [NP_, 2, G, D])
        tp = g.ps[:, 4:7, :]
        xp = g.ps[0:2 * D, 7, :]
        xp_last = g.ps[0:2 * D, 3, 0:NP_]
        gates_ps = g.ps[0:NP_, 0:3, :].rearrange("p q c -> p (q c)")
        gflat = gates_ps[:, 0:G * P].rearrange("p (j c) -> p j c", c=P)
        ones_set = g.sem("n1_ones")
        with nc.Block() as block:
            @block.sync
            def _(sp):
                x_v = g.x1.rearrange("(p j) f -> p (j f)", p=NP_)

                def load(buf, arrived, i, b):
                    sp.dma_start(buf[:, b].rearrange("p j f -> p (j f)"), x_v[:, bass.ds(i * (2 * G * D) + b * G * D, G * D)])\
                      .then_inc(arrived[b], 16)
                for b in range(2):
                    load(xt, s.x_product, 0, b)
                    load(xg, s.x_in, 0, b)
                with sp.Fori(0, GROUPS // 2 - 1) as i:
                    for b in range(2):
                        sp.wait_ge(s.x_turned[b], i + 1)
                        load(xt, s.x_product, i + 1, b)
                        sp.wait_ge(s.free[b], i + 1)
                        load(xg, s.x_in, i + 1, b)
                for b in range(2):
                    sp.wait_ge(s.stored[b], 32 * (GROUPS // 2 + 1))

            @block.gpsimd
            def _(pool):
                for b in range(2):
                    pool.sem_inc(s.stored[b], 32)
                pool.sem_inc(s.prods_used[0], 1)
                node_gathers(nc, g, pool, s, nidx, agg, g.rows1)
                clear_past(g, pool)

            @block.tensor
            def _(pe):
                def turn(i, b, before):
                    if before:
                        pe.wait_ge(s.x_turned_sb[before[1]], before[0] + 1)
                        pe.wait_ge(s.turned_sb[before[1]], before[0] + 1)
                    pe.wait_ge(s.x_product[b], 16 * i + 16)
                    pe.nop(nofuse=True)
                    for q in range(G // 2):
                        last = nc.tensor.transpose(xp[:, q * P:q * P + NP_] if q < 4 else xp_last,
                                                   xt[:, b, 2 * q:2 * q + 2, :].rearrange("p j f -> p (j f)"),
                                                   g.ident[0:NP_, 0:NP_])
                    last.then_inc(s.x_turned[b], 1)
                    pe.wait_ge(s.agg_ready[b], i + 1)
                    for c in range(G):
                        last = nc.tensor.transpose(tp[:, c // 4, (c % 4) * P:(c % 4) * P + NP_], alpha[:, b, c, :],
                                                   g.ident[0:NP_, 0:NP_])
                    last.then_inc(s.turned[b], 1)

                def gates(i, b):
                    pe.wait_ge(s.x_turned_sb[b], i + 1)
                    pe.wait_ge(s.turned_sb[b], i + 1)
                    pe.wait_ge(s.prods_used[0], i * 2 + (b + 1))
                    for q in range(G // 2):
                        nc.tensor.matmul(gates_ps[:, q * 2 * P:(q + 1) * 2 * P], xturned[:, b, q, 0:NP_],
                                         g.bdhh[:, :, :].rearrange("p k c -> p (k c)"), start=(q % 2 == 0), stop=True,
                                         skip_group_check=True)
                    for c in range(G):
                        last = nc.tensor.matmul(gates_ps[:, c * P:(c + 1) * P], aturned[:, b, c, 0:NP_],
                                                g.wc[:, :], start=False, stop=True, skip_group_check=True)
                    last.then_inc(s.product[b], 1)

                def step(at):
                    if at(2):
                        turn(*at(2), at(1))
                    if at(1):
                        gates(*at(1))

                pe.wait_ge(ones_set, 1)
                turn(0, 0, None)
                turn(0, 1, (0, 0))
                gates(0, 0)
                pipelined(pe.Fori, step)

            @block.scalar
            def _(act):
                a = nc.scalar

                def copy(i, b):
                    act.wait_ge(s.x_turned[b], i + 1)
                    a.activation(xturned[0:2 * D, b, 0:4, 0:NP_], xp.rearrange("p (q n) -> p q n", q=4)[:, :, 0:NP_], ACT.Copy)
                    a.activation(xturned[0:2 * D, b, 4, 0:NP_], xp_last, ACT.Copy).then_inc(s.x_turned_sb[b], 1)
                    act.wait_ge(s.turned[b], i + 1)
                    for q, (c, k) in enumerate(QUADS):
                        last = a.activation(aturned[:, b, c:c + k, 0:NP_],
                                            tp[:, q, 0:k * P].rearrange("p (k n) -> p k n", k=k)[:, :, 0:NP_], ACT.Copy)
                    last.then_inc(s.turned_sb[b], 1)

                def nonlinear(i, b):
                    act.wait_ge(s.product[b], i + 1)
                    a.activation(rz[:, b], gflat[:, :, 0:2 * D], ACT.Tanh, scale=0.5).then_inc(s.gates_act[b], 1)
                    act.wait_ge(s.hidden[b], i + 1)
                    a.activation(hid[:, b], hid[:, b], ACT.Tanh).then_inc(s.hidden_act[b], 1)
                    act.wait_ge(s.low[b], i + 1)
                    a.activation(low[:, b], low[:, b], ACT.Exp).then_inc(s.low_act[b], 1)

                def root(i, b):
                    layernorm_sqrt(nc, act, s, i, b, stat)

                def store(i, b):
                    node_stores(nc, g, act, s, i, b, None, [(new, g.x2), (scaled, g.table2)])

                def step(at):
                    if at(-1):
                        root(*at(-1))
                    if at(0):
                        nonlinear(*at(0))
                    if at(-1):
                        store(*at(-1))
                    if at(2):
                        copy(*at(2))

                copy(0, 0)
                copy(0, 1)
                pipelined(act.Fori, step)

            @block.vector
            def _(dve):
                v = nc.vector

                def means(i, b, first=False):
                    dve.wait_ge(s.gathered[b], 16 * G * i + 16 * G)
                    v.tensor_scalar(rden[:, b], agg[:, b, :, H:2 * H], 1e-30, None, ALU.max)
                    dve.drain()
                    v.reciprocal(rden[:, b], rden[:, b])
                    dve.drain()
                    if not first:
                        dve.wait_ge(s.turned[b], i)
                    for h in range(H):
                        v.tensor_tensor(alpha[:, b, :, h * D:(h + 1) * D], agg[:, b, :, 2 * H + h * D:2 * H + (h + 1) * D],
                                        bcast(rden[:, b, :, h], 2, D), ALU.mult)
                    dve.drain().then_inc(s.agg_ready[b], 1)
                    next_index(nc, g, dve, s, nidx, i + 1, b)

                def cell(i, b):
                    dve.wait_ge(s.gates_act[b], i + 1)
                    v.scalar_tensor_tensor(t[:, b], rz[:, b, :, 0:D], 1.0, gflat[:, :, 3 * D:4 * D], ALU.add, ALU.mult)
                    dve.drain()
                    v.scalar_tensor_tensor(hid[:, b], t[:, b], 0.5, gflat[:, :, 2 * D:3 * D], ALU.mult, ALU.add)\
                        .then_inc(s.hidden[b], 1)
                    dve.drain().then_inc(s.prods_used[0], 1)
                    dve.wait_ge(s.hidden_act[b], i + 1)
                    dve.wait_ge(s.x_in[b], 16 * i + 16)
                    v.tensor_tensor(t[:, b], xg[:, b], hid[:, b], ALU.subtract)
                    dve.drain()
                    v.scalar_tensor_tensor(t[:, b], rz[:, b, :, D:2 * D], 1.0, t[:, b], ALU.add, ALU.mult)
                    dve.drain()
                    v.scalar_tensor_tensor(r[:, b], t[:, b], 0.5, hid[:, b], ALU.mult, ALU.add)
                    dve.drain()
                    v.tensor_scalar(low[:, b], r[:, b], 0.0, None, ALU.min).then_inc(s.low[b], 1)
                    v.scalar_tensor_tensor(r[:, b], r[:, b], 0.0, xg[:, b], ALU.max, ALU.add)
                    dve.drain().then_inc(s.free[b], 1)
                    dve.wait_ge(s.low_act[b], i + 1)
                    v.scalar_tensor_tensor(r[:, b], low[:, b], -1.0, r[:, b], ALU.add, ALU.add)
                    dve.drain()
                    layernorm_moments(nc, dve, s, b, r[:, b], t[:, b], stat)

                def finish(i, b):
                    cols = group_cols(i, b)
                    dve.wait_ge(s.stored[b], 32 * i + 32)
                    layernorm_scale(nc, dve, s, i, b, r[:, b], stat, new[:, b])
                    dve.drain()
                    v.tensor_tensor(scaled[:, b], new[:, b], bcast(g.norm[:, 0, cols], 2, D), ALU.mult)
                    dve.drain().then_inc(s.new_ready[b], 1)

                v.memset(xturned[2 * D:2 * D + 1, :, :, :], 1.0)
                for b in range(2):
                    next_index(nc, g, dve, s, nidx, 0, b)
                dve.drain().then_inc(ones_set, 1)

                def step(at):
                    if at(2):
                        means(*at(2))
                    if at(-1):
                        finish(*at(-1))
                    if at(0):
                        cell(*at(0))

                means(0, 0, first=True)
                means(0, 1, first=True)
                pipelined(dve.Fori, step)


def edge_stage_tensor_product(nc, g):
    with ExitStack() as ph:
        sb = lambda n, s_, d=F32: ph.enter_context(nc.sbuf_tensor(f"e3_{n}", s_, d))
        s = EdgeSems(g.sem, g.gather_sem, "e3")
        STEPS = J // SC
        W = SC * P
        gat = sb("gat", [P, 2, J, D])
        sh = sb("sh", [P, 2, J, 4])
        h2 = sb("h2", [HR + 1, 2, J * P])
        vs = sb("vs", [P, J, MUL, 3])
        fac = sb("fac", [P, 2, J, 3, MUL])
        cv = sb("cv", [P, 2, J, 3, MUL])
        prod = sb("prod", [P, 2, SC, 6, MUL, MUL])
        half = sb("half", [P, 2, SC * 6 * MUL, 4])
        quarter = sb("quarter", [P, 2 * SC * 6 * MUL, 2])
        red = sb("red", [P, J, 6, MUL])
        msg = sb("msg", [P, 2, D, J])
        out = sb("out", [P, 2, J, D])
        contw = sb("contw", [P, 2, D, J])
        cont_first = sb("cont_first", [P, 2, 1])
        tp_made, tp_used = ([g.sem(f"e3_{n}{k}") for k in range(2)] for n in ("tp", "tp_used"))
        sh_in, h2_in, h2_free, gat_free, factored, used = (
            [g.sem(f"e3_{n}{b}") for b in range(2)] for n in ("sh_in", "h2_in", "h2_free", "gat_free", "factored", "used"))
        ones_set = g.sem("e3_ones")
        turned = [g.sem(f"e3_turned{b}") for b in range(2)]
        with nc.Block() as block:
            @block.gpsimd
            def _(pool):
                for b in range(2):
                    pool.sem_inc(gat_free[b], 1)
                    pool.sem_inc(used[b], 1)
                    pool.sem_inc(turned[b], 1)
                    pool.sem_inc(s.buf_free[b], 16)
                with pool.Fori(0, PAIRS) as i:
                    for b in range(2):
                        pool.wait_ge(s.idx_in[b], 16 * i + 16)
                        pool.wait_ge(gat_free[b], i + 1)
                        pool.nop(nofuse=True)
                        for j in range(J):
                            pool.indirect_dma_start(gat[:, b, j, :], None, g.x3[:, :],
                                                    bass.IndirectOffsetOnAxis(g.idx[:, b, j:j + 1], 0)).then_inc(s.rows_in[b], 16)
                clear_past(g, pool)

            @block.sync
            def _(sp):
                sh_v = g.edge_sh.rearrange("(p c) h -> p (c h)", p=P)
                chunk = lambda i, b, width: bass.ds(i * (2 * J * width) + b * J * width, J * width)
                for b in range(2):
                    sp.dma_start(g.idx[:, b, :], g.src_cols[:, b * J:(b + 1) * J]).then_inc(s.idx_in[b], 16)
                    sp.dma_start(h2[0:HR, b, :], g.hidden[:, b * J * P:(b + 1) * J * P]).then_inc(h2_in[b], 16)
                    sp.dma_start(sh[:, b].rearrange("p j h -> p (j h)"), sh_v[:, b * J * 4:(b + 1) * J * 4]).then_inc(sh_in[b], 16)
                with sp.Fori(0, PAIRS - 1) as i:
                    for b in range(2):
                        sp.wait_ge(s.rows_in[b], (16 * J) * i + 16 * J)
                        sp.dma_start(g.idx[:, b, :], g.src_cols[:, chunk(i, b + 2, 1)]).then_inc(s.idx_in[b], 16)
                        sp.wait_ge(h2_free[b], i + 1)
                        sp.dma_start(h2[0:HR, b, :], g.hidden[:, chunk(i, b + 2, P)]).then_inc(h2_in[b], 16)
                        sp.wait_ge(used[b], i + 2)
                        sp.dma_start(sh[:, b].rearrange("p j h -> p (j h)"), sh_v[:, chunk(i, b + 2, 4)]).then_inc(sh_in[b], 16)
                for b in range(2):
                    sp.wait_ge(s.buf_free[b], 16 * PAIRS + 16)

            @block.tensor
            def _(pe):
                pe.wait_ge(ones_set, 1)
                for k in range(2):
                    pe.sem_inc(tp_used[k], 1)
                with pe.Fori(0, PAIRS) as i:
                    for b in range(2):
                        pe.wait_ge(h2_in[b], 16 * i + 16)
                        for m in range(STEPS):
                            n = b * STEPS + m
                            k = n % 2
                            pe.wait_ge(tp_used[k], i * STEPS + n // 2 + 1)
                            for c in range(SC):
                                at = (m * SC + c) * P
                                last = nc.tensor.matmul(g.ps[:, 4 * k + c // 2, (c % 2) * NTP:(c % 2 + 1) * NTP],
                                                        h2[:, b, at:at + P], g.w3p[:, :], start=True, stop=True)
                            last.then_inc(tp_made[k], 1)
                        pe.drain().then_inc(h2_free[b], 1)

            @block.scalar
            def _(act):
                rows_v = g.rows3[0:EROWS, :].rearrange("(p c) f -> p (c f)", p=P)

                def factors(i, b):
                    act.wait_ge(s.rows_in[b], (16 * J) * i + 16 * J)
                    act.wait_ge(sh_in[b], 16 * i + 16)
                    act.wait_ge(used[b], i + 1)
                    cols = i * (2 * J) + b * J
                    nc.scalar.activation(contw[:, b, :, 1:J], bcast(g.cont[:, bass.ds(cols + 1, J - 1)], 1, D), ACT.Copy)
                    nc.scalar.activation(cont_first[:, b, :], g.cont[:, bass.ds(cols, 1)], ACT.Copy)
                    nc.scalar.activation(fac[:, b, :, 2, :], gat[:, b, :, 0:MUL], ACT.Copy)
                    for j in range(J):
                        nc.scalar.mul(fac[:, b, j, 0, :], gat[:, b, j, 0:MUL], sh[:, b, j, 0:1])
                        last = nc.scalar.mul(cv[:, b, j], gat[:, b, j, MUL:D].rearrange("p (u i) -> p i u", i=3),
                                             sh[:, b, j, 0:1])
                        if j % SC == SC - 1:
                            last.then_inc(factored[b], 1)

                def store(i, b):
                    act.wait_ge(s.scanned[b], i + 1)
                    act.wait_ge(s.buf_free[b], 16 * i + 16)
                    nc.scalar.activation(out[:, b], msg[:, b].rearrange("p f j -> p j f"), ACT.Copy).then_inc(turned[b], 1)
                    act.wait_ge(turned[b], i + 2)
                    act.dma_start(rows_v[:, chunk_cols(i, b, D)], out[:, b].rearrange("p j f -> p (j f)"))\
                       .then_inc(s.buf_free[b], 16)

                factors(0, 0)
                with act.Fori(0, PAIRS - 1) as i:
                    factors(i, 1)
                    store(i, 0)
                    factors(i + 1, 0)
                    store(i, 1)
                factors(PAIRS - 1, 1)
                store(PAIRS - 1, 0)
                store(PAIRS - 1, 1)

            @block.vector
            def _(dve):
                v = nc.vector
                v.memset(h2[HR:HR + 1, :, :], 1.0)
                v.memset(msg[:, 1, :, J - 1], 0.0)
                v.memset(contw[:, :, :, 0:1], 0.0)
                dve.drain().then_inc(ones_set, 1)
                with dve.Fori(0, PAIRS) as i:
                    for b in range(2):
                        dve.wait_ge(sh_in[b], 16 * i + 16)
                        dve.wait_ge(s.rows_in[b], (16 * J) * i + 16 * J)
                        hv = gat[:, b, :, MUL:D].rearrange("p j (u i) -> p j u i", i=3)
                        sh1 = sh[:, b, :, 1:4]
                        v.tensor_tensor(vs[:, :, :, :], hv, bcast(sh1, 2, MUL), ALU.mult)
                        dve.drain()
                        v.tensor_reduce(fac[:, b, :, 1, :], vs[:, :, :, :], AX.X, ALU.add)
                        dve.drain()
                        for m in range(STEPS):
                            n = b * STEPS + m
                            k = n % 2
                            c0, c1 = m * SC, (m + 1) * SC
                            if m < STEPS // 2:
                                dve.wait_ge(factored[b], i * STEPS + (m + 1))
                            elif m == STEPS // 2:
                                dve.wait_ge(factored[b], i * STEPS + STEPS)
                                dve.sem_inc(gat_free[b], 1)
                            dve.wait_ge(tp_made[k], i * STEPS + n // 2 + 1)
                            tp = g.ps[:, 4 * k:4 * k + 4, :].rearrange("p a (c x) -> p (a c) x", x=NTP)
                            v.tensor_tensor(prod[:, k, :, 0:3], tp[:, :, 0:192].rearrange("p c (f w u) -> p c f w u", f=3, w=MUL),
                                            bcast(fac[:, b, c0:c1], 3, MUL), ALU.mult)
                            v.tensor_tensor(prod[:, k, :, 3:6], bcast(tp[:, :, 192:256].rearrange("p c (w u) -> p c w u", w=MUL), 2, 3),
                                            bcast(cv[:, b, c0:c1], 3, MUL), ALU.mult)
                            dve.drain().then_inc(tp_used[k], 1)
                            by_u = prod[:, k].rearrange("p c f w u -> p (c f w) u")
                            v.tensor_tensor(half[:, k], by_u[:, :, 0:4], by_u[:, :, 4:8], ALU.add)
                            if k == 1:
                                dve.drain()
                                two = half[:, :, :, :].rearrange("p k x u -> p (k x) u")
                                v.tensor_tensor(quarter[:, :, :], two[:, :, 0:2], two[:, :, 2:4], ALU.add)
                                dve.drain()
                                v.tensor_tensor(red[:, c0 - SC:c1].rearrange("p c f w -> p (c f w)"),
                                                quarter[:, :, 0], quarter[:, :, 1], ALU.add)
                        dve.drain()
                        dve.wait_ge(turned[b], i + 1)
                        by_j = msg[:, b].rearrange("p f j -> p j f")
                        v.tensor_tensor(by_j[:, :, 0:MUL], red[:, :, 0, :], red[:, :, 1, :], ALU.add)
                        v.tensor_tensor(vs[:, :, :, :], bcast(red[:, :, 2, :], 3, 3), bcast(sh1, 2, MUL), ALU.mult)
                        dve.drain()
                        v.tensor_tensor(by_j[:, :, MUL:D].rearrange("p j (w i) -> p j w i", i=3), vs[:, :, :, :],
                                        red[:, :, 3:6, :].rearrange("p j i w -> p j w i"), ALU.add)
                        dve.drain()
                        v.scalar_tensor_tensor(msg[:, b, :, 0], msg[:, 1 - b, :, J - 1], cont_first[:, b, 0:1], msg[:, b, :, 0],
                                               ALU.mult, ALU.add)
                        dve.drain()
                        flat = msg[:, b].rearrange("p f j -> p (f j)")
                        v.tensor_tensor_scan(flat, contw[:, b].rearrange("p f j -> p (f j)"), flat, 0.0, ALU.mult, ALU.add)
                        dve.drain().then_inc(s.scanned[b], 1)
                        dve.sem_inc(used[b], 1)
                v.tensor_copy(g.carry[:, 0:D], msg[:, 1, :, J - 1])
                dve.drain()


def program(nc, x, src_cols, dst_flat, edge_sh, edge_rad, w, out):
    with ExitStack() as ctx:
        g = Graph()
        g.sem_for_good, g.gather_count = (lambda n: ctx.enter_context(nc.semaphore(n))), count()
        g.past_held, g.past_sems = ExitStack(), []
        sb = lambda n, s, d=F32: ctx.enter_context(nc.sbuf_tensor(n, s, d))
        dram = lambda n, s, d=F32: nc.dram_tensor(n, s, d, kind="Internal").ap()
        g.src_cols, g.dst_flat, g.edge_sh, g.edge_rad = src_cols, dst_flat, edge_sh, edge_rad
        g.rows0 = dram("rows0", (EROWS + 1, D))
        g.rows1 = dram("rows1", (EROWS + 1, ROW1))
        g.rows2 = dram("rows2", (EROWS + 1, D))
        g.rows3 = dram("rows3", (EROWS + 1, D))
        g.er_edges = dram("er_edges", (EROWS + N, H))
        g.table1 = dram("table1", (N, T1W))
        g.table2 = dram("table2", (N, D))
        g.x1, g.x2, g.x3 = (dram(f"x{k}", (N, D)) for k in (1, 2, 3))
        g.hidden = dram("hidden", (HR, EROWS))

        g.ps = ctx.enter_context(nc.psum_tensor("ps", [P, 8, 512], F32))
        g.idx = sb("idx", [P, 2, J], I32)
        g.cont = sb("cont", [P, EC])
        g.carry = sb("carry", [P, ROW1])
        g.ident = sb("ident", [P, P])
        g.ltri = sb("ltri", [P, P])
        g.iota_i = sb("iota_i", [P, P], I32)
        g.node_i = sb("node_i", [P, NC_], I32)
        g.first_edge_i = sb("first_edge_i", [P, 1], I32)
        g.dst0_f, g.dst0_i = sb("dst0_f", [P, 1]), sb("dst0_i", [P, 1], I32)
        g.row_dst0 = sb("row_dst0", [P, T1W])
        g.border_idx = sb("border_idx", [P, 1], I32)
        g.cont0, g.linked, g.link = sb("cont0", [P, P]), sb("linked", [P, P]), sb("link", [P, P])
        g.deg, g.norm = sb("deg", [NP_, 2, NC_]), sb("norm", [NP_, 2, NC_])
        g.last_i, g.first_i = sb("last_i", [NP_, NC_ + 2 * G], I32), sb("first_i", [NP_, NC_], I32)
        g.er_nodes = sb("er_nodes", [NP_, NC_, H])
        g.bd0, g.bd2, g.bdself = sb("bd0", [P, P]), sb("bd2", [P, P]), sb("bdself", [P, P])
        g.bdel = sb("bdel", [P, 8 * H])
        g.bdhh = sb("bdhh", [2 * D + 1, 2, P])
        g.wc = sb("wc", [P, P])
        g.w1, g.w2, g.w3p = sb("w1", [8, HR]), sb("w2", [HR, HR]), sb("w3p", [HR + 1, NTP])
        g.b1, g.b2, g.b2row = sb("b1", [HR, 1]), sb("b2", [HR, 1]), sb("b2row", [NP_, D])

        with stage(nc, g):
            edge_stage_plain(nc, g, "e0", x[:, :], g.rows0, weights=w)
        with stage(nc, g):
            index_stage(nc, g)
        with stage(nc, g):
            border_stage_plain(nc, g, "b0", g.rows0)
        with stage(nc, g):
            node_stage_plain(nc, g, "n0", 0, g.rows0, x, [("x", g.x1), ("t1", g.table1)])
        with stage(nc, g):
            edge_stage_attention(nc, g)
        with stage(nc, g):
            border_stage_attention(nc, g)
        with stage(nc, g):
            node_stage_gru(nc, g)
        with stage(nc, g):
            edge_stage_plain(nc, g, "e2", g.table2[:, :], g.rows2)
        with stage(nc, g):
            border_stage_plain(nc, g, "b2", g.rows2)
        with stage(nc, g):
            node_stage_plain(nc, g, "n2", 2, g.rows2, g.x2, [("x", g.x3)])
        with stage(nc, g):
            edge_stage_tensor_product(nc, g)
        with stage(nc, g):
            border_stage_plain(nc, g, "b3", g.rows3)
        with stage(nc, g):
            node_stage_plain(nc, g, "n3", 3, g.rows3, g.x3, [("x", out)])
        with nc.Block() as block:
            @block.gpsimd
            def _(pool):
                clear_past(g, pool)
        g.past_held.close()


def kernel(x, src, dst, edge_attr_4, edge_attr_8, L0_gnn_W, L1_gnn_W_gat, L1_gnn_attn_l, L1_gnn_attn_r, L1_gnn_W_ih,
           L1_gnn_W_hh, L1_gnn_b_ih, L1_gnn_b_hh, L2_gnn_W, L2_gnn_b, L3_gnn_W1, L3_gnn_b1, L3_gnn_W2, L3_gnn_b2,
           L3_gnn_W3, L3_gnn_b3, L3_gnn_Ws, L3_gnn_Wv):
    import concourse.bacc as bacc
    from concourse.bass_utils import run_bass_kernel_spmd

    a = np.ascontiguousarray
    pad = EROWS - E
    src_cols = np.pad(np.pad(np.asarray(src), (0, pad)).reshape(P, EC), ((0, 0), (0, 2 * J)))
    dst_flat = np.concatenate([np.full(1, -1, np.int32), np.asarray(dst), np.full(pad, N, np.int32)]).reshape(1, -1)
    rad = np.pad(np.asarray(edge_attr_8), ((0, pad), (0, 0))).reshape(P, EC, 8).transpose(2, 1, 0)
    rad = np.pad(rad, ((0, 0), (0, 2 * J), (0, 0))).reshape(8, -1)
    data = {
        "x": np.asarray(x),
        "src_cols": src_cols,
        "dst_flat": dst_flat,
        "edge_sh": np.pad(np.asarray(edge_attr_4), ((0, pad), (0, 0))),
        "edge_rad": rad,
    }
    attn = np.zeros((H * D, 2 * H), np.float32)
    for h in range(H):
        attn[h * D:(h + 1) * D, h] = np.asarray(L1_gnn_attn_l)[h]
        attn[h * D:(h + 1) * D, H + h] = np.asarray(L1_gnn_attn_r)[h]
    self_w = np.zeros((D, D), np.float32)
    self_w[:MUL, :MUL] = np.asarray(L3_gnn_Ws)
    for i in range(3):
        self_w[MUL + i::3, MUL + i::3] = np.asarray(L3_gnn_Wv)
    weights = {
        "W0": np.asarray(L0_gnn_W), "gatT": np.asarray(L1_gnn_W_gat).T, "attn": attn,
        "wihT": np.asarray(L1_gnn_W_ih).T, "whhT": np.asarray(L1_gnn_W_hh).T,
        "b_ih": np.asarray(L1_gnn_b_ih).reshape(1, -1), "b_hh": np.asarray(L1_gnn_b_hh).reshape(1, -1),
        "W2g": np.asarray(L2_gnn_W), "b2g": np.tile(np.asarray(L2_gnn_b).reshape(1, -1), (NP_, 1)),
        "W1": np.asarray(L3_gnn_W1), "b1": np.asarray(L3_gnn_b1).reshape(-1, 1),
        "W2": np.asarray(L3_gnn_W2), "b2": np.asarray(L3_gnn_b2).reshape(-1, 1),
        "W3": np.asarray(L3_gnn_W3), "b3": np.asarray(L3_gnn_b3).reshape(1, -1),
        "self": self_w,
    }
    nc = bacc.Bacc("TRN2", target_bir_lowering=False, num_devices=1)
    arrays = {f"in_{n}": a(v) for n, v in {**data, **weights}.items()}
    aps = {n: nc.dram_tensor(n, v.shape, mybir.dt.from_np(v.dtype), kind="ExternalInput").ap() for n, v in arrays.items()}
    out = nc.dram_tensor("out", (N, D), F32, kind="ExternalOutput").ap()
    program(nc, *(aps[f"in_{n}"] for n in data), {n: aps[f"in_{n}"] for n in weights}, out)
    r = run_bass_kernel_spmd(nc, [arrays], core_ids=[0])
    return r.results[0]["out"]
```
